# Optimizing a Trainium2 kernel written in Bass

```python
import numpy as np
import jax
import jax.numpy as jnp

def _softmax(x, axis=-1):
    return jax.nn.softmax(x, axis=axis)

def _gelu(x):
    return jax.nn.gelu(x, approximate=True)

def _silu(x):
    return jax.nn.silu(x)

def _sigmoid(x):
    return jax.nn.sigmoid(x)

def _layernorm(x, axis=-1, eps=1e-05):
    m = jnp.mean(x, axis=axis, keepdims=True)
    v = jnp.var(x, axis=axis, keepdims=True)
    return (x - m) / jnp.sqrt(v + eps)

def _scatter_add(tgt, idx, src, axis=0):
    return tgt.at[idx].add(src)

def _segment_sum(src, seg, n):
    return jax.ops.segment_sum(src, seg, n)
kernel_name = 'mk_macaron_d1_jaxref_r8_ecc560'

def setup_inputs(seed: int=0):
    np.random.seed(seed)
    _w = jnp.asarray

    def _L0_attn_setup():
        import jax, jax.numpy as jnp
        import numpy as np
        B, L, DM = (4, 256, 128)
        EXPAND, N, W = (2, 16, 4)
        DIN = EXPAND * DM

        def _ssm_fft_conv(x, log_dt, A_re, A_im, C_re, C_im, D_skip):
            Ll = x.shape[-1]
            dt = jnp.exp(log_dt)[:, None]
            A = A_re + 1j * A_im
            C = C_re + 1j * C_im
            dtA = dt * A
            dB = (jnp.exp(dtA) - 1.0) / A
            ell = jnp.arange(Ll, dtype=jnp.float32)
            vand = jnp.exp(dtA[:, :, None] * ell)
            K = 2.0 * jnp.real(jnp.einsum('hn,hnl->hl', C * dB, vand))
            n_fft = 2 * Ll
            y = jnp.fft.irfft(jnp.fft.rfft(x, n=n_fft) * jnp.fft.rfft(K, n=n_fft)[None], n=n_fft)[..., :Ll]
            return y + D_skip[None, :, None] * x
        key = jax.random.key(seed)
        ks = jax.random.split(key, 9)
        hidden_states = jax.random.normal(ks[0], (B, L, DM), dtype=jnp.float32)
        in_proj_w = jax.random.normal(ks[1], (2 * DIN, DM), dtype=jnp.float32) * 0.02
        conv_w = jax.random.normal(ks[2], (DIN, W), dtype=jnp.float32) * 0.2
        conv_b = jnp.zeros((DIN,), dtype=jnp.float32)
        out_proj_w = jax.random.normal(ks[3], (DM, DIN), dtype=jnp.float32) * 0.02
        log_dt = jax.random.uniform(ks[4], (DIN,), dtype=jnp.float32, minval=jnp.log(0.001), maxval=jnp.log(0.1))
        A_re = -0.5 * jnp.ones((DIN, N), dtype=jnp.float32)
        A_im = jnp.broadcast_to(jnp.pi * jnp.arange(N, dtype=jnp.float32), (DIN, N)).copy()
        C_re = jax.random.normal(ks[5], (DIN, N), dtype=jnp.float32) * 0.5
        C_im = jax.random.normal(ks[6], (DIN, N), dtype=jnp.float32) * 0.5
        D_skip = jax.random.normal(ks[7], (DIN,), dtype=jnp.float32)
        return {'hidden_states': hidden_states, 'in_proj_w': in_proj_w, 'conv_w': conv_w, 'conv_b': conv_b, 'out_proj_w': out_proj_w, 'log_dt': log_dt, 'A_re': A_re, 'A_im': A_im, 'C_re': C_re, 'C_im': C_im, 'D_skip': D_skip}
    _L0_attn_in = _L0_attn_setup()

    def _L0_ffn_setup():
        import jax, jax.numpy as jnp
        import numpy as np
        DIM = 128
        DEPTH = 2
        HEADS = 8
        DIM_HEAD = 64
        WINDOW = 64
        INNER = HEADS * DIM_HEAD
        HID = int(DIM * 4 * 2 / 3)
        B, N = (2, 1024)
        QK_SCALE = 8.0

        def shift_token(t):
            t1, t2 = jnp.split(t, 2, axis=-1)
            t2 = jnp.pad(t2, ((0, 0), (1, 0), (0, 0)))[:, :-1]
            return jnp.concatenate([t1, t2], axis=-1)

        def l2norm(t):
            return t / jnp.clip(jnp.linalg.norm(t, axis=-1, keepdims=True), 1e-12)

        def rotate_half(x):
            x1, x2 = jnp.split(x, 2, axis=-1)
            return jnp.concatenate([-x2, x1], axis=-1)

        def rotary_xpos(q, k):
            n = q.shape[-2]
            half_idx = jnp.arange(0, DIM_HEAD, 2, dtype=jnp.float32)
            inv_freq = 1.0 / 10000.0 ** (half_idx / DIM_HEAD)
            t = jnp.arange(n, dtype=jnp.float32)
            freqs = t[:, None] * inv_freq[None, :]
            freqs = jnp.concatenate([freqs, freqs], axis=-1)
            base = (half_idx + 0.4 * DIM_HEAD) / (1.4 * DIM_HEAD)
            power = (t - n // 2) / float(WINDOW // 2)
            scale = base[None, :] ** power[:, None]
            scale = jnp.concatenate([scale, scale], axis=-1)
            cos, sin = (jnp.cos(freqs), jnp.sin(freqs))
            q = q * cos * scale + rotate_half(q) * sin * scale
            k = k * cos / scale + rotate_half(k) * sin / scale
            return (q, k)

        def local_attention(q, k, v):
            b, h, n, d = q.shape
            w = n // WINDOW
            bq = q.reshape(b, h, w, WINDOW, d) * QK_SCALE
            bk = k.reshape(b, h, w, WINDOW, d)
            bv = v.reshape(b, h, w, WINDOW, d)

            def look_around(t):
                p = jnp.pad(t, ((0, 0), (0, 0), (1, 0), (0, 0), (0, 0)))
                return jnp.concatenate([p[:, :, :w], p[:, :, 1:]], axis=3)
            bk, bv = (look_around(bk), look_around(bv))
            bt = jnp.arange(n).reshape(w, WINDOW)
            btp = jnp.pad(bt, ((1, 0), (0, 0)), constant_values=-1)
            btk = jnp.concatenate([btp[:w], btp[1:]], axis=1)
            sim = jnp.einsum('bhwid,bhwjd->bhwij', bq, bk)
            i = bt[:, :, None]
            j = btk[:, None, :]
            mask = (i < j) | (i > j + WINDOW) | (j == -1)
            sim = jnp.where(mask, -jnp.finfo(sim.dtype).max, sim)
            attn = jax.nn.softmax(sim, axis=-1)
            out = jnp.einsum('bhwij,bhwjd->bhwid', attn, bv)
            return out.reshape(b, h, n, d)

        def _layer(x, wqkv, qs, ksc, wo, lg, lb, w1, b1, w2, b2):
            b, n, _ = x.shape
            h = shift_token(x)
            qkv = h @ wqkv
            q, k, v = jnp.split(qkv, 3, axis=-1)
            to_heads = lambda t: t.reshape(b, n, HEADS, DIM_HEAD).transpose(0, 2, 1, 3)
            q, k, v = (to_heads(q), to_heads(k), to_heads(v))
            q = l2norm(q) * qs
            k = l2norm(k) * ksc
            q, k = rotary_xpos(q, k)
            o = local_attention(q, k, v)
            o = o.transpose(0, 2, 1, 3).reshape(b, n, INNER)
            x = x + o @ wo
            h = shift_token(x)
            mu = h.mean(-1, keepdims=True)
            var = h.var(-1, keepdims=True)
            h = (h - mu) / jnp.sqrt(var + 1e-05) * lg + lb
            h = h @ w1 + b1
            a, g = jnp.split(h, 2, axis=-1)
            h = a * jax.nn.gelu(g, approximate=False)
            x = x + h @ w2 + b2
            return x
        key = jax.random.key(seed)
        ks = jax.random.split(key, 6)
        return {'x': jax.random.normal(ks[0], (B, N, DIM), jnp.float32), 'wqkv': jax.random.normal(ks[1], (DEPTH, DIM, 3 * INNER), jnp.float32) * 0.02, 'q_scale': jnp.ones((DEPTH, DIM_HEAD), jnp.float32), 'k_scale': jnp.ones((DEPTH, DIM_HEAD), jnp.float32), 'wo': jax.random.normal(ks[2], (DEPTH, INNER, DIM), jnp.float32) * 0.02, 'ln_g': jnp.ones((DEPTH, DIM), jnp.float32), 'ln_b': jnp.zeros((DEPTH, DIM), jnp.float32), 'w1': jax.random.normal(ks[3], (DEPTH, DIM, 2 * HID), jnp.float32) * 0.02, 'b1': jnp.zeros((DEPTH, 2 * HID), jnp.float32), 'w2': jax.random.normal(ks[4], (DEPTH, HID, DIM), jnp.float32) * 0.02, 'b2': jnp.zeros((DEPTH, DIM), jnp.float32)}
    _L0_ffn_in = _L0_ffn_setup()
    _d = {'L0_attn_hidden_states': _L0_attn_in['hidden_states'], 'L0_attn_in_proj_w': _L0_attn_in['in_proj_w'], 'L0_attn_conv_w': _L0_attn_in['conv_w'], 'L0_attn_conv_b': _L0_attn_in['conv_b'], 'L0_attn_out_proj_w': _L0_attn_in['out_proj_w'], 'L0_attn_log_dt': _L0_attn_in['log_dt'], 'L0_attn_A_re': _L0_attn_in['A_re'], 'L0_attn_A_im': _L0_attn_in['A_im'], 'L0_attn_C_re': _L0_attn_in['C_re'], 'L0_attn_C_im': _L0_attn_in['C_im'], 'L0_attn_D_skip': _L0_attn_in['D_skip'], 'L0_ffn_wqkv': _L0_ffn_in['wqkv'], 'L0_ffn_q_scale': _L0_ffn_in['q_scale'], 'L0_ffn_k_scale': _L0_ffn_in['k_scale'], 'L0_ffn_wo': _L0_ffn_in['wo'], 'L0_ffn_ln_g': _L0_ffn_in['ln_g'], 'L0_ffn_ln_b': _L0_ffn_in['ln_b'], 'L0_ffn_w1': _L0_ffn_in['w1'], 'L0_ffn_b1': _L0_ffn_in['b1'], 'L0_ffn_w2': _L0_ffn_in['w2'], 'L0_ffn_b2': _L0_ffn_in['b2']}
    _x0 = _d['L0_attn_hidden_states']
    _d['L0_attn_hidden_states'] = jax.random.normal(jax.random.fold_in(jax.random.key(seed), 1), (2, 1024, 128), dtype=_x0.dtype)
    del _x0
    return _d

def reference(L0_attn_hidden_states, L0_attn_in_proj_w, L0_attn_conv_w, L0_attn_conv_b, L0_attn_out_proj_w, L0_attn_log_dt, L0_attn_A_re, L0_attn_A_im, L0_attn_C_re, L0_attn_C_im, L0_attn_D_skip, L0_ffn_wqkv, L0_ffn_q_scale, L0_ffn_k_scale, L0_ffn_wo, L0_ffn_ln_g, L0_ffn_ln_b, L0_ffn_w1, L0_ffn_b1, L0_ffn_w2, L0_ffn_b2):

    def _L0_attn_ref(hidden_states, in_proj_w, conv_w, conv_b, out_proj_w, log_dt, A_re, A_im, C_re, C_im, D_skip):
        import jax, jax.numpy as jnp
        import numpy as np
        B, L, DM = (4, 256, 128)
        EXPAND, N, W = (2, 16, 4)
        DIN = EXPAND * DM

        def _ssm_fft_conv(x, log_dt, A_re, A_im, C_re, C_im, D_skip):
            Ll = x.shape[-1]
            dt = jnp.exp(log_dt)[:, None]
            A = A_re + 1j * A_im
            C = C_re + 1j * C_im
            dtA = dt * A
            dB = (jnp.exp(dtA) - 1.0) / A
            ell = jnp.arange(Ll, dtype=jnp.float32)
            vand = jnp.exp(dtA[:, :, None] * ell)
            K = 2.0 * jnp.real(jnp.einsum('hn,hnl->hl', C * dB, vand))
            n_fft = 2 * Ll
            y = jnp.fft.irfft(jnp.fft.rfft(x, n=n_fft) * jnp.fft.rfft(K, n=n_fft)[None], n=n_fft)[..., :Ll]
            return y + D_skip[None, :, None] * x
        b, l, d = hidden_states.shape
        xz = jnp.einsum('bld,ed->bel', hidden_states, in_proj_w)
        x, z = jnp.split(xz, 2, axis=1)
        xp = jnp.pad(x, ((0, 0), (0, 0), (W - 1, 0)))
        x = jax.lax.conv_general_dilated(xp, conv_w[:, None, :], window_strides=(1,), padding='VALID', dimension_numbers=('NCH', 'OIH', 'NCH'), feature_group_count=x.shape[1])
        x = jax.nn.silu(x + conv_b[None, :, None])
        x = _ssm_fft_conv(x, log_dt, A_re, A_im, C_re, C_im, D_skip)
        x = x * jax.nn.silu(z)
        out = jnp.einsum('bel,de->bld', x, out_proj_w)
        return out

    def _L0_ffn_ref(x, wqkv, q_scale, k_scale, wo, ln_g, ln_b, w1, b1, w2, b2):
        import jax, jax.numpy as jnp
        import numpy as np
        DIM = 128
        DEPTH = 2
        HEADS = 8
        DIM_HEAD = 64
        WINDOW = 64
        INNER = HEADS * DIM_HEAD
        HID = int(DIM * 4 * 2 / 3)
        B, N = (2, 1024)
        QK_SCALE = 8.0

        def shift_token(t):
            t1, t2 = jnp.split(t, 2, axis=-1)
            t2 = jnp.pad(t2, ((0, 0), (1, 0), (0, 0)))[:, :-1]
            return jnp.concatenate([t1, t2], axis=-1)

        def l2norm(t):
            return t / jnp.clip(jnp.linalg.norm(t, axis=-1, keepdims=True), 1e-12)

        def rotate_half(x):
            x1, x2 = jnp.split(x, 2, axis=-1)
            return jnp.concatenate([-x2, x1], axis=-1)

        def rotary_xpos(q, k):
            n = q.shape[-2]
            half_idx = jnp.arange(0, DIM_HEAD, 2, dtype=jnp.float32)
            inv_freq = 1.0 / 10000.0 ** (half_idx / DIM_HEAD)
            t = jnp.arange(n, dtype=jnp.float32)
            freqs = t[:, None] * inv_freq[None, :]
            freqs = jnp.concatenate([freqs, freqs], axis=-1)
            base = (half_idx + 0.4 * DIM_HEAD) / (1.4 * DIM_HEAD)
            power = (t - n // 2) / float(WINDOW // 2)
            scale = base[None, :] ** power[:, None]
            scale = jnp.concatenate([scale, scale], axis=-1)
            cos, sin = (jnp.cos(freqs), jnp.sin(freqs))
            q = q * cos * scale + rotate_half(q) * sin * scale
            k = k * cos / scale + rotate_half(k) * sin / scale
            return (q, k)

        def local_attention(q, k, v):
            b, h, n, d = q.shape
            w = n // WINDOW
            bq = q.reshape(b, h, w, WINDOW, d) * QK_SCALE
            bk = k.reshape(b, h, w, WINDOW, d)
            bv = v.reshape(b, h, w, WINDOW, d)

            def look_around(t):
                p = jnp.pad(t, ((0, 0), (0, 0), (1, 0), (0, 0), (0, 0)))
                return jnp.concatenate([p[:, :, :w], p[:, :, 1:]], axis=3)
            bk, bv = (look_around(bk), look_around(bv))
            bt = jnp.arange(n).reshape(w, WINDOW)
            btp = jnp.pad(bt, ((1, 0), (0, 0)), constant_values=-1)
            btk = jnp.concatenate([btp[:w], btp[1:]], axis=1)
            sim = jnp.einsum('bhwid,bhwjd->bhwij', bq, bk)
            i = bt[:, :, None]
            j = btk[:, None, :]
            mask = (i < j) | (i > j + WINDOW) | (j == -1)
            sim = jnp.where(mask, -jnp.finfo(sim.dtype).max, sim)
            attn = jax.nn.softmax(sim, axis=-1)
            out = jnp.einsum('bhwij,bhwjd->bhwid', attn, bv)
            return out.reshape(b, h, n, d)

        def _layer(x, wqkv, qs, ksc, wo, lg, lb, w1, b1, w2, b2):
            b, n, _ = x.shape
            h = shift_token(x)
            qkv = h @ wqkv
            q, k, v = jnp.split(qkv, 3, axis=-1)
            to_heads = lambda t: t.reshape(b, n, HEADS, DIM_HEAD).transpose(0, 2, 1, 3)
            q, k, v = (to_heads(q), to_heads(k), to_heads(v))
            q = l2norm(q) * qs
            k = l2norm(k) * ksc
            q, k = rotary_xpos(q, k)
            o = local_attention(q, k, v)
            o = o.transpose(0, 2, 1, 3).reshape(b, n, INNER)
            x = x + o @ wo
            h = shift_token(x)
            mu = h.mean(-1, keepdims=True)
            var = h.var(-1, keepdims=True)
            h = (h - mu) / jnp.sqrt(var + 1e-05) * lg + lb
            h = h @ w1 + b1
            a, g = jnp.split(h, 2, axis=-1)
            h = a * jax.nn.gelu(g, approximate=False)
            x = x + h @ w2 + b2
            return x
        for l in range(DEPTH):
            x = _layer(x, wqkv[l], q_scale[l], k_scale[l], wo[l], ln_g[l], ln_b[l], w1[l], b1[l], w2[l], b2[l])
        return x
    x = L0_attn_hidden_states
    x = x + 0.5 * _L0_ffn_ref(_layernorm(x, axis=-1), L0_ffn_wqkv, L0_ffn_q_scale, L0_ffn_k_scale, L0_ffn_wo, L0_ffn_ln_g, L0_ffn_ln_b, L0_ffn_w1, L0_ffn_b1, L0_ffn_w2, L0_ffn_b2)
    x = x + _L0_attn_ref(_layernorm(x, axis=-1), L0_attn_in_proj_w, L0_attn_conv_w, L0_attn_conv_b, L0_attn_out_proj_w, L0_attn_log_dt, L0_attn_A_re, L0_attn_A_im, L0_attn_C_re, L0_attn_C_im, L0_attn_D_skip)
    x = x + 0.5 * _L0_ffn_ref(_layernorm(x, axis=-1), L0_ffn_wqkv, L0_ffn_q_scale, L0_ffn_k_scale, L0_ffn_wo, L0_ffn_ln_g, L0_ffn_ln_b, L0_ffn_w1, L0_ffn_b1, L0_ffn_w2, L0_ffn_b2)
    return x

_drawn_inputs = setup_inputs


def setup_inputs(seed=0):
    import zlib

    import numpy as np

    out = dict(_drawn_inputs(seed))
    spreads = {'L0_attn_conv_b': (0.0, 0.8),
     'L0_attn_A_re': (-0.5, 0.6),
     'L0_ffn_q_scale': (1.0, 0.6),
     'L0_ffn_k_scale': (1.0, 0.6),
     'L0_ffn_ln_g': (1.0, 0.6),
     'L0_ffn_ln_b': (0.0, 0.8),
     'L0_ffn_b1': (0.0, 0.8),
     'L0_ffn_b2': (0.0, 0.1)}
    factors = {'L0_attn_in_proj_w': 8.0,
     'L0_attn_conv_w': 8.0,
     'L0_attn_out_proj_w': 8.0,
     'L0_attn_log_dt': 64.0,
     'L0_attn_A_im': 64.0,
     'L0_attn_C_re': 64.0,
     'L0_attn_C_im': 64.0,
     'L0_attn_D_skip': 8.0,
     'L0_ffn_wqkv': 3.356,
     'L0_ffn_wo': 3.345,
     'L0_ffn_w1': 5.294,
     'L0_ffn_w2': 5.208}
    for name, (base, spread) in spreads.items():
        noise = np.random.default_rng([zlib.crc32(name.encode()), seed]).standard_normal(out[name].shape)
        drawn = base * np.exp(spread * noise) if base else spread * noise
        out[name] = jnp.asarray(drawn.astype(out[name].dtype))
    for name, factor in factors.items():
        out[name] = (out[name] * factor).astype(out[name].dtype)
    return out
```

```python
from contextlib import ExitStack

import numpy as np

import concourse.bass as bass
from concourse import mybir

F32 = mybir.dt.float32
BF16 = mybir.dt.bfloat16
ALU = mybir.AluOpType
ACT = mybir.ActivationFunctionType
AX = mybir.AxisListType

P = 128
B, N = 2, 1024
T = B * N
TILES = T // P
SEQ_TILES = N // P
CHUNK = 512
CHUNKS = T // CHUNK
D = 128
H, DH = 8, 64
INNER = H * DH
WIN = 64
DEPTH = 2
HID = D * 4 * 2 // 3
HB = [(f, min(P, HID - f)) for f in range(0, HID, P)]
EPS = 1e-5
MASKED = -1e38

C_ID, C_CEN, C_ONE, C_FLAG, C_W = 0, P, 2 * P, 3 * P, 3 * P + TILES
NPAR = 10

INITS = 8
DIN, NS = 2 * D, 16
GC = P // NS
GR = DIN // GC
TV = list(range(16)) + [16 * a for a in range(8)] + [16 * a + 1 for a in range(8)] + [P]
NTV = len(TV)
SEL = 2 * P - GC
TRING = 2
ARENA = 37920
MIX_LOADS = 8
PI_A = 6.28125
PI_B = float(np.float32(np.round((2 * np.pi - PI_A) * 2 ** 20) / 2 ** 20))
PI_C = float(np.float32(2 * np.pi - PI_A - PI_B))
PI_IN = 3.1415925
MAGIC = 1.5 * 2 ** 23
T_BANKS = 2


def bc(ap, shape):
    return ap.to_broadcast(list(shape))


def build(nc, ins, kpad, out):
    with ExitStack() as ctx:
        def sb(name, shape, dt=F32):
            return ctx.enter_context(nc.sbuf_tensor(name, shape, dt))

        def sem(name):
            return ctx.enter_context(nc.semaphore(name))

        consts = sb("consts", [P, C_W])
        ident = consts[:, C_ID:C_ID + P]
        center = consts[:, C_CEN:C_CEN + P]
        ones = consts[:, C_ONE:C_ONE + P]
        flag = consts[:, C_FLAG:C_FLAG + TILES]
        ident_bf = sb("ident_bf", [P, P], BF16)
        masks = sb("masks", [P, TILES, P], BF16)
        par = sb("par", [P, NPAR])
        x_main = sb("x_main", [P, T])
        xa = sb("xa", [P, 1 + T])
        xb = sb("xb", [P, 1 + T])
        wqkv = sb("wqkv", [P, 3 * INNER])
        wo = sb("wo", [P, INNER // P, D])
        w1 = sb("w1", [P, 2 * HID])
        w2 = sb("w2", [P, len(HB), D])
        exp_half = sb("exp_half", [P, TILES])
        kT = sb("kT", [P, 4, 4, WIN])
        v = [sb(f"v{i}", [P, H, DH + 1]) for i in range(2)]
        vmix = [sb(f"vmix{i}", [P, H, DH + 1]) for i in range(2)]
        ssum = sb("ssum", [P, 2 * H])
        smax = sb("smax", [P, 2 * H])
        rn = sb("rn", [P, 2 * H])
        mx = sb("mx", [P, H])
        rsum = sb("rsum", [P, H])
        vare = sb("vare", [P, TILES])
        rstd = sb("rstd", [P, TILES])
        arena = sb("arena", [P, ARENA])

        def carver(at):
            def take(*shape):
                nonlocal at
                n = int(np.prod(shape))
                ap = arena[:, at:at + n]
                at += n
                assert at <= ARENA, at
                names = "abcde"[:len(shape)]
                if len(shape) > 1:
                    ap = ap.rearrange(f"p ({' '.join(names)}) -> p {' '.join(names)}",
                                      **{k: v_ for k, v_ in zip(names, shape)})
                return ap
            return take
        common = 2 * CHUNK + CHUNK
        take = carver(0)
        sqf = take(2, CHUNK)
        diag = take(4, P)
        rot_a = take(DEPTH, TILES, 2, DH)
        rot_b = take(DEPTH, TILES, 2, DH)
        raw_c = take(SEQ_TILES, 2, DH)
        raw_s = take(SEQ_TILES, 2, DH)
        qks = take(DEPTH, 2, DH)
        raw_m = take(2, P)
        hs = [take(P) for _ in range(2)]
        sq = take(2 * INNER)
        t1 = take(2 * INNER)
        t2 = take(2 * INNER)
        qkn = take(2 * INNER)
        qT = take(4, P)
        subt = take(2, 4, P)
        prob = take(2, 4, P)
        pT = take(2, 4, P)
        on = take(H, DH)
        oT = take(4, P)
        hsh = take(2, CHUNK)
        y = take(T)
        gel = take(2, CHUNK)
        hid = take(2, CHUNK)
        take = carver(common)
        v_t = take(2, GR, P)
        g_t = take(2, GR, P)
        xs = take(2, TILES, P)
        ysb = xs.rearrange("p a b c -> p (a b c)").rearrange("p (h t) -> p h t", t=TILES)
        x_tok = take(DIN, TILES)
        zs1 = take(T)
        zs = [xb[:, 1:1 + T], zs1]
        toep = take(TRING, GC, P)
        w_t = take(2, GR, NTV)
        ust = take(2, GR, TILES)
        sh = take(2, GR, TILES)
        rbd = take(2, 2, 4, GC, TILES)
        tmp = sqf
        yz = rbd.rearrange("p a b c d e -> p (a b c d e)").rearrange("p (a b) -> p a b", a=4)
        ipw = take(2 * DIN)
        opw = take(2, D)
        sel = take(SEL)
        tv = take(NTV)
        blockd = take(GC)
        early = rbd.rearrange("p a b c d e -> p (a b c d e)")
        cw, ipk = (early[:, i * 4 * DIN:(i + 1) * 4 * DIN].rearrange("p (k h) -> p k h", k=4) for i in range(2))
        prm = take(5, GR)
        chp = take(4)
        early = sh.rearrange("p a b c -> p (a b c)")
        sm = early[:, 0:12 * GR].rearrange("p (i g) -> p i g", g=GR)
        ca = early[:, 16 * GR:32 * GR].rearrange("p (c g a) -> p c g a", c=2, g=GR)
        kp = ust.rearrange("p a b c -> p (a b c)")[:, 0:4 * P].rearrange("p (a t) -> p a t", a=2)
        pre = [x_tok.rearrange("p a b -> p (a b)"), xs.rearrange("p a b c -> p (a b c)")]

        bank = [ctx.enter_context(nc.psum_tensor(f"bank{i}", [P, CHUNK], F32)) for i in range(8)]
        QK = [bank[0], bank[1]]
        SC = [bank[2], bank[3]]
        TB = [bank[4], bank[5]]
        OB = [bank[6], bank[7]]
        WO = bank[7][:, 384:512]

        s_const = sem("s_const")
        s_mask = sem("s_mask")
        s_raw = sem("s_raw")
        s_x = sem("s_x")
        s_wa = sem("s_wa")
        s_wf = sem("s_wf")
        s_rot = sem("s_rot")
        s_init = sem("s_init")
        s_hs = sem("s_hs")
        s_qk = sem("s_qk")
        s_sq = sem("s_sq")
        s_t12 = sem("s_t12")
        s_ss = sem("s_ss")
        s_ssm = sem("s_ssm")
        s_rn = sem("s_rn")
        s_add = sem("s_add")
        s_qkn = sem("s_qkn")
        s_T = sem("s_T")
        s_Tf = sem("s_Tf")
        s_sc = sem("s_sc")
        s_mx = sem("s_mx")
        s_sub = sem("s_sub")
        s_exp = sem("s_exp")
        s_pv = sem("s_pv")
        s_vm = sem("s_vm")
        s_rs = sem("s_rs")
        s_on = sem("s_on")
        s_wo = sem("s_wo")
        s_res = sem("s_res")
        s_hsh = sem("s_hsh")
        s_cen = sem("s_cen")
        s_csb = sem("s_csb")
        s_sqf = sem("s_sqf")
        s_var = sem("s_var")
        s_vare = sem("s_vare")
        s_rstd = sem("s_rstd")
        s_diag = sem("s_diag")
        s_rb = sem("s_rb")
        s_yn = sem("s_yn")
        s_y = sem("s_y")
        s_ag = sem("s_ag")
        s_gel = sem("s_gel")
        s_hid = sem("s_hid")
        s_down = sem("s_down")
        s_xa = sem("s_xa")
        s_mac = sem("s_mac")
        s_mc = sem("s_mc")
        s_dt = sem("s_dt")
        s_tr = sem("s_tr")
        s_mag = sem("s_mag")
        s_ph = sem("s_ph")
        s_trig = sem("s_trig")
        s_link = sem("s_link")
        s_g = sem("s_g")
        s_row = sem("s_row")
        s_vt = sem("s_vt")
        s_ve = sem("s_ve")
        s_kk = sem("s_kk")
        s_kp = sem("s_kp")
        s_kd = sem("s_kd")
        s_toep = [sem(f"s_toep{i}") for i in range(TRING)]
        s_ipk = sem("s_ipk")
        s_in = sem("s_in")
        s_silu = sem("s_silu")
        s_xt = sem("s_xt")
        s_xe = sem("s_xe")
        s_u = sem("s_u")
        s_um = sem("s_um")
        s_ur = sem("s_ur")
        s_r = sem("s_r")
        s_yg = sem("s_yg")
        s_yb = sem("s_yb")
        s_ye = sem("s_ye")
        s_yt = sem("s_yt")
        s_yz = sem("s_yz")
        s_op = sem("s_op")
        s_mix = sem("s_mix")
        s_out = sem("s_out")

        K_SLOT = {(0, 0): 0, (1, 0): 1, (1, 1): 2, (0, 1): 3}

        def xa_count(layers, m):
            return (layers + 2 * m + 1) * CHUNKS

        def t_before(s):
            return 3 + 6 * (s - 2)

        def t_base(lx):
            return lx * (6 * TILES)

        def steps(eng, step):
            step(0, 0)
            step(1, 1)
            step(2, 0)
            step(3, 1)
            with eng.Fori(0, (TILES - 4) // 2) as i:
                step(2 * i + 4, 0)
                step(2 * i + 5, 1)
            step(TILES, 0)
            step(TILES + 1, 1)

        def live(s, lag):
            return not isinstance(s, int) or 0 <= s - lag < TILES

        def t_uses(s):
            if isinstance(s, int) and s < 2:
                names = ["qT", "kT", "v"] if s == 1 else []
                first, par_ = 0, 0
            elif isinstance(s, int) and s == TILES + 1:
                names = ["pT0", "pT1", "oT"]
                first, par_ = t_before(s), 1
            else:
                names = ["qT", "kT", "pT0", "pT1", "v", "oT"]
                first, par_ = t_before(s), 1
            return {n: (first + j, (par_ + j) % 2) for j, n in enumerate(names)}

        def col(t, width=P):
            return bass.ds(t * P, width)

        def attention_pe(pe, lx):
            pe.wait_ge(s_wa, (lx + 1) * 32)
            base, tb = lx * TILES, t_base(lx)

            def take(uses, name):
                n, b = uses[name]
                if not isinstance(n, int) or n >= T_BANKS:
                    pe.wait_ge(s_Tf, tb + n - 1)
                return TB[b]

            def step(s, p):
                uses = t_uses(s)
                if live(s, 1):
                    pe.wait_ge(s_qkn, base + s)
                    for name, o in (("qT", 0), ("kT", INNER)):
                        bk = take(uses, name)
                        for j in range(4):
                            last = pe.transpose(bk[:, j * P:(j + 1) * P], qkn[:, o + j * P:o + (j + 1) * P], ident)
                        last.then_inc(s_T, 1)
                if live(s, 0):
                    pe.wait_ge(s_hs, base + s + 1)
                    if not isinstance(s, int) or s > 0:
                        pe.wait_ge(s_sq, base + s)
                    for j in range(2):
                        last = pe.matmul(QK[j][:, :], hs[p][:, :], wqkv[:, j * INNER:(j + 1) * INNER],
                                         start=True, stop=True)
                    last.then_inc(s_qk, 1)
                if live(s, 2):
                    pe.wait_ge(s_exp, base + s - 1)
                    for r in range(2):
                        bk = take(uses, f"pT{r}")
                        for j in range(4):
                            last = pe.transpose(bk[:, j * P:(j + 1) * P], prob[:, r, j, :], ident)
                        last.then_inc(s_T, 1)
                if live(s, 1):
                    pe.wait_ge(s_Tf, tb + uses["kT"][0] + 1)
                    if not isinstance(s, int) or s > 1:
                        pe.wait_ge(s_sub, base + s - 1)
                    q = 1 - p
                    for r in range(2):
                        pe.matmul(SC[r][:, :], ident_bf[:, :],
                                  bc(masks[:, bass.ds(s - 1, 1), :], (P, 4, P)),
                                  start=True, stop=False, skip_group_check=True)
                    for hb in range(4):
                        for w in range(2):
                            ka = K_SLOT[(q, 0)]
                            kb = K_SLOT[(q, 1)] if w else K_SLOT[(1 - q, 1)]
                            for r in range(2):
                                last = pe.matmul(
                                    SC[r][WIN * w:WIN * (w + 1), hb * P:(hb + 1) * P],
                                    qT[DH * r:DH * (r + 1), hb, WIN * w:WIN * (w + 1)],
                                    kT[DH * r:DH * (r + 1), hb, ka:kb + 1:kb - ka, :],
                                    start=False, stop=True, skip_group_check=True)
                    last.then_inc(s_sc, 1)
                if live(s, 2):
                    pe.wait_ge(s_Tf, tb + uses["pT1"][0] + 1)
                    pe.wait_ge(s_vm, base + s - 1)
                    if not isinstance(s, int) or s > 2:
                        pe.wait_ge(s_on, base + s - 2)
                        pe.wait_ge(s_res, base + s - 2)
                    for h in range(H):
                        for w, vv in ((0, vmix[p]), (1, v[p])):
                            last = pe.matmul(OB[h // 4][WIN * w:WIN * (w + 1), (h % 4) * 65:(h % 4 + 1) * 65],
                                             pT[:, h % 2, h // 2, WIN * w:WIN * (w + 1)], vv[:, h, :],
                                             start=True, stop=True, skip_group_check=True)
                    last.then_inc(s_pv, 1)
                if live(s, 1):
                    bk = take(uses, "v")
                    pe.matmul(bk[:, :], hs[1 - p][:, :], wqkv[:, 2 * INNER:3 * INNER],
                              start=True, stop=True).then_inc(s_T, 1)
                if live(s, 2):
                    pe.wait_ge(s_on, base + s - 1)
                    bk = take(uses, "oT")
                    for j in range(4):
                        last = pe.transpose(bk[:, j * P:(j + 1) * P],
                                            on[:, 2 * j:2 * j + 2, :].rearrange("p a b -> p (a b)"), ident)
                    last.then_inc(s_T, 1)
                    pe.wait_ge(s_Tf, tb + uses["oT"][0] + 1)
                    for j in range(4):
                        last = pe.matmul(WO, wo[:, j, :], oT[:, j, :], start=(j == 0), stop=(j == 3),
                                         skip_group_check=True)
                    last.then_inc(s_wo, 1)
            steps(pe, step)

        def attention_act(act, lx):
            base, tb = lx * TILES, t_base(lx)

            def empty(uses, name, dst, src_rearr=None):
                n, b = uses[name]
                act.wait_ge(s_T, tb + n + 1)
                src = TB[b][:, :]
                if src_rearr:
                    src = src.rearrange(src_rearr[0], **src_rearr[1])
                act.activation(dst, src, ACT.Copy).then_inc(s_Tf, 1)

            def step(s, p):
                uses = t_uses(s)
                q = 1 - p
                if live(s, 1):
                    if not isinstance(s, int) or s > 1:
                        act.wait_ge(s_sc, base + s - 1)
                    empty(uses, "qT", qT[:, :, :], ("p (j c) -> p j c", dict(j=4)))
                    a, c = K_SLOT[(q, 0)], K_SLOT[(q, 1)]
                    empty(uses, "kT", kT[:, :, a:c + 1:c - a, :], ("p (j h c) -> p j h c", dict(j=4, h=2)))
                if live(s, 0):
                    if not isinstance(s, int) or s > 0:
                        act.wait_ge(s_ss, base + s)
                    for j in range(2):
                        act.wait_ge(s_t12, 2 * (base + s) + j + 1)
                        last = act.activation(sq[:, j * INNER:(j + 1) * INNER], QK[j][:, :], ACT.Square)
                    last.then_inc(s_sq, 1)
                if live(s, 2):
                    if not isinstance(s, int) or s > 2:
                        act.wait_ge(s_pv, base + s - 2)
                    for r in range(2):
                        empty(uses, f"pT{r}", pT[:, r, :, :], ("p (j c) -> p j c", dict(j=4)))
                if live(s, 1):
                    if not isinstance(s, int) or s > 2:
                        act.wait_ge(s_vm, base + s - 2)
                    empty(uses, "v", v[q][:, :, 0:DH], ("p (h c) -> p h c", dict(h=H)))
                if live(s, 2):
                    if not isinstance(s, int) or s > 2:
                        act.wait_ge(s_wo, base + s - 2)
                    empty(uses, "oT", oT[:, :, :], ("p (j c) -> p j c", dict(j=4)))
                if live(s, 1):
                    act.wait_ge(s_sub, base + s)
                    if not isinstance(s, int) or s > 1:
                        act.wait_ge(s_T, tb + (uses["pT1"][0] + 1))
                    act.activation(prob[:, :, :, :].rearrange("p a b c -> p (a b c)"),
                                   subt[:, :, :, :].rearrange("p a b c -> p (a b c)"), ACT.Exp).then_inc(s_exp, 1)
            steps(act, step)

        def attention_dve(dve, lx, l):
            base, tb = lx * TILES, t_base(lx)

            def stage(s, p):
                if not isinstance(s, int) or s > 1:
                    dve.wait_ge(s_T, tb + t_before(s))
                dve.tensor_tensor(hs[p][64:128, 0:1], xa[64:128, bass.ds(s * P, 1)],
                                  flag[64:128, bass.ds(s, 1)], ALU.mult)
                dve.tensor_copy(hs[p][0:64, :], xa[0:64, bass.ds(s * P + 1, P)])
                dve.tensor_copy(hs[p][64:128, 1:P], xa[64:128, bass.ds(s * P + 1, P - 1)]).then_inc(s_hs, 1)

            def step(s, p):
                if live(s, 0):
                    stage(s, p)
                    dve.wait_ge(s_qk, base + s + 1)
                    if not isinstance(s, int) or s > 0:
                        dve.wait_ge(s_qkn, base + s)
                    row = l * TILES + s
                    ta = rot_a[:, :, :, :, :].rearrange("p l t a d -> p (l t) a d")[:, bass.ds(row, 1), :, :]
                    tbb = rot_b[:, :, :, :, :].rearrange("p l t a d -> p (l t) a d")[:, bass.ds(row, 1), :, :]
                    for j in range(2):
                        src = QK[j][:, :].rearrange("p (h d) -> p h d", h=H)
                        o1 = t1[:, j * INNER:(j + 1) * INNER].rearrange("p (h d) -> p h d", h=H)
                        o2 = t2[:, j * INNER:(j + 1) * INNER].rearrange("p (h d) -> p h d", h=H)
                        dve.tensor_tensor(o1, src, bc(ta[:, :, j, :], (P, H, DH)), ALU.mult)
                        dve.tensor_tensor(o2[:, :, 0:32], src[:, :, 32:64], bc(tbb[:, :, j, 0:32], (P, H, 32)), ALU.mult)
                        dve.tensor_tensor(o2[:, :, 32:64], src[:, :, 0:32], bc(tbb[:, :, j, 32:64], (P, H, 32)),
                                          ALU.mult).then_inc(s_t12, 1)
                    dve.wait_ge(s_sq, base + s + 1)
                    dve.tensor_reduce(ssum[:, :], sq[:, :].rearrange("p (h d) -> p h d", d=DH), AX.X, ALU.add).then_inc(s_ss, 1)
                if live(s, 1):
                    dve.wait_ge(s_sc, base + s)
                    for r in range(2):
                        last = dve.tensor_reduce(mx[:, 4 * r:4 * r + 4], SC[r][:, :].rearrange("p (h d) -> p h d", d=P), AX.X, ALU.max)
                    last.then_inc(s_mx, 1)
                if live(s, 0):
                    dve.wait_ge(s_ss, base + s + 1)
                    if not isinstance(s, int) or s > 0:
                        dve.wait_ge(s_rn, base + s)
                    dve.tensor_scalar(smax[:, :], ssum[:, :], 1e-24, None, ALU.max).then_inc(s_ssm, 1)
                if live(s, 1):
                    dve.wait_ge(s_mx, base + s)
                    if not isinstance(s, int) or s > 1:
                        dve.wait_ge(s_exp, base + s - 1)
                    for r in range(2):
                        last = dve.tensor_tensor(subt[:, r, :, :], SC[r][:, :].rearrange("p (h d) -> p h d", d=P),
                                                 bc(mx[:, 4 * r:4 * r + 4].unsqueeze(2), (P, 4, P)), ALU.subtract)
                    last.then_inc(s_sub, 1)
                if live(s, 2):
                    dve.wait_ge(s_pv, base + s - 1)
                    for g in range(2):
                        ob = OB[g][:, 0:260].rearrange("p (h d) -> p h d", h=4)
                        last = dve.reciprocal(rsum[:, 4 * g:4 * g + 4].unsqueeze(2), ob[:, :, 64:65])
                    last.then_inc(s_rs, 1)
                    dve.wait_ge(s_rs, base + s - 1)
                    for g in range(2):
                        ob = OB[g][:, 0:260].rearrange("p (h d) -> p h d", h=4)
                        last = dve.tensor_tensor(on[:, 4 * g:4 * g + 4, :], ob[:, :, 0:64],
                                                 bc(rsum[:, 4 * g:4 * g + 4].unsqueeze(2), (P, 4, DH)), ALU.mult)
                    last.then_inc(s_on, 1)
                    dve.wait_ge(s_wo, base + s - 1)
                    t = s - 2
                    dve.tensor_tensor(xb[:, bass.ds(t * P + 1, P)], xa[:, bass.ds(t * P + 1, P)], WO, ALU.add).then_inc(s_res, 1)
                if live(s, 1):
                    dve.wait_ge(s_Tf, tb + (t_uses(s)["v"][0] + 1))
                    dve.tensor_copy(vmix[1 - p][0:64, :, :], v[1 - p][0:64, :, :])
                    if not isinstance(s, int) or s > 1:
                        dve.wait_ge(s_pv, base + s - 1)
                    dve.tensor_copy(vmix[p][64:128, :, :], v[1 - p][64:128, :, :]).then_inc(s_vm, 1)
            steps(dve, step)

        def attention_pool(pool, lx):
            base, tb = lx * TILES, t_base(lx)

            def step(s, p):
                if live(s, 0):
                    pool.wait_ge(s_t12, 2 * (base + s + 1))
                    pool.tensor_tensor(t1[:, :], t1[:, :], t2[:, :], ALU.add).then_inc(s_add, 1)
                    pool.wait_ge(s_ssm, base + s + 1)
                    pool.tensor_tensor(rn[:, :], smax[:, :], exp_half[:, :], ALU.pow).then_inc(s_rn, 1)
                if live(s, 0):
                    pool.wait_ge(s_rn, base + s + 1)
                    pool.wait_ge(s_add, base + s + 1)
                    if not isinstance(s, int) or s > 0:
                        n = 2 if isinstance(s, int) and s == 1 else t_before(s) + 2
                        pool.wait_ge(s_T, tb + n)
                    pool.tensor_tensor(qkn[:, :].rearrange("p (h d) -> p h d", d=DH),
                                       t1[:, :].rearrange("p (h d) -> p h d", d=DH),
                                       bc(rn[:, :].unsqueeze(2), (P, 2 * H, DH)), ALU.mult).then_inc(s_qkn, 1)
            steps(pool, step)

        def shift_dve(dve, n, src, ready):
            for c in range(CHUNKS):
                if c > 1:
                    dve.wait_ge(s_cen, n * CHUNKS + c - 1)
                first = int(c % (N // CHUNK) == 0)
                at = c * CHUNK + 1
                dve.wait_ge(*ready(c))
                dve.tensor_copy(hsh[0:64, c % 2, :], src[0:64, at:at + CHUNK])
                if first:
                    dve.memset(hsh[64:128, c % 2, 0:1], 0.0)
                dve.tensor_copy(hsh[64:128, c % 2, first:CHUNK],
                                src[64:128, at - 1 + first:at - 1 + CHUNK]).then_inc(s_hsh, 1)

        def norm_pool(pool, n):
            pool.wait_ge(s_vare, n + 1)
            pool.tensor_tensor(rstd[:, :], vare[:, :], exp_half[:, 0:TILES], ALU.pow).then_inc(s_rstd, 1)

        def norm_pe(pe, n, src, shifted, ready, n_plain=0):
            def var(c):
                pe.wait_ge(s_sqf, n * CHUNKS + c + 1)
                for j in range(4):
                    last = pe.matmul(bank[4][:, 4 * c + j:4 * c + j + 1], sqf[:, c % 2, j * P:(j + 1) * P],
                                     ones[:, 0:1], start=True, stop=True, skip_group_check=True)
                last.then_inc(s_var, 1)
            for c in range(CHUNKS):
                k = n * CHUNKS + c
                if shifted:
                    pe.wait_ge(s_hsh, (n - n_plain) * CHUNKS + c + 1)
                    rhs = hsh[:, c % 2, :]
                else:
                    pe.wait_ge(*ready(c))
                    rhs = src[:, c * CHUNK:(c + 1) * CHUNK]
                pe.matmul(bank[c][:, :], center, rhs, start=True, stop=True).then_inc(s_cen, 1)
                if c:
                    var(c - 1)
            var(CHUNKS - 1)
            for c in range(CHUNKS):
                k = n * CHUNKS + c
                pe.wait_ge(s_diag, k + 1)
                if c > 1:
                    pe.wait_ge(s_yn, k - 1)
                pe.matmul(bank[5 + c % 2][:, :], ones, diag[:, :, :].rearrange("p a b -> p (a b)"),
                          start=True, stop=True).then_inc(s_rb, 1)

        def norm_act(act, n, dst, off):
            for c in range(CHUNKS):
                k = n * CHUNKS + c
                act.wait_ge(s_cen, k + 1)
                if c > 1:
                    act.wait_ge(s_var, k - 1)
                act.activation(sqf[:, c % 2, :], bank[c][:, :], ACT.Square).then_inc(s_sqf, 1)
                act.activation(dst[:, off + c * CHUNK:off + (c + 1) * CHUNK], bank[c][:, :], ACT.Copy).then_inc(s_csb, 1)

        def norm_dve(dve, n, dst, off, gb):
            dve.wait_ge(s_var, (n + 1) * CHUNKS)
            dve.tensor_scalar(vare[:, :], bank[4][:, 0:TILES], 1.0 / D, EPS, ALU.mult, ALU.add).then_inc(s_vare, 1)
            dve.wait_ge(s_rstd, n + 1)
            for c in range(CHUNKS):
                k = n * CHUNKS + c
                if c:
                    dve.wait_ge(s_rb, k)
                dve.tensor_tensor(diag[:, :, :], bc(ident.unsqueeze(1), (P, 4, P)),
                                  bc(rstd[:, 4 * c:4 * c + 4].unsqueeze(2), (P, 4, P)), ALU.mult).then_inc(s_diag, 1)
                dve.wait_ge(s_rb, k + 1)
                dve.wait_ge(s_csb, k + 1)
                d = dst[:, off + c * CHUNK:off + (c + 1) * CHUNK]
                dve.tensor_tensor(d, d, bank[5 + c % 2][:, :], ALU.mult).then_inc(s_yn, 1)
                if gb is not None:
                    dve.wait_ge(s_yn, k + 1)
                    dve.tensor_scalar(d, d, gb[0], gb[1], ALU.mult, ALU.add).then_inc(s_y, 1)
                else:
                    dve.wait_ge(s_yn, k + 1)
                    dve.sem_inc(s_y, 1)
                    dve.sem_inc(s_xa, 1)

        FB = len(HB)

        def up(c):
            return 2 * (c % 2)

        def ffn_pe(pe, lx, n, m):
            pe.wait_ge(s_wf, (lx + 1) * (16 * (FB + 2)))
            pe.wait_ge(s_csb, (n + 1) * CHUNKS)
            kb = lx * (CHUNKS * FB)

            def down(u):
                c, f = divmod(u, FB)
                _, w = HB[f]
                if f == 0:
                    if c > 1:
                        pe.wait_ge(s_xa, xa_count(lx, m) + c - 1)
                    else:
                        pe.wait_ge(s_yn, (n + 1) * CHUNKS)
                pe.wait_ge(s_hid, kb + u + 1)
                last = pe.matmul(bank[6 + c % 2][:, :], w2[0:w, f, :], hid[0:w, u % 2, :],
                                 start=(f == 0), stop=(f == FB - 1))
                last.then_inc(s_down, 1)
            for u in range(CHUNKS * FB):
                c, f = divmod(u, FB)
                at, w = HB[f]
                if f == 0:
                    pe.wait_ge(s_y, n * CHUNKS + c + 1)
                if u > 1:
                    pe.wait_ge(s_hid, kb + u - 1)
                for g in range(2):
                    last = pe.matmul(bank[2 * (u % 2) + g][0:w, :], w1[:, g * HID + at:g * HID + at + w],
                                     y[:, c * CHUNK:(c + 1) * CHUNK], start=True, stop=True)
                last.then_inc(s_ag, 1)
                if u:
                    down(u - 1)
            down(CHUNKS * FB - 1)

        def ffn_act(act, lx):
            kb = lx * (CHUNKS * FB)
            for u in range(CHUNKS * FB):
                c, f = divmod(u, FB)
                _, w = HB[f]
                act.wait_ge(s_ag, kb + u + 1)
                if u > 1:
                    act.wait_ge(s_hid, kb + u - 1)
                act.activation(gel[0:w, u % 2, :], bank[2 * (u % 2) + 1][0:w, :], ACT.Gelu,
                               bias=par[0:w, 7 + f:8 + f]).then_inc(s_gel, 1)

        def ffn_dve(dve, lx):
            kb = lx * (CHUNKS * FB)

            def finish(c):
                dve.wait_ge(s_down, kb + (c + 1) * FB)
                sl = slice(1 + c * CHUNK, 1 + (c + 1) * CHUNK)
                dve.scalar_tensor_tensor(out=xa[:, sl], in0=bank[6 + c % 2][:, :], scalar=par[:, 2:3],
                                         in1=xb[:, sl], op0=ALU.add, op1=ALU.add).then_inc(s_xa, 1)
            for u in range(CHUNKS * FB):
                c, f = divmod(u, FB)
                _, w = HB[f]
                dve.wait_ge(s_gel, kb + u + 1)
                if u > 1:
                    dve.wait_ge(s_down, kb + u - 1)
                dve.scalar_tensor_tensor(out=hid[0:w, u % 2, :], in0=bank[2 * (u % 2)][0:w, :],
                                         scalar=par[0:w, 4 + f:5 + f], in1=gel[0:w, u % 2, :],
                                         op0=ALU.add, op1=ALU.mult).then_inc(s_hid, 1)
                if f == 0 and c:
                    finish(c - 1)
            finish(CHUNKS - 1)

        def layer_norm_index(m, l):
            return 4 * m + 1 + l

        def outer(m):
            return 4 * m

        def main_ready(m):
            return lambda c: (s_x, 16) if m == 0 else (s_mix, CHUNKS)

        def masks_dve(dve):
            dve.tensor_copy(ident_bf[:, :], ident)
            for t in range(0, TILES, SEQ_TILES):
                dve.tensor_copy(masks[:, t, :], raw_m[:, 0, :])
                last = dve.tensor_copy(masks[:, t + 1:t + SEQ_TILES, :], bc(raw_m[:, 1:2, :], (P, SEQ_TILES - 1, P)))
            last.then_inc(s_mask, 1)

        def rotary_dve(dve, m):
            dve.wait_ge(s_raw, 48 * (m + 1))
            for l in range(DEPTH):
                for half in range(B):
                    t = slice(half * SEQ_TILES, (half + 1) * SEQ_TILES)
                    for tab, raw, to, fro in ((rot_a, raw_c, slice(0, DH), slice(0, DH)),
                                              (rot_b, raw_s, slice(0, 32), slice(32, 64)),
                                              (rot_b, raw_s, slice(32, 64), slice(0, 32))):
                        last = dve.tensor_tensor(tab[:, l, t, :, to], raw[:, :, :, to],
                                                 bc(qks[:, l, :, fro].unsqueeze(1), (P, SEQ_TILES, 2, to.stop - to.start)),
                                                 ALU.mult)
            last.then_inc(s_rot, 1)
            dve.wait_ge(s_rot, m + 1)

        def macaron_pe(pe, m):
            norm_pe(pe, outer(m), x_main, False, main_ready(m))
            with pe.Fori(0, DEPTH) as l:
                lx = l + DEPTH * m
                attention_pe(pe, lx)
                norm_pe(pe, layer_norm_index(m, l), xb, True, None, n_plain=1 + 2 * m - 0)
                ffn_pe(pe, lx, layer_norm_index(m, l), m)

        def macaron_act(act, m):
            norm_act(act, outer(m), xa, 1)
            with act.Fori(0, DEPTH) as l:
                lx = l + DEPTH * m
                attention_act(act, lx)
                norm_act(act, layer_norm_index(m, l), y, 0)
                ffn_act(act, lx)

        def macaron_dve(dve, m):
            rotary_dve(dve, m)
            norm_dve(dve, outer(m), xa, 1, None)
            with dve.Fori(0, DEPTH) as l:
                lx = l + DEPTH * m
                dve.wait_ge(s_y, layer_norm_index(m, l) * CHUNKS)
                attention_dve(dve, lx, l)
                shift_dve(dve, layer_norm_index(m, l), xb, lambda c: (s_res, lx * TILES + (c + 1) * (CHUNK // P)))
                dve.wait_ge(s_wf, (lx + 1) * (16 * (FB + 2)))
                norm_dve(dve, layer_norm_index(m, l), y, 0, (par[:, 0:1], par[:, 1:2]))
                ffn_dve(dve, lx)
            dve.wait_ge(s_xa, xa_count(DEPTH * (m + 1), m))
            dve.scalar_tensor_tensor(out=x_main[:, :], in0=xa[:, 1:1 + T], scalar=0.5, in1=x_main[:, :],
                                     op0=ALU.mult, op1=ALU.add).then_inc(s_mac, 1)

        def macaron_pool(pool, m):
            norm_pool(pool, outer(m))
            with pool.Fori(0, DEPTH) as l:
                lx = l + DEPTH * m
                pool.wait_ge(s_y, layer_norm_index(m, l) * CHUNKS)
                pool.wait_ge(s_xa, xa_count(lx, m))
                attention_pool(pool, lx)
                norm_pool(pool, layer_norm_index(m, l))

        NMIX = outer(0) + 3

        def mixer_pe(pe):
            pe.wait_ge(s_mc, 16 * MIX_LOADS)
            pe.wait_ge(s_g, 1)
            pe.wait_ge(s_mac, 1)
            for g in range(GR):
                q, half = g % (P // GC), g // (P // GC)
                last = pe.matmul(bank[7][:, half * P:(half + 1) * P], sel[:, P - GC - GC * q:2 * P - GC - GC * q],
                                 g_t[:, 0, g, :], start=(q == 0), stop=(q == P // GC - 1), skip_group_check=True)
            last.then_inc(s_kk, 1)
            for c in range(2):
                pe.wait_ge(s_row, c + 1)
                row = pre[1].rearrange("p (g t) -> p g t", g=GR)
                for k in range(GR // 4):
                    n = c * (GR // 4) + k
                    if n > 1:
                        pe.wait_ge(s_ve, n - 1)
                    for j in range(4):
                        last = pe.transpose(bank[n % 2][:, j * P:(j + 1) * P], row[:, 4 * k + j, :], ident)
                    last.then_inc(s_vt, 1)
            pe.wait_ge(s_ve, 2 * (GR // 4))
            norm_pe(pe, NMIX, x_main, False, lambda c: (s_mac, 1))
            pe.wait_ge(s_ipk, 1)
            u = 0
            for e in range(4):
                for c in range(CHUNKS):
                    if e == 0:
                        pe.wait_ge(s_y, NMIX * CHUNKS + CHUNKS)
                        pe.wait_ge(s_csb, (NMIX + 1) * CHUNKS)
                    if u > 1:
                        pe.wait_ge(s_silu, u - 1)
                    bk = bank[u % 2]
                    at = 1 + c * CHUNK
                    if e < 2:
                        for k in range(4):
                            cut = k if c % 2 == 0 else 0
                            last = pe.matmul(bk[:, cut:CHUNK], ipk[:, 3 - k, e * P:(e + 1) * P],
                                             xa[:, at + cut - k:at + CHUNK - k], start=(k == 0), stop=(k == 3),
                                             skip_group_check=True)
                    else:
                        last = pe.matmul(bk[:, :], ipw[:, e * P:(e + 1) * P], xa[:, at:at + CHUNK],
                                         start=True, stop=True)
                    last.then_inc(s_in, 1)
                    u += 1
            for blk in range(2):
                for c in range(CHUNKS):
                    n = blk * CHUNKS + c
                    pe.wait_ge(s_silu, n + 1)
                    if n > 1:
                        pe.wait_ge(s_xe, n - 1)
                    for j in range(4):
                        last = pe.transpose(bank[2 + n % 2][:, j * P:(j + 1) * P], xs[:, blk, 4 * c + j, :], ident)
                    last.then_inc(s_xt, 1)
            pe.wait_ge(s_xe, 2 * CHUNKS)
            for q in range(GR // 4):
                for c in range(2):
                    n = 2 * q + c
                    if n > 1:
                        pe.wait_ge(s_um, n - 1)
                    for j in range(4):
                        g = 4 * q + j
                        last = pe.matmul(bank[4 + n % 2][:, j * P:(j + 1) * P], v_t[:, c, g, :],
                                         x_tok[:, g * GC:(g + 1) * GC, :].rearrange("p h t -> p (h t)"),
                                         start=True, stop=True, skip_group_check=True)
                    last.then_inc(s_u, 1)
            for q in range(GR // 4):
                pe.wait_ge(s_r, 2 * q + 2)
                if q > 1:
                    pe.wait_ge(s_ye, q - 1)
                for j in range(4):
                    g = 4 * q + j
                    pe.wait_ge(s_toep[g % TRING], 16 * (g // TRING + 1))
                    for c in range(2):
                        pe.matmul(bank[6 + q % 2][:, j * P:(j + 1) * P], g_t[:, c, g, :],
                                  rbd[:, q % 2, c, j, :, :].rearrange("p h t -> p (h t)"),
                                  start=(c == 0), stop=False, skip_group_check=True)
                    for hh in range(GC):
                        last = pe.matmul(bank[6 + q % 2][:, j * P + hh * TILES:j * P + (hh + 1) * TILES],
                                         toep[:, g % TRING, hh, :], x_tok[:, g * GC + hh, :],
                                         start=False, stop=True, skip_group_check=True)
                    last.then_inc(s_yg, 1)
            pe.wait_ge(s_ye, GR // 4)

            def project(c):
                pe.wait_ge(s_yz, 2 * c + 2)
                if c > 1:
                    pe.wait_ge(s_mix, c - 1)
                for blk in range(2):
                    last = pe.matmul(bank[2 + c % 2][:, :], opw[:, blk, :], yz[:, 2 * (c % 2) + blk, :],
                                     start=(blk == 0), stop=(blk == 1))
                last.then_inc(s_op, 1)
            for c in range(CHUNKS):
                for blk in range(2):
                    n = 2 * c + blk
                    if n > 1:
                        pe.wait_ge(s_yz, n - 1)
                    for j in range(4):
                        last = pe.transpose(bank[n % 2][:, j * P:(j + 1) * P],
                                            ysb[:, blk * P:(blk + 1) * P, 4 * c + j], ident)
                    last.then_inc(s_yt, 1)
                if c:
                    project(c - 1)
            project(CHUNKS - 1)

        def mixer_act(act):
            act.wait_ge(s_mc, 16 * MIX_LOADS)
            act.activation(sm[:, 0, :], prm[:, 0, :], ACT.Exp).then_inc(s_dt, 1)
            act.wait_ge(s_tr, 1)
            wf = w_t.rearrange("p c g t -> p c (g t)")
            act.activation(pre[0][:, 0:GR * NTV], pre[0][:, 0:GR * NTV], ACT.Exp).then_inc(s_mag, 1)
            act.wait_ge(s_ph, 1)
            act.activation(wf[:, 1, :], wf[:, 1, :], ACT.Sin).then_inc(s_trig, 1)
            act.activation(wf[:, 0, :], wf[:, 0, :], ACT.Sin).then_inc(s_trig, 1)
            for n in range(2 * (GR // 4)):
                c, k = divmod(n, GR // 4)
                act.wait_ge(s_vt, n + 1)
                act.activation(v_t[:, c, 4 * k:4 * k + 4, :].rearrange("p g t -> p (g t)"), bank[n % 2][:, :],
                               ACT.Copy).then_inc(s_ve, 1)
            norm_act(act, NMIX, xa, 1)
            u = 0
            for e in range(4):
                for c in range(CHUNKS):
                    act.wait_ge(s_in, u + 1)
                    if e < 2:
                        act.activation(xs[:, e, 4 * c:4 * c + 4, ::-1], bank[u % 2][:, :].rearrange("p (t i) -> p t i", i=P),
                                       ACT.Silu, bias=chp[:, e:e + 1]).then_inc(s_silu, 1)
                    else:
                        act.activation(zs[e - 2][:, c * CHUNK:(c + 1) * CHUNK], bank[u % 2][:, :],
                                       ACT.Silu).then_inc(s_silu, 1)
                    u += 1
            for n in range(2 * CHUNKS):
                blk, c = divmod(n, CHUNKS)
                act.wait_ge(s_xt, n + 1)
                act.activation(x_tok[:, blk * P:(blk + 1) * P, 4 * c:4 * c + 4].rearrange("p h t -> p t h"),
                               bank[2 + n % 2][:, :].rearrange("p (t h) -> p t h", t=4), ACT.Copy).then_inc(s_xe, 1)
            for q in range(GR // 4):
                act.wait_ge(s_yg, 4 * q + 4)
                act.activation(ysb[:, 4 * q * GC:4 * (q + 1) * GC, :].rearrange("p h t -> p (h t)"),
                               bank[6 + q % 2][:, :], ACT.Copy).then_inc(s_ye, 1)

        def mixer_dve(dve):
            linked = [0]

            def link(ins):
                linked[0] += 1
                ins.then_inc(s_link, 1)
                dve.wait_ge(s_link, linked[0])
            dve.wait_ge(s_mc, 16 * MIX_LOADS)
            wf = w_t.rearrange("p c g t -> p c (g t)")
            n_t = GR * NTV
            dt, ar, ai = sm[:, 0, :], sm[:, 1, :], sm[:, 2, :]
            a_re, a_im, c_re, c_im = (prm[:, i, :] for i in range(1, 5))
            dve.tensor_tensor(ipk, cw, bc(ipw[:, 0:DIN].unsqueeze(1), (P, 4, DIN)), ALU.mult).then_inc(s_ipk, 1)
            dve.wait_ge(s_dt, 1)
            dve.tensor_tensor(ar, dt, a_re, ALU.mult)
            link(dve.tensor_tensor(ai, dt, a_im, ALU.mult))
            gt = lambda ap: ap.rearrange("p (g t) -> p g t", g=GR)
            ph = pre[1][:, 0:n_t]
            kk = pre[1][:, n_t:2 * n_t]
            tvb = bc(tv.unsqueeze(1), (P, GR, NTV))
            dve.tensor_tensor(gt(pre[0][:, 0:n_t]), bc(ar.unsqueeze(2), (P, GR, NTV)), tvb, ALU.mult).then_inc(s_tr, 1)
            link(dve.tensor_tensor(gt(ph), bc(ai.unsqueeze(2), (P, GR, NTV)), tvb, ALU.mult))
            for c, quarter in ((1, 0.0), (0, 0.25)):
                r = wf[:, c, :]
                link(dve.tensor_scalar(kk, ph, 1 / (2 * np.pi), quarter, ALU.mult, ALU.add))
                link(dve.tensor_scalar(kk, kk, MAGIC, None, ALU.add))
                link(dve.tensor_scalar(kk, kk, -MAGIC, None, ALU.add))
                link(dve.scalar_tensor_tensor(out=r, in0=kk, scalar=-PI_A, in1=ph, op0=ALU.mult, op1=ALU.add))
                link(dve.scalar_tensor_tensor(out=r, in0=kk, scalar=-PI_B, in1=r, op0=ALU.mult, op1=ALU.add))
                link(dve.scalar_tensor_tensor(out=r, in0=kk, scalar=-PI_C, in1=r, op0=ALU.mult, op1=ALU.add))
                link(dve.tensor_scalar(r, r, 2 * np.pi * quarter, PI_IN, ALU.add, ALU.min))
                last = dve.tensor_scalar(r, r, -PI_IN, None, ALU.max)
                link(last)
            dve.sem_inc(s_ph, 1)
            dve.wait_ge(s_mag, 1)
            dve.wait_ge(s_trig, 2)
            link(dve.tensor_tensor(w_t.rearrange("p c g t -> p c (g t)"), w_t.rearrange("p c g t -> p c (g t)"),
                                   bc(pre[0][:, 0:n_t].unsqueeze(1), (P, 2, n_t)), ALU.mult))
            w1r, w1i = w_t[:, 0, :, 1], w_t[:, 1, :, 1]
            s_ = lambda i: sm[:, i, :]
            tt = dve.tensor_tensor
            tt(s_(3), a_re, a_re, ALU.mult)
            link(tt(s_(4), a_im, a_im, ALU.mult))
            link(tt(s_(3), s_(3), s_(4), ALU.add))
            link(dve.reciprocal(s_(3), s_(3)))
            link(dve.tensor_scalar(s_(4), w1r, -1.0, None, ALU.add))
            tt(s_(5), s_(4), a_re, ALU.mult)
            tt(s_(6), w1i, a_im, ALU.mult)
            tt(s_(7), w1i, a_re, ALU.mult)
            link(tt(s_(8), s_(4), a_im, ALU.mult))
            tt(s_(5), s_(5), s_(6), ALU.add)
            link(tt(s_(7), s_(7), s_(8), ALU.subtract))
            tt(s_(5), s_(5), s_(3), ALU.mult)
            link(tt(s_(7), s_(7), s_(3), ALU.mult))
            tt(s_(6), c_re, s_(5), ALU.mult)
            tt(s_(8), c_im, s_(7), ALU.mult)
            tt(s_(9), c_re, s_(7), ALU.mult)
            link(tt(s_(10), c_im, s_(5), ALU.mult))
            tt(s_(6), s_(6), s_(8), ALU.subtract)
            link(tt(s_(9), s_(9), s_(10), ALU.add))
            dve.tensor_scalar(s_(6), s_(6), 2.0, None, ALU.mult)
            link(dve.tensor_scalar(s_(9), s_(9), 2.0, None, ALU.mult))
            war, wai = w_t[:, 0, :, 16:24], w_t[:, 1, :, 16:24]
            b8 = lambda i: bc(s_(i).unsqueeze(2), (P, GR, 8))
            x8 = [pre[0][:, i * GR * 8:(i + 1) * GR * 8].rearrange("p (g a) -> p g a", g=GR) for i in range(2)]
            tt(ca[:, 0, :, :], b8(6), war, ALU.mult)
            tt(x8[0], b8(9), wai, ALU.mult)
            tt(ca[:, 1, :, :], b8(6), wai, ALU.mult)
            link(tt(x8[1], b8(9), war, ALU.mult))
            tt(ca[:, 0, :, :], ca[:, 0, :, :], x8[0], ALU.subtract)
            link(tt(ca[:, 1, :, :], ca[:, 1, :, :], x8[1], ALU.add))

            def outer_product(out, ar_, ai_, imag, negate=False):
                o4 = out.rearrange("p g (a b) -> p g a b", b=16)
                t4 = pre[0].rearrange("p (g a b) -> p g a b", g=GR, b=16)
                lo = lambda ap, k: bc(ap[:, k, :].unsqueeze(2), (P, 8, 16))
                wb = w_t[:, :, :, 0:16]
                shape = (P, GR, 8, 16)
                left = lambda ap: bc(ap.unsqueeze(3), shape)
                right = lambda c: bc(wb[:, c, :, :].unsqueeze(2), shape)
                tt(o4, left(ar_), right(1 if imag else 0), ALU.mult)
                link(tt(t4, left(ai_), right(0 if imag else 1), ALU.mult))
                of, tf = out.rearrange("p g t -> p (g t)"), pre[0]
                if negate:
                    return dve.scalar_tensor_tensor(out=of, in0=of, scalar=-1.0, in1=tf, op0=ALU.mult, op1=ALU.subtract)
                return tt(of, of, tf, ALU.add if imag else ALU.subtract)
            outer_product(g_t[:, 0, :, :], ca[:, 0, :, :], ca[:, 1, :, :], False).then_inc(s_g, 1)
            dve.wait_ge(s_g, 1)
            link(outer_product(g_t[:, 1, :, :], ca[:, 0, :, :], ca[:, 1, :, :], True, True))
            row = pre[1].rearrange("p (g t) -> p g t", g=GR)
            for c in range(2):
                if c:
                    dve.wait_ge(s_vt, GR // 4)
                outer_product(row, w_t[:, 0, :, 24:32], w_t[:, 1, :, 24:32], c == 1).then_inc(s_row, 1)
                dve.wait_ge(s_row, c + 1)
            link(dve.memset(kp, 0.0))
            dve.wait_ge(s_kk, 1)
            link(dve.tensor_copy(kp[:, :, P - 1:2 * P - 1], bank[7][:, 0:2 * P].rearrange("p (a t) -> p a t", a=2)))
            tt(kp[:, :, P - 1:P], kp[:, :, P - 1:P], chp[:, 2:4].unsqueeze(2), ALU.add).then_inc(s_kp, 1)
            norm_dve(dve, NMIX, xa, 1, None)
            dve.wait_ge(s_kd, 16)
            for n in range(2 * (GR // 4)):
                q, c = divmod(n, 2)
                dve.wait_ge(s_u, n + 1)
                if n > 1:
                    dve.wait_ge(s_ur, n - 1)
                t4 = tmp[:, n % 2, :].rearrange("p (g h t) -> p g h t", g=4, h=GC)
                tt(t4, bank[4 + n % 2][:, :].rearrange("p (g h t) -> p g h t", g=4, h=GC),
                   bc(blockd.unsqueeze(1).unsqueeze(3), (P, 4, GC, TILES)), ALU.mult).then_inc(s_um, 1)
                dve.wait_ge(s_um, n + 1)
                dve.tensor_reduce(ust[:, c, 4 * q:4 * q + 4, :], t4.rearrange("p g h t -> p g t h"), AX.X,
                                  ALU.add).then_inc(s_ur, 1)
            dve.wait_ge(s_ur, 2 * (GR // 4))
            u5 = ust.rearrange("p c g (b j) -> p c g b j", b=B)
            wr = bc(w_t[:, 0, :, NTV - 1].unsqueeze(1).unsqueeze(3), (P, 2, GR, B))
            wi = bc(w_t[:, 1, :, NTV - 1].unsqueeze(2), (P, GR, B))
            pa = tmp[:, 0, 0:2 * GR * B].rearrange("p (c g b) -> p c g b", c=2, g=GR)
            pb = tmp[:, 1, 0:2 * GR * B].rearrange("p (c g b) -> p c g b", c=2, g=GR)
            for j in range(1, SEQ_TILES):
                tt(pa, u5[:, :, :, :, j - 1], wr, ALU.mult)
                tt(pb[:, 0], u5[:, 1, :, :, j - 1], wi, ALU.mult)
                link(tt(pb[:, 1], u5[:, 0, :, :, j - 1], wi, ALU.mult))
                link(tt(u5[:, :, :, :, j], u5[:, :, :, :, j], pa, ALU.add))
                tt(u5[:, 0, :, :, j], u5[:, 0, :, :, j], pb[:, 0], ALU.subtract)
                link(tt(u5[:, 1, :, :, j], u5[:, 1, :, :, j], pb[:, 1], ALU.add))
            s6 = sh.rearrange("p c g (b j) -> p (c g) b j", b=B)
            dve.memset(s6[:, :, :, 0:1], 0.0)
            link(dve.tensor_copy(s6[:, :, :, 1:SEQ_TILES],
                                 ust.rearrange("p c g (b j) -> p (c g) b j", b=B)[:, :, :, 0:SEQ_TILES - 1]))
            for q in range(GR // 4):
                if q > 1:
                    dve.wait_ge(s_yg, 4 * (q - 1))
                for c in range(2):
                    tt(rbd[:, q % 2, c], bc(sh[:, c, 4 * q:4 * q + 4, :].unsqueeze(2), (P, 4, GC, TILES)),
                       bc(blockd.unsqueeze(1).unsqueeze(3), (P, 4, GC, TILES)), ALU.mult).then_inc(s_r, 1)

            def residual(c):
                dve.wait_ge(s_op, c + 1)
                xm = x_main[:, c * CHUNK:(c + 1) * CHUNK]
                tt(xm, xm, bank[2 + c % 2][:, :], ALU.add).then_inc(s_mix, 1)
            for n in range(2 * CHUNKS):
                c, blk = divmod(n, 2)
                dve.wait_ge(s_yt, n + 1)
                if blk == 0 and c > 1:
                    dve.wait_ge(s_op, c - 1)
                tt(yz[:, 2 * (c % 2) + blk, :], bank[n % 2][:, :], zs[blk][:, c * CHUNK:(c + 1) * CHUNK],
                   ALU.mult).then_inc(s_yz, 1)
                if blk and c:
                    residual(c - 1)
            residual(CHUNKS - 1)

        def mixer_pool(pool):
            norm_pool(pool, NMIX)

        def mixer_sync(sp):
            sp.wait_ge(s_mac, 1)
            for dst, name in ((prm, "prm"), (tv, "tv"), (blockd, "blockd"), (sel, "sel"), (ipw, "ipw"), (opw, "opw"),
                              (cw, "cw"), (chp, "chp")):
                sp.dma_start(dst, ins[name]).then_inc(s_mc, 16)
            sp.wait_ge(s_kp, 1)
            sp.dma_start(kpad.rearrange("(a p) t -> p a t", p=P), kp).then_inc(s_kd, 16)
            sp.wait_ge(s_kd, 16)
            for g in range(GR):
                if g >= TRING:
                    sp.wait_ge(s_yg, g - TRING + 1)
                src = bass.AP(tensor=kpad.tensor, offset=kpad.offset + g * GC * 2 * P, ap=[[1, P], [2 * P, GC], [1, P]])
                sp.dma_start(toep[:, g % TRING, :, :], src).then_inc(s_toep[g % TRING], 16)

        block = ctx.enter_context(nc.Block())

        @block.sync
        def _(sp):
            sp.dma_start(consts[:, :], ins["consts"]).then_inc(s_const, 16)
            sp.dma_start(x_main[:, :], ins["x"]).then_inc(s_x, 16)
            sp.dma_start(raw_m, ins["masks"]).then_inc(s_const, 16)
            def rotary_loads():
                sp.dma_start(raw_c, ins["rot_c"]).then_inc(s_raw, 16)
                sp.dma_start(raw_s, ins["rot_s"]).then_inc(s_raw, 16)
                sp.dma_start(qks, ins["qks"]).then_inc(s_raw, 16)
            rotary_loads()
            for lx in range(2 * DEPTH):
                l = lx % DEPTH
                if lx:
                    sp.wait_ge(s_wo, lx * TILES)
                sp.dma_start(wqkv[:, :], ins["wqkv"][l]).then_inc(s_wa, 16)
                sp.dma_start(wo[:, :, :], ins["wo"][l].rearrange("(j p) n -> p j n", p=P)).then_inc(s_wa, 16)
                if lx:
                    sp.wait_ge(s_xa, xa_count(lx, (lx - 1) // DEPTH))
                sp.dma_start(w1[:, :], ins["w1"][l]).then_inc(s_wf, 16)
                for f, (at, w) in enumerate(HB):
                    sp.dma_start(w2[0:w, f, :], ins["w2"][l][at:at + w, :]).then_inc(s_wf, 16)
                sp.dma_start(par[:, :], ins["par"][l]).then_inc(s_wf, 16)
                if lx == DEPTH:
                    mixer_sync(sp)
                    sp.wait_ge(s_mix, CHUNKS)
                    rotary_loads()
            sp.wait_ge(s_mac, 2)
            sp.dma_start(out, x_main[:, :]).then_inc(s_out, 16)
            sp.wait_ge(s_out, 16)

        @block.gpsimd
        def _(pool):
            pool.memset(exp_half[:, :], -0.5).then_inc(s_init, 1)
            pool.memset(xa[:, 0:1], 0.0).then_inc(s_init, 1)
            pool.memset(xb[:, 0:1], 0.0).then_inc(s_init, 1)
            pool.memset(kT[:, :, :, :], 0.0).then_inc(s_init, 1)
            for i in range(2):
                pool.memset(v[i][:, :, :], 1.0).then_inc(s_init, 1)
                pool.memset(vmix[i][:, :, :], 0.0).then_inc(s_init, 1)
            pool.wait_ge(s_init, INITS)
            pool.wait_ge(s_const, 32)
            macaron_pool(pool, 0)
            mixer_pool(pool)
            macaron_pool(pool, 1)

        @block.scalar
        def _(act):
            act.wait_ge(s_init, INITS)
            macaron_act(act, 0)
            mixer_act(act)
            macaron_act(act, 1)

        @block.vector
        def _(dve):
            dve.wait_ge(s_const, 32)
            masks_dve(dve)
            dve.wait_ge(s_init, INITS)
            macaron_dve(dve, 0)
            mixer_dve(dve)
            macaron_dve(dve, 1)

        @block.tensor
        def _(pe):
            pe.wait_ge(s_const, 32)
            pe.wait_ge(s_mask, 1)
            macaron_pe(pe, 0)
            mixer_pe(pe)
            macaron_pe(pe, 1)


def shape_constants():
    consts = np.zeros((P, C_W), np.float32)
    consts[:, C_ID:C_ID + P] = np.eye(P)
    consts[:, C_CEN:C_CEN + P] = np.eye(P) - 1.0 / P
    consts[:, C_ONE:C_ONE + P] = 1.0
    flag = np.ones(TILES)
    flag[::SEQ_TILES] = 0
    consts[:, C_FLAG:] = flag
    i = np.arange(WIN)[:, None]
    j = np.arange(WIN)[None, :]
    own, older = i >= j, j >= i
    keep = np.zeros((2, P, P), bool)
    keep[:, 0:WIN, 0:WIN], keep[:, 0:WIN, WIN:] = own, older
    keep[:, WIN:, 0:WIN], keep[:, WIN:, WIN:] = older, own
    keep[0, 0:WIN, WIN:] = False
    masks = np.where(keep, 0.0, MASKED).transpose(1, 0, 2).astype(np.float32)
    half = np.arange(0, DH, 2, dtype=np.float32)
    inv = np.float32(1.0) / np.power(np.float32(10000.0), half / np.float32(DH)).astype(np.float32)
    t = np.arange(N, dtype=np.float32)
    fr = (t[:, None] * inv[None, :]).astype(np.float32).astype(np.float64)
    base = (half.astype(np.float64) + 0.4 * DH) / (1.4 * DH)
    sc = base[None, :] ** ((t - N // 2) / float(WIN // 2))[:, None].astype(np.float64)
    cos, sin = np.cos(fr), np.sin(fr)
    qk_scale = 8.0
    c = np.stack([np.tile(cos * sc, 2) * qk_scale, np.tile(cos / sc, 2)], 1)
    s = np.stack([np.concatenate([-sin * sc, sin * sc], 1) * qk_scale, np.concatenate([-sin / sc, sin / sc], 1)], 1)
    lay = lambda a: np.ascontiguousarray(a.astype(np.float32).reshape(SEQ_TILES, P, 2, DH).transpose(1, 0, 2, 3))
    blockd = (np.arange(P)[:, None] // NS == np.arange(GC)).astype(np.float32)
    sel = np.zeros((P, SEL), np.float32)
    sel[:, P - GC:P] = blockd
    tvs = np.ascontiguousarray(np.broadcast_to(np.array(TV, np.float32), (P, NTV)))
    return dict(blockd=blockd, sel=sel, tv=tvs, consts=consts, masks=np.ascontiguousarray(masks), rot_c=lay(c), rot_s=lay(s))


def kernel(**inputs):
    import concourse.bacc as bacc
    from concourse.bass_utils import run_bass_kernel_spmd

    a = {k.replace("L0_", ""): np.asarray(v) for k, v in inputs.items()}
    f32 = np.float32
    arrays = shape_constants()
    arrays["x"] = np.ascontiguousarray(a["attn_hidden_states"].reshape(T, D).T)
    arrays["wqkv"] = a["ffn_wqkv"]
    arrays["wo"] = a["ffn_wo"]
    arrays["w1"] = a["ffn_w1"]
    arrays["w2"] = a["ffn_w2"]
    qk = np.stack([a["ffn_q_scale"], a["ffn_k_scale"]], 1)
    arrays["qks"] = np.ascontiguousarray(np.broadcast_to(qk, (P, DEPTH, 2, DH)))
    pp = np.zeros((DEPTH, P, NPAR), f32)
    for l in range(DEPTH):
        pp[l, :, 0], pp[l, :, 1], pp[l, :, 2] = a["ffn_ln_g"][l], a["ffn_ln_b"][l], a["ffn_b2"][l]
        for g in range(2):
            for f, (at, w) in enumerate(HB):
                pp[l, :w, 4 + 3 * g + f] = a["ffn_b1"][l, g * HID + at:g * HID + at + w]
    arrays["par"] = pp

    rows = lambda z: z.reshape(GR, P).T
    arrays["prm"] = np.stack([rows(np.repeat(a["attn_log_dt"][:, None], NS, 1))]
                             + [rows(a["attn_" + k]) for k in ("A_re", "A_im", "C_re", "C_im")], 1)
    arrays["ipw"] = a["attn_in_proj_w"].T
    arrays["opw"] = a["attn_out_proj_w"].T.reshape(2, P, D).transpose(1, 0, 2)
    arrays["cw"] = np.broadcast_to(a["attn_conv_w"].T, (P, 4, DIN))
    arrays["chp"] = np.concatenate([a["attn_conv_b"].reshape(2, P).T, a["attn_D_skip"].reshape(2, P).T], 1)

    nc = bacc.Bacc("TRN2", target_bir_lowering=False, num_devices=1)
    aps, feeds = {}, {}
    for name, arr in arrays.items():
        arr = np.ascontiguousarray(arr)
        feeds["in_" + name] = arr
        aps[name] = nc.dram_tensor("in_" + name, arr.shape, mybir.dt.from_np(arr.dtype), kind="ExternalInput").ap()
    out = nc.dram_tensor("out_x", (P, T), F32, kind="ExternalOutput").ap()
    kpad = nc.dram_tensor("kpad", (DIN, 2 * P), F32, kind="Internal").ap()
    build(nc, aps, kpad, out)
    got = run_bass_kernel_spmd(nc, [feeds], core_ids=[0]).results[0]["out_x"]
    return np.ascontiguousarray(got.T).reshape(B, N, D)
```

```python
from contextlib import ExitStack

import numpy as np

import concourse.bass as bass
from concourse import mybir

F32 = mybir.dt.float32
BF16 = mybir.dt.bfloat16
ALU = mybir.AluOpType
ACT = mybir.ActivationFunctionType
AX = mybir.AxisListType

P = 128
B, N = 2, 1024
T = B * N
TILES = T // P
SEQ_TILES = N // P
CHUNK = 512
CHUNKS = T // CHUNK
D = 128
H, DH = 8, 64
INNER = H * DH
WIN = 64
DEPTH = 2
HID = D * 4 * 2 // 3
HB = [(f, min(P, HID - f)) for f in range(0, HID, P)]
EPS = 1e-5
MASKED = -1e38

C_ID, C_CEN, C_ONE, C_FLAG, C_W = 0, P, 2 * P, 3 * P, 3 * P + TILES
NPAR = 10

INITS = 8
DIN, NS = 2 * D, 16
GC = P // NS
GR = DIN // GC
TV = list(range(16)) + [16 * a for a in range(8)] + [16 * a + 1 for a in range(8)] + [P]
NTV = len(TV)
SEL = 2 * P - GC
TRING = 2
ARENA = 37920
MIX_LOADS = 8
PI_A = 6.28125
PI_B = float(np.float32(np.round((2 * np.pi - PI_A) * 2 ** 20) / 2 ** 20))
PI_C = float(np.float32(2 * np.pi - PI_A - PI_B))
PI_IN = 3.1415925
MAGIC = 1.5 * 2 ** 23
T_BANKS = 2


def bc(ap, shape):
    return ap.to_broadcast(list(shape))


def build(nc, ins, kpad, out):
    with ExitStack() as ctx:
        def sb(name, shape, dt=F32):
            return ctx.enter_context(nc.sbuf_tensor(name, shape, dt))

        def sem(name):
            return ctx.enter_context(nc.semaphore(name))

        consts = sb("consts", [P, C_W])
        ident = consts[:, C_ID:C_ID + P]
        center = consts[:, C_CEN:C_CEN + P]
        ones = consts[:, C_ONE:C_ONE + P]
        flag = consts[:, C_FLAG:C_FLAG + TILES]
        ident_bf = sb("ident_bf", [P, P], BF16)
        masks = sb("masks", [P, TILES, P], BF16)
        par = sb("par", [P, NPAR])
        x_main = sb("x_main", [P, T])
        xa = sb("xa", [P, 1 + T])
        xb = sb("xb", [P, 1 + T])
        wqkv = sb("wqkv", [P, 3 * INNER])
        wo = sb("wo", [P, INNER // P, D])
        w1 = sb("w1", [P, 2 * HID])
        w2 = sb("w2", [P, len(HB), D])
        exp_half = sb("exp_half", [P, TILES])
        kT = sb("kT", [P, 4, 4, WIN])
        v = [sb(f"v{i}", [P, H, DH + 1]) for i in range(2)]
        vmix = [sb(f"vmix{i}", [P, H, DH + 1]) for i in range(2)]
        ssum = sb("ssum", [P, 2 * H])
        smax = sb("smax", [P, 2 * H])
        rn = sb("rn", [P, 2 * H])
        mx = sb("mx", [P, H])
        rsum = sb("rsum", [P, H])
        vare = sb("vare", [P, TILES])
        rstd = sb("rstd", [P, TILES])
        arena = sb("arena", [P, ARENA])

        def carver(at):
            def take(*shape):
                nonlocal at
                n = int(np.prod(shape))
                ap = arena[:, at:at + n]
                at += n
                assert at <= ARENA, at
                names = "abcde"[:len(shape)]
                if len(shape) > 1:
                    ap = ap.rearrange(f"p ({' '.join(names)}) -> p {' '.join(names)}",
                                      **{k: v_ for k, v_ in zip(names, shape)})
                return ap
            return take
        common = 2 * CHUNK + CHUNK
        take = carver(0)
        sqf = take(2, CHUNK)
        diag = take(4, P)
        rot_a = take(DEPTH, TILES, 2, DH)
        rot_b = take(DEPTH, TILES, 2, DH)
        raw_c = take(SEQ_TILES, 2, DH)
        raw_s = take(SEQ_TILES, 2, DH)
        qks = take(DEPTH, 2, DH)
        raw_m = take(2, P)
        hs = [take(P) for _ in range(2)]
        sq = [take(2 * INNER) for _ in range(2)]
        t1 = [take(2 * INNER) for _ in range(2)]
        t2 = [take(2 * INNER) for _ in range(2)]
        qkn = take(2 * INNER)
        qT = take(4, P)
        prob = take(2, 4, P)
        pT = take(2, 4, P)
        on = take(H, DH)
        oT = take(4, P)
        hsh = take(2, CHUNK)
        y = take(T)
        gel = take(2, CHUNK)
        hid = take(2, CHUNK)
        take = carver(common)
        v_t = take(2, GR, P)
        g_t = take(2, GR, P)
        xs = take(2, TILES, P)
        ysb = xs.rearrange("p a b c -> p (a b c)").rearrange("p (h t) -> p h t", t=TILES)
        x_tok = take(DIN, TILES)
        zs1 = take(T)
        zs = [xb[:, 1:1 + T], zs1]
        toep = take(TRING, GC, P)
        w_t = take(2, GR, NTV)
        ust = take(2, GR, TILES)
        sh = take(2, GR, TILES)
        rbd = take(2, 2, 4, GC, TILES)
        tmp = sqf
        yz = rbd.rearrange("p a b c d e -> p (a b c d e)").rearrange("p (a b) -> p a b", a=4)
        ipw = take(2 * DIN)
        opw = take(2, D)
        sel = take(SEL)
        tv = take(NTV)
        blockd = take(GC)
        early = rbd.rearrange("p a b c d e -> p (a b c d e)")
        cw, ipk = (early[:, i * 4 * DIN:(i + 1) * 4 * DIN].rearrange("p (k h) -> p k h", k=4) for i in range(2))
        prm = take(5, GR)
        chp = take(4)
        early = sh.rearrange("p a b c -> p (a b c)")
        sm = early[:, 0:12 * GR].rearrange("p (i g) -> p i g", g=GR)
        ca = early[:, 16 * GR:32 * GR].rearrange("p (c g a) -> p c g a", c=2, g=GR)
        kp = ust.rearrange("p a b c -> p (a b c)")[:, 0:4 * P].rearrange("p (a t) -> p a t", a=2)
        pre = [x_tok.rearrange("p a b -> p (a b)"), xs.rearrange("p a b c -> p (a b c)")]

        bank = [ctx.enter_context(nc.psum_tensor(f"bank{i}", [P, CHUNK], F32)) for i in range(8)]
        QK = [bank[0], bank[1]]
        SC = [bank[2], bank[3]]
        TB = [bank[4], bank[5]]
        OB = [bank[6], bank[7]]
        WO = bank[7][:, 384:512]

        s_const = sem("s_const")
        s_mask = sem("s_mask")
        s_raw = sem("s_raw")
        s_x = sem("s_x")
        s_wa = sem("s_wa")
        s_wf = sem("s_wf")
        s_rot = sem("s_rot")
        s_init = sem("s_init")
        s_hs = sem("s_hs")
        s_qk = sem("s_qk")
        s_sq = sem("s_sq")
        s_t12 = sem("s_t12")
        s_ss = sem("s_ss")
        s_ssm = sem("s_ssm")
        s_rn = sem("s_rn")
        s_add = sem("s_add")
        s_qkn = sem("s_qkn")
        s_T = sem("s_T")
        s_Tf = sem("s_Tf")
        s_sc = sem("s_sc")
        s_mx = sem("s_mx")
        s_exp = sem("s_exp")
        s_pv = sem("s_pv")
        s_vm = sem("s_vm")
        s_rs = sem("s_rs")
        s_on = sem("s_on")
        s_wo = sem("s_wo")
        s_res = sem("s_res")
        s_hsh = sem("s_hsh")
        s_cen = sem("s_cen")
        s_csb = sem("s_csb")
        s_sqf = sem("s_sqf")
        s_var = sem("s_var")
        s_vare = sem("s_vare")
        s_rstd = sem("s_rstd")
        s_diag = sem("s_diag")
        s_rb = sem("s_rb")
        s_yn = sem("s_yn")
        s_y = sem("s_y")
        s_ag = sem("s_ag")
        s_gel = sem("s_gel")
        s_hid = sem("s_hid")
        s_down = sem("s_down")
        s_xa = sem("s_xa")
        s_mac = sem("s_mac")
        s_mc = sem("s_mc")
        s_dt = sem("s_dt")
        s_tr = sem("s_tr")
        s_mag = sem("s_mag")
        s_ph = sem("s_ph")
        s_trig = sem("s_trig")
        s_link = sem("s_link")
        s_g = sem("s_g")
        s_row = sem("s_row")
        s_vt = sem("s_vt")
        s_ve = sem("s_ve")
        s_kk = sem("s_kk")
        s_kp = sem("s_kp")
        s_kd = sem("s_kd")
        s_toep = [sem(f"s_toep{i}") for i in range(TRING)]
        s_ipk = sem("s_ipk")
        s_in = sem("s_in")
        s_silu = sem("s_silu")
        s_xt = sem("s_xt")
        s_xe = sem("s_xe")
        s_u = sem("s_u")
        s_um = sem("s_um")
        s_ur = sem("s_ur")
        s_r = sem("s_r")
        s_yg = sem("s_yg")
        s_yb = sem("s_yb")
        s_ye = sem("s_ye")
        s_yt = sem("s_yt")
        s_yz = sem("s_yz")
        s_op = sem("s_op")
        s_mix = sem("s_mix")
        s_out = sem("s_out")

        K_SLOT = {(0, 0): 0, (1, 0): 1, (1, 1): 2, (0, 1): 3}

        def xa_count(layers, m):
            return (layers + 2 * m + 1) * CHUNKS

        def t_before(s):
            if isinstance(s, int):
                return sum(len(t_names(r)) for r in range(s))
            return t_before(4) + 6 * (s - 4)

        def t_base(lx):
            return lx * (6 * TILES)

        def steps(eng, step):
            for s in range(4):
                step(s, s % 2)
            with eng.Fori(0, (TILES - 4) // 2) as i:
                step(2 * i + 4, 0)
                step(2 * i + 5, 1)
            for s in range(TILES, TILES + 4):
                step(s, s % 2)

        def past(s, lag):
            return not isinstance(s, int) or s >= lag

        def live(s, lag):
            return not isinstance(s, int) or 0 <= s - lag < TILES

        def t_names(s):
            lags = (("oT", 4), ("qT", 2), ("kT", 2), ("pT0", 3), ("pT1", 3), ("v", 1))
            return [n for n, lag in lags if live(s, lag)]

        def t_uses(s):
            even = t_before(s if isinstance(s, int) else 4) % 2
            return {n: (t_before(s) + j, (even + j) % 2) for j, n in enumerate(t_names(s))}

        def attention_pe(pe, lx):
            pe.wait_ge(s_wa, (lx + 1) * 32)
            base, tb = lx * TILES, t_base(lx)

            def done(s, lag):
                return base + s - lag + 1

            def take(uses, name):
                n, b = uses[name]
                if not isinstance(n, int) or n >= T_BANKS:
                    pe.wait_ge(s_Tf, tb + n - 1)
                return TB[b]

            def step(s, p):
                uses = t_uses(s)
                if live(s, 0):
                    pe.wait_ge(s_hs, done(s, 0))
                    if past(s, 1):
                        pe.wait_ge(s_sq, done(s, 1))
                    for j in range(2):
                        pe.matmul(QK[j][:, :], hs[p], wqkv[:, j * INNER:(j + 1) * INNER],
                                  start=True, stop=True).then_inc(s_qk, 1)
                if live(s, 4):
                    pe.wait_ge(s_on, done(s, 4))
                    bk = take(uses, "oT")
                    for j in range(4):
                        last = pe.transpose(bk[:, j * P:(j + 1) * P],
                                            on[:, 2 * j:2 * j + 2, :].rearrange("p a b -> p (a b)"), ident)
                    last.then_inc(s_T, 1)
                if live(s, 2):
                    pe.wait_ge(s_qkn, done(s, 2))
                    bk = take(uses, "qT")
                    for j in range(4):
                        last = pe.transpose(bk[:, j * P:(j + 1) * P], qkn[:, j * P:(j + 1) * P], ident)
                    last.then_inc(s_T, 1)
                    bk = take(uses, "kT")
                    for j in range(4):
                        last = pe.transpose(bk[:, j * P:(j + 1) * P], qkn[:, INNER + j * P:INNER + (j + 1) * P], ident)
                    last.then_inc(s_T, 1)

                def prob_t(r):
                    bk = take(uses, f"pT{r}")
                    for j in range(4):
                        last = pe.transpose(bk[:, j * P:(j + 1) * P], prob[:, r, j, :], ident)
                    last.then_inc(s_T, 1)
                if live(s, 3):
                    pe.wait_ge(s_exp, done(s, 3))
                    prob_t(0)
                if live(s, 4):
                    pe.wait_ge(s_Tf, tb + uses["oT"][0] + 1)
                    for j in range(4):
                        last = pe.matmul(WO, wo[:, j, :], oT[:, j, :], start=(j == 0), stop=(j == 3),
                                         skip_group_check=True)
                    last.then_inc(s_wo, 1)
                if live(s, 3):
                    prob_t(1)
                if live(s, 2):
                    if past(s, 3):
                        pe.wait_ge(s_exp, done(s, 3))
                    pe.wait_ge(s_Tf, tb + uses["kT"][0] + 1)
                    for r in range(2):
                        pe.matmul(SC[r][:, :], ident_bf[:, :],
                                  bc(masks[:, bass.ds(s - 2, 1), :], (P, 4, P)),
                                  start=True, stop=False, skip_group_check=True)
                    for hb in range(4):
                        for w in range(2):
                            ka = K_SLOT[(p, 0)]
                            kb = K_SLOT[(p, 1)] if w else K_SLOT[(1 - p, 1)]
                            for r in range(2):
                                last = pe.matmul(
                                    SC[r][WIN * w:WIN * (w + 1), hb * P:(hb + 1) * P],
                                    qT[DH * r:DH * (r + 1), hb, WIN * w:WIN * (w + 1)],
                                    kT[DH * r:DH * (r + 1), hb, ka:kb + 1:kb - ka, :],
                                    start=False, stop=True, skip_group_check=True)
                    last.then_inc(s_sc, 1)
                if live(s, 1):
                    bk = take(uses, "v")
                    pe.matmul(bk[:, :], hs[1 - p], wqkv[:, 2 * INNER:3 * INNER],
                              start=True, stop=True).then_inc(s_T, 1)
                if live(s, 3):
                    pe.wait_ge(s_Tf, tb + uses["pT1"][0] + 1)
                    pe.wait_ge(s_vm, done(s, 3))
                    if past(s, 4):
                        pe.wait_ge(s_on, done(s, 4))
                        pe.wait_ge(s_res, done(s, 4))
                    q = 1 - p
                    for h in range(H):
                        for w, vv in ((0, vmix[q]), (1, v[q])):
                            last = pe.matmul(OB[h // 4][WIN * w:WIN * (w + 1), (h % 4) * 65:(h % 4 + 1) * 65],
                                             pT[:, h % 2, h // 2, WIN * w:WIN * (w + 1)], vv[:, h, :],
                                             start=True, stop=True, skip_group_check=True)
                    last.then_inc(s_pv, 1)
            steps(pe, step)

        def attention_act(act, lx):
            base, tb = lx * TILES, t_base(lx)

            def done(s, lag):
                return base + s - lag + 1

            def empty(uses, name, dst, pattern, **sizes):
                n, b = uses[name]
                act.wait_ge(s_T, tb + n + 1)
                act.activation(dst, TB[b][:, :].rearrange(pattern, **sizes), ACT.Copy).then_inc(s_Tf, 1)

            def step(s, p):
                uses = t_uses(s)
                if live(s, 4):
                    empty(uses, "oT", oT, "p (j c) -> p j c", j=4)
                if live(s, 2):
                    empty(uses, "qT", qT, "p (j c) -> p j c", j=4)
                    a, c = K_SLOT[(p, 0)], K_SLOT[(p, 1)]
                    empty(uses, "kT", kT[:, :, a:c + 1:c - a, :], "p (j h c) -> p j h c", j=4, h=2)
                if live(s, 3):
                    for r in range(2):
                        empty(uses, f"pT{r}", pT[:, r, :, :], "p (j c) -> p j c", j=4)
                if live(s, 0):
                    if past(s, 2):
                        act.wait_ge(s_ss, done(s, 2))
                    for j in range(2):
                        act.wait_ge(s_t12, 2 * (base + s) + j + 1)
                        last = act.activation(sq[p][:, j * INNER:(j + 1) * INNER], QK[j][:, :], ACT.Square)
                    last.then_inc(s_sq, 1)
                if live(s, 2):
                    act.wait_ge(s_mx, done(s, 2))
                    for r in range(2):
                        for j in range(4):
                            last = act.activation(prob[:, r, j, :], SC[r][:, j * P:(j + 1) * P], ACT.Exp,
                                                  bias=mx[:, 4 * r + j:4 * r + j + 1])
                    last.then_inc(s_exp, 1)
                if live(s, 1):
                    if past(s, 3):
                        act.wait_ge(s_pv, done(s, 3))
                    if past(s, 2):
                        act.wait_ge(s_vm, done(s, 2))
                    empty(uses, "v", v[1 - p][:, :, 0:DH], "p (h c) -> p h c", h=H)
            steps(act, step)

        def attention_dve(dve, lx, l):
            base, tb = lx * TILES, t_base(lx)

            def done(s, lag):
                return base + s - lag + 1

            def stage(s, p):
                if past(s, 2):
                    dve.wait_ge(s_T, tb + t_before(s))
                dve.tensor_tensor(hs[p][64:128, 0:1], xa[64:128, bass.ds(s * P, 1)],
                                  flag[64:128, bass.ds(s, 1)], ALU.mult)
                dve.tensor_copy(hs[p][0:64, :], xa[0:64, bass.ds(s * P + 1, P)])
                dve.tensor_copy(hs[p][64:128, 1:P], xa[64:128, bass.ds(s * P + 1, P - 1)]).then_inc(s_hs, 1)

            def step(s, p):
                if live(s, 0):
                    stage(s, p)
                if live(s, 4):
                    dve.wait_ge(s_pv, done(s, 4))
                    for g in range(2):
                        ob = OB[g][:, 0:260].rearrange("p (h d) -> p h d", h=4)
                        last = dve.reciprocal(rsum[:, 4 * g:4 * g + 4].unsqueeze(2), ob[:, :, 64:65])
                    last.then_inc(s_rs, 1)
                    dve.wait_ge(s_rs, done(s, 4))
                    for g in range(2):
                        ob = OB[g][:, 0:260].rearrange("p (h d) -> p h d", h=4)
                        last = dve.tensor_tensor(on[:, 4 * g:4 * g + 4, :], ob[:, :, 0:64],
                                                 bc(rsum[:, 4 * g:4 * g + 4].unsqueeze(2), (P, 4, DH)), ALU.mult)
                    last.then_inc(s_on, 1)
                if live(s, 2):
                    dve.wait_ge(s_Tf, tb + t_before(s))
                    dve.tensor_copy(vmix[p][0:64, :, :], v[p][0:64, :, :])
                    dve.tensor_copy(vmix[p][64:128, :, :], v[1 - p][64:128, :, :]).then_inc(s_vm, 1)
                if live(s, 1):
                    dve.wait_ge(s_sq, done(s, 1))
                    dve.tensor_reduce(ssum[:, :], sq[1 - p].rearrange("p (h d) -> p h d", d=DH), AX.X,
                                      ALU.add).then_inc(s_ss, 1)
                if live(s, 0):
                    if past(s, 2):
                        dve.wait_ge(s_qkn, done(s, 2))
                    row = l * TILES + s
                    ta = rot_a.rearrange("p l t a d -> p (l t) a d")[:, bass.ds(row, 1), :, :]
                    tbb = rot_b.rearrange("p l t a d -> p (l t) a d")[:, bass.ds(row, 1), :, :]
                    for j in range(2):
                        dve.wait_ge(s_qk, 2 * (base + s) + j + 1)
                        src = QK[j][:, :].rearrange("p (h d) -> p h d", h=H)
                        o1 = t1[p][:, j * INNER:(j + 1) * INNER].rearrange("p (h d) -> p h d", h=H)
                        o2 = t2[p][:, j * INNER:(j + 1) * INNER].rearrange("p (h d) -> p h d", h=H)
                        dve.tensor_tensor(o1, src, bc(ta[:, :, j, :], (P, H, DH)), ALU.mult)
                        dve.tensor_tensor(o2[:, :, 0:32], src[:, :, 32:64], bc(tbb[:, :, j, 0:32], (P, H, 32)),
                                          ALU.mult)
                        dve.tensor_tensor(o2[:, :, 32:64], src[:, :, 0:32], bc(tbb[:, :, j, 32:64], (P, H, 32)),
                                          ALU.mult).then_inc(s_t12, 1)
                        if j == 0 and live(s, 1):
                            clip(s)
                elif live(s, 1):
                    clip(s)
                if live(s, 4):
                    dve.wait_ge(s_wo, done(s, 4))
                    t = s - 4
                    dve.tensor_tensor(xb[:, bass.ds(t * P + 1, P)], xa[:, bass.ds(t * P + 1, P)], WO,
                                      ALU.add).then_inc(s_res, 1)
                if live(s, 2):
                    dve.wait_ge(s_sc, done(s, 2))
                    if past(s, 3):
                        dve.wait_ge(s_exp, done(s, 3))
                    for r in range(2):
                        last = dve.tensor_reduce(mx[:, 4 * r:4 * r + 4], SC[r][:, :].rearrange("p (h d) -> p h d", d=P),
                                                 AX.X, ALU.max, negate=True)
                    last.then_inc(s_mx, 1)

            def clip(s):
                dve.wait_ge(s_ss, done(s, 1))
                if past(s, 2):
                    dve.wait_ge(s_rn, done(s, 2))
                dve.tensor_scalar(smax[:, :], ssum[:, :], 1e-24, None, ALU.max).then_inc(s_ssm, 1)
            steps(dve, step)

        def attention_pool(pool, lx):
            base, tb = lx * TILES, t_base(lx)

            def done(s, lag):
                return base + s - lag + 1

            def step(s, p):
                if live(s, 1):
                    if past(s, 2):
                        pool.wait_ge(s_qkn, done(s, 2))
                    pool.wait_ge(s_ssm, done(s, 1))
                    pool.tensor_tensor(rn[:, :], smax[:, :], exp_half[:, :], ALU.pow).then_inc(s_rn, 1)
                    pool.wait_ge(s_rn, done(s, 1))
                    pool.wait_ge(s_add, done(s, 1))
                    if live(s, 2):
                        pool.wait_ge(s_T, tb + t_uses(s)["kT"][0] + 1)
                    pool.tensor_tensor(qkn.rearrange("p (h d) -> p h d", d=DH),
                                       t1[1 - p].rearrange("p (h d) -> p h d", d=DH),
                                       bc(rn[:, :].unsqueeze(2), (P, 2 * H, DH)), ALU.mult).then_inc(s_qkn, 1)
                if live(s, 0):
                    pool.wait_ge(s_t12, 2 * done(s, 0))
                    pool.tensor_tensor(t1[p], t1[p], t2[p], ALU.add).then_inc(s_add, 1)
            steps(pool, step)

        def shift_dve(dve, n, src, ready):
            for c in range(CHUNKS):
                if c > 1:
                    dve.wait_ge(s_cen, n * CHUNKS + c - 1)
                first = int(c % (N // CHUNK) == 0)
                at = c * CHUNK + 1
                dve.wait_ge(*ready(c))
                dve.tensor_copy(hsh[0:64, c % 2, :], src[0:64, at:at + CHUNK])
                if first:
                    dve.memset(hsh[64:128, c % 2, 0:1], 0.0)
                dve.tensor_copy(hsh[64:128, c % 2, first:CHUNK],
                                src[64:128, at - 1 + first:at - 1 + CHUNK]).then_inc(s_hsh, 1)

        def norm_pool(pool, n):
            pool.wait_ge(s_vare, n + 1)
            pool.tensor_tensor(rstd[:, :], vare[:, :], exp_half[:, 0:TILES], ALU.pow).then_inc(s_rstd, 1)

        def norm_pe(pe, n, src, shifted, ready, n_plain=0):
            def var(c):
                pe.wait_ge(s_sqf, n * CHUNKS + c + 1)
                for j in range(4):
                    last = pe.matmul(bank[4][:, 4 * c + j:4 * c + j + 1], sqf[:, c % 2, j * P:(j + 1) * P],
                                     ones[:, 0:1], start=True, stop=True, skip_group_check=True)
                last.then_inc(s_var, 1)
            for c in range(CHUNKS):
                k = n * CHUNKS + c
                if shifted:
                    pe.wait_ge(s_hsh, (n - n_plain) * CHUNKS + c + 1)
                    rhs = hsh[:, c % 2, :]
                else:
                    pe.wait_ge(*ready(c))
                    rhs = src[:, c * CHUNK:(c + 1) * CHUNK]
                pe.matmul(bank[c][:, :], center, rhs, start=True, stop=True).then_inc(s_cen, 1)
                if c:
                    var(c - 1)
            var(CHUNKS - 1)
            for c in range(CHUNKS):
                k = n * CHUNKS + c
                pe.wait_ge(s_diag, k + 1)
                if c > 1:
                    pe.wait_ge(s_yn, k - 1)
                pe.matmul(bank[5 + c % 2][:, :], ones, diag[:, :, :].rearrange("p a b -> p (a b)"),
                          start=True, stop=True).then_inc(s_rb, 1)

        def norm_act(act, n, dst, off):
            for c in range(CHUNKS):
                k = n * CHUNKS + c
                act.wait_ge(s_cen, k + 1)
                if c > 1:
                    act.wait_ge(s_var, k - 1)
                act.activation(sqf[:, c % 2, :], bank[c][:, :], ACT.Square).then_inc(s_sqf, 1)
                act.activation(dst[:, off + c * CHUNK:off + (c + 1) * CHUNK], bank[c][:, :], ACT.Copy).then_inc(s_csb, 1)

        def norm_dve(dve, n, dst, off, gb):
            dve.wait_ge(s_var, (n + 1) * CHUNKS)
            dve.tensor_scalar(vare[:, :], bank[4][:, 0:TILES], 1.0 / D, EPS, ALU.mult, ALU.add).then_inc(s_vare, 1)
            dve.wait_ge(s_rstd, n + 1)
            for c in range(CHUNKS):
                k = n * CHUNKS + c
                if c:
                    dve.wait_ge(s_rb, k)
                dve.tensor_tensor(diag[:, :, :], bc(ident.unsqueeze(1), (P, 4, P)),
                                  bc(rstd[:, 4 * c:4 * c + 4].unsqueeze(2), (P, 4, P)), ALU.mult).then_inc(s_diag, 1)
                dve.wait_ge(s_rb, k + 1)
                dve.wait_ge(s_csb, k + 1)
                d = dst[:, off + c * CHUNK:off + (c + 1) * CHUNK]
                dve.tensor_tensor(d, d, bank[5 + c % 2][:, :], ALU.mult).then_inc(s_yn, 1)
                if gb is not None:
                    dve.wait_ge(s_yn, k + 1)
                    dve.tensor_scalar(d, d, gb[0], gb[1], ALU.mult, ALU.add).then_inc(s_y, 1)
                else:
                    dve.wait_ge(s_yn, k + 1)
                    dve.sem_inc(s_y, 1)
                    dve.sem_inc(s_xa, 1)

        FB = len(HB)

        def up(c):
            return 2 * (c % 2)

        def ffn_pe(pe, lx, n, m):
            pe.wait_ge(s_wf, (lx + 1) * (16 * (FB + 2)))
            pe.wait_ge(s_csb, (n + 1) * CHUNKS)
            kb = lx * (CHUNKS * FB)

            def down(u):
                c, f = divmod(u, FB)
                _, w = HB[f]
                if f == 0:
                    if c > 1:
                        pe.wait_ge(s_xa, xa_count(lx, m) + c - 1)
                    else:
                        pe.wait_ge(s_yn, (n + 1) * CHUNKS)
                pe.wait_ge(s_hid, kb + u + 1)
                last = pe.matmul(bank[6 + c % 2][:, :], w2[0:w, f, :], hid[0:w, u % 2, :],
                                 start=(f == 0), stop=(f == FB - 1))
                last.then_inc(s_down, 1)
            for u in range(CHUNKS * FB):
                c, f = divmod(u, FB)
                at, w = HB[f]
                if f == 0:
                    pe.wait_ge(s_y, n * CHUNKS + c + 1)
                if u > 1:
                    pe.wait_ge(s_hid, kb + u - 1)
                for g in range(2):
                    last = pe.matmul(bank[2 * (u % 2) + g][0:w, :], w1[:, g * HID + at:g * HID + at + w],
                                     y[:, c * CHUNK:(c + 1) * CHUNK], start=True, stop=True)
                last.then_inc(s_ag, 1)
                if u:
                    down(u - 1)
            down(CHUNKS * FB - 1)

        def ffn_act(act, lx):
            kb = lx * (CHUNKS * FB)
            for u in range(CHUNKS * FB):
                c, f = divmod(u, FB)
                _, w = HB[f]
                act.wait_ge(s_ag, kb + u + 1)
                if u > 1:
                    act.wait_ge(s_hid, kb + u - 1)
                act.activation(gel[0:w, u % 2, :], bank[2 * (u % 2) + 1][0:w, :], ACT.Gelu,
                               bias=par[0:w, 7 + f:8 + f]).then_inc(s_gel, 1)

        def ffn_dve(dve, lx):
            kb = lx * (CHUNKS * FB)

            def finish(c):
                dve.wait_ge(s_down, kb + (c + 1) * FB)
                sl = slice(1 + c * CHUNK, 1 + (c + 1) * CHUNK)
                dve.scalar_tensor_tensor(out=xa[:, sl], in0=bank[6 + c % 2][:, :], scalar=par[:, 2:3],
                                         in1=xb[:, sl], op0=ALU.add, op1=ALU.add).then_inc(s_xa, 1)
            for u in range(CHUNKS * FB):
                c, f = divmod(u, FB)
                _, w = HB[f]
                dve.wait_ge(s_gel, kb + u + 1)
                if u > 1:
                    dve.wait_ge(s_down, kb + u - 1)
                dve.scalar_tensor_tensor(out=hid[0:w, u % 2, :], in0=bank[2 * (u % 2)][0:w, :],
                                         scalar=par[0:w, 4 + f:5 + f], in1=gel[0:w, u % 2, :],
                                         op0=ALU.add, op1=ALU.mult).then_inc(s_hid, 1)
                if f == 0 and c:
                    finish(c - 1)
            finish(CHUNKS - 1)

        def layer_norm_index(m, l):
            return 4 * m + 1 + l

        def outer(m):
            return 4 * m

        def main_ready(m):
            return lambda c: (s_x, 16) if m == 0 else (s_mix, CHUNKS)

        def masks_dve(dve):
            dve.tensor_copy(ident_bf[:, :], ident)
            for t in range(0, TILES, SEQ_TILES):
                dve.tensor_copy(masks[:, t, :], raw_m[:, 0, :])
                last = dve.tensor_copy(masks[:, t + 1:t + SEQ_TILES, :], bc(raw_m[:, 1:2, :], (P, SEQ_TILES - 1, P)))
            last.then_inc(s_mask, 1)

        def rotary_dve(dve, m):
            dve.wait_ge(s_raw, 48 * (m + 1))
            for l in range(DEPTH):
                for half in range(B):
                    t = slice(half * SEQ_TILES, (half + 1) * SEQ_TILES)
                    for tab, raw, to, fro in ((rot_a, raw_c, slice(0, DH), slice(0, DH)),
                                              (rot_b, raw_s, slice(0, 32), slice(32, 64)),
                                              (rot_b, raw_s, slice(32, 64), slice(0, 32))):
                        last = dve.tensor_tensor(tab[:, l, t, :, to], raw[:, :, :, to],
                                                 bc(qks[:, l, :, fro].unsqueeze(1), (P, SEQ_TILES, 2, to.stop - to.start)),
                                                 ALU.mult)
            last.then_inc(s_rot, 1)
            dve.wait_ge(s_rot, m + 1)

        def macaron_pe(pe, m):
            norm_pe(pe, outer(m), x_main, False, main_ready(m))
            with pe.Fori(0, DEPTH) as l:
                lx = l + DEPTH * m
                attention_pe(pe, lx)
                norm_pe(pe, layer_norm_index(m, l), xb, True, None, n_plain=1 + 2 * m - 0)
                ffn_pe(pe, lx, layer_norm_index(m, l), m)

        def macaron_act(act, m):
            norm_act(act, outer(m), xa, 1)
            with act.Fori(0, DEPTH) as l:
                lx = l + DEPTH * m
                attention_act(act, lx)
                norm_act(act, layer_norm_index(m, l), y, 0)
                ffn_act(act, lx)

        def macaron_dve(dve, m):
            rotary_dve(dve, m)
            norm_dve(dve, outer(m), xa, 1, None)
            with dve.Fori(0, DEPTH) as l:
                lx = l + DEPTH * m
                dve.wait_ge(s_y, layer_norm_index(m, l) * CHUNKS)
                attention_dve(dve, lx, l)
                shift_dve(dve, layer_norm_index(m, l), xb, lambda c: (s_res, lx * TILES + (c + 1) * (CHUNK // P)))
                dve.wait_ge(s_wf, (lx + 1) * (16 * (FB + 2)))
                norm_dve(dve, layer_norm_index(m, l), y, 0, (par[:, 0:1], par[:, 1:2]))
                ffn_dve(dve, lx)
            dve.wait_ge(s_xa, xa_count(DEPTH * (m + 1), m))
            dve.scalar_tensor_tensor(out=x_main[:, :], in0=xa[:, 1:1 + T], scalar=0.5, in1=x_main[:, :],
                                     op0=ALU.mult, op1=ALU.add).then_inc(s_mac, 1)

        def macaron_pool(pool, m):
            norm_pool(pool, outer(m))
            with pool.Fori(0, DEPTH) as l:
                lx = l + DEPTH * m
                pool.wait_ge(s_y, layer_norm_index(m, l) * CHUNKS)
                pool.wait_ge(s_xa, xa_count(lx, m))
                attention_pool(pool, lx)
                norm_pool(pool, layer_norm_index(m, l))

        NMIX = outer(0) + 3

        def mixer_pe(pe):
            pe.wait_ge(s_mc, 16 * MIX_LOADS)
            pe.wait_ge(s_g, 1)
            pe.wait_ge(s_mac, 1)
            for g in range(GR):
                q, half = g % (P // GC), g // (P // GC)
                last = pe.matmul(bank[7][:, half * P:(half + 1) * P], sel[:, P - GC - GC * q:2 * P - GC - GC * q],
                                 g_t[:, 0, g, :], start=(q == 0), stop=(q == P // GC - 1), skip_group_check=True)
            last.then_inc(s_kk, 1)
            for c in range(2):
                pe.wait_ge(s_row, c + 1)
                row = pre[1].rearrange("p (g t) -> p g t", g=GR)
                for k in range(GR // 4):
                    n = c * (GR // 4) + k
                    if n > 1:
                        pe.wait_ge(s_ve, n - 1)
                    for j in range(4):
                        last = pe.transpose(bank[n % 2][:, j * P:(j + 1) * P], row[:, 4 * k + j, :], ident)
                    last.then_inc(s_vt, 1)
            pe.wait_ge(s_ve, 2 * (GR // 4))
            norm_pe(pe, NMIX, x_main, False, lambda c: (s_mac, 1))
            pe.wait_ge(s_ipk, 1)
            u = 0
            for e in range(4):
                for c in range(CHUNKS):
                    if e == 0:
                        pe.wait_ge(s_y, NMIX * CHUNKS + CHUNKS)
                        pe.wait_ge(s_csb, (NMIX + 1) * CHUNKS)
                    if u > 1:
                        pe.wait_ge(s_silu, u - 1)
                    bk = bank[u % 2]
                    at = 1 + c * CHUNK
                    if e < 2:
                        for k in range(4):
                            cut = k if c % 2 == 0 else 0
                            last = pe.matmul(bk[:, cut:CHUNK], ipk[:, 3 - k, e * P:(e + 1) * P],
                                             xa[:, at + cut - k:at + CHUNK - k], start=(k == 0), stop=(k == 3),
                                             skip_group_check=True)
                    else:
                        last = pe.matmul(bk[:, :], ipw[:, e * P:(e + 1) * P], xa[:, at:at + CHUNK],
                                         start=True, stop=True)
                    last.then_inc(s_in, 1)
                    u += 1
            for blk in range(2):
                for c in range(CHUNKS):
                    n = blk * CHUNKS + c
                    pe.wait_ge(s_silu, n + 1)
                    if n > 1:
                        pe.wait_ge(s_xe, n - 1)
                    for j in range(4):
                        last = pe.transpose(bank[2 + n % 2][:, j * P:(j + 1) * P], xs[:, blk, 4 * c + j, :], ident)
                    last.then_inc(s_xt, 1)
            pe.wait_ge(s_xe, 2 * CHUNKS)
            for q in range(GR // 4):
                for c in range(2):
                    n = 2 * q + c
                    if n > 1:
                        pe.wait_ge(s_um, n - 1)
                    for j in range(4):
                        g = 4 * q + j
                        last = pe.matmul(bank[4 + n % 2][:, j * P:(j + 1) * P], v_t[:, c, g, :],
                                         x_tok[:, g * GC:(g + 1) * GC, :].rearrange("p h t -> p (h t)"),
                                         start=True, stop=True, skip_group_check=True)
                    last.then_inc(s_u, 1)
            for q in range(GR // 4):
                pe.wait_ge(s_r, 2 * q + 2)
                if q > 1:
                    pe.wait_ge(s_ye, q - 1)
                for j in range(4):
                    g = 4 * q + j
                    pe.wait_ge(s_toep[g % TRING], 16 * (g // TRING + 1))
                    for c in range(2):
                        pe.matmul(bank[6 + q % 2][:, j * P:(j + 1) * P], g_t[:, c, g, :],
                                  rbd[:, q % 2, c, j, :, :].rearrange("p h t -> p (h t)"),
                                  start=(c == 0), stop=False, skip_group_check=True)
                    for hh in range(GC):
                        last = pe.matmul(bank[6 + q % 2][:, j * P + hh * TILES:j * P + (hh + 1) * TILES],
                                         toep[:, g % TRING, hh, :], x_tok[:, g * GC + hh, :],
                                         start=False, stop=True, skip_group_check=True)
                    last.then_inc(s_yg, 1)
            pe.wait_ge(s_ye, GR // 4)

            def project(c):
                pe.wait_ge(s_yz, 2 * c + 2)
                if c > 1:
                    pe.wait_ge(s_mix, c - 1)
                for blk in range(2):
                    last = pe.matmul(bank[2 + c % 2][:, :], opw[:, blk, :], yz[:, 2 * (c % 2) + blk, :],
                                     start=(blk == 0), stop=(blk == 1))
                last.then_inc(s_op, 1)
            for c in range(CHUNKS):
                for blk in range(2):
                    n = 2 * c + blk
                    if n > 1:
                        pe.wait_ge(s_yz, n - 1)
                    for j in range(4):
                        last = pe.transpose(bank[n % 2][:, j * P:(j + 1) * P],
                                            ysb[:, blk * P:(blk + 1) * P, 4 * c + j], ident)
                    last.then_inc(s_yt, 1)
                if c:
                    project(c - 1)
            project(CHUNKS - 1)

        def mixer_act(act):
            act.wait_ge(s_mc, 16 * MIX_LOADS)
            act.activation(sm[:, 0, :], prm[:, 0, :], ACT.Exp).then_inc(s_dt, 1)
            act.wait_ge(s_tr, 1)
            wf = w_t.rearrange("p c g t -> p c (g t)")
            act.activation(pre[0][:, 0:GR * NTV], pre[0][:, 0:GR * NTV], ACT.Exp).then_inc(s_mag, 1)
            act.wait_ge(s_ph, 1)
            act.activation(wf[:, 1, :], wf[:, 1, :], ACT.Sin).then_inc(s_trig, 1)
            act.activation(wf[:, 0, :], wf[:, 0, :], ACT.Sin).then_inc(s_trig, 1)
            for n in range(2 * (GR // 4)):
                c, k = divmod(n, GR // 4)
                act.wait_ge(s_vt, n + 1)
                act.activation(v_t[:, c, 4 * k:4 * k + 4, :].rearrange("p g t -> p (g t)"), bank[n % 2][:, :],
                               ACT.Copy).then_inc(s_ve, 1)
            norm_act(act, NMIX, xa, 1)
            u = 0
            for e in range(4):
                for c in range(CHUNKS):
                    act.wait_ge(s_in, u + 1)
                    if e < 2:
                        act.activation(xs[:, e, 4 * c:4 * c + 4, ::-1], bank[u % 2][:, :].rearrange("p (t i) -> p t i", i=P),
                                       ACT.Silu, bias=chp[:, e:e + 1]).then_inc(s_silu, 1)
                    else:
                        act.activation(zs[e - 2][:, c * CHUNK:(c + 1) * CHUNK], bank[u % 2][:, :],
                                       ACT.Silu).then_inc(s_silu, 1)
                    u += 1
            for n in range(2 * CHUNKS):
                blk, c = divmod(n, CHUNKS)
                act.wait_ge(s_xt, n + 1)
                act.activation(x_tok[:, blk * P:(blk + 1) * P, 4 * c:4 * c + 4].rearrange("p h t -> p t h"),
                               bank[2 + n % 2][:, :].rearrange("p (t h) -> p t h", t=4), ACT.Copy).then_inc(s_xe, 1)
            for q in range(GR // 4):
                act.wait_ge(s_yg, 4 * q + 4)
                act.activation(ysb[:, 4 * q * GC:4 * (q + 1) * GC, :].rearrange("p h t -> p (h t)"),
                               bank[6 + q % 2][:, :], ACT.Copy).then_inc(s_ye, 1)

        def mixer_dve(dve):
            linked = [0]

            def link(ins):
                linked[0] += 1
                ins.then_inc(s_link, 1)
                dve.wait_ge(s_link, linked[0])
            dve.wait_ge(s_mc, 16 * MIX_LOADS)
            wf = w_t.rearrange("p c g t -> p c (g t)")
            n_t = GR * NTV
            dt, ar, ai = sm[:, 0, :], sm[:, 1, :], sm[:, 2, :]
            a_re, a_im, c_re, c_im = (prm[:, i, :] for i in range(1, 5))
            dve.tensor_tensor(ipk, cw, bc(ipw[:, 0:DIN].unsqueeze(1), (P, 4, DIN)), ALU.mult).then_inc(s_ipk, 1)
            dve.wait_ge(s_dt, 1)
            dve.tensor_tensor(ar, dt, a_re, ALU.mult)
            link(dve.tensor_tensor(ai, dt, a_im, ALU.mult))
            gt = lambda ap: ap.rearrange("p (g t) -> p g t", g=GR)
            ph = pre[1][:, 0:n_t]
            kk = pre[1][:, n_t:2 * n_t]
            tvb = bc(tv.unsqueeze(1), (P, GR, NTV))
            dve.tensor_tensor(gt(pre[0][:, 0:n_t]), bc(ar.unsqueeze(2), (P, GR, NTV)), tvb, ALU.mult).then_inc(s_tr, 1)
            link(dve.tensor_tensor(gt(ph), bc(ai.unsqueeze(2), (P, GR, NTV)), tvb, ALU.mult))
            for c, quarter in ((1, 0.0), (0, 0.25)):
                r = wf[:, c, :]
                link(dve.tensor_scalar(kk, ph, 1 / (2 * np.pi), quarter, ALU.mult, ALU.add))
                link(dve.tensor_scalar(kk, kk, MAGIC, None, ALU.add))
                link(dve.tensor_scalar(kk, kk, -MAGIC, None, ALU.add))
                link(dve.scalar_tensor_tensor(out=r, in0=kk, scalar=-PI_A, in1=ph, op0=ALU.mult, op1=ALU.add))
                link(dve.scalar_tensor_tensor(out=r, in0=kk, scalar=-PI_B, in1=r, op0=ALU.mult, op1=ALU.add))
                link(dve.scalar_tensor_tensor(out=r, in0=kk, scalar=-PI_C, in1=r, op0=ALU.mult, op1=ALU.add))
                link(dve.tensor_scalar(r, r, 2 * np.pi * quarter, PI_IN, ALU.add, ALU.min))
                last = dve.tensor_scalar(r, r, -PI_IN, None, ALU.max)
                link(last)
            dve.sem_inc(s_ph, 1)
            dve.wait_ge(s_mag, 1)
            dve.wait_ge(s_trig, 2)
            link(dve.tensor_tensor(w_t.rearrange("p c g t -> p c (g t)"), w_t.rearrange("p c g t -> p c (g t)"),
                                   bc(pre[0][:, 0:n_t].unsqueeze(1), (P, 2, n_t)), ALU.mult))
            w1r, w1i = w_t[:, 0, :, 1], w_t[:, 1, :, 1]
            s_ = lambda i: sm[:, i, :]
            tt = dve.tensor_tensor
            tt(s_(3), a_re, a_re, ALU.mult)
            link(tt(s_(4), a_im, a_im, ALU.mult))
            link(tt(s_(3), s_(3), s_(4), ALU.add))
            link(dve.reciprocal(s_(3), s_(3)))
            link(dve.tensor_scalar(s_(4), w1r, -1.0, None, ALU.add))
            tt(s_(5), s_(4), a_re, ALU.mult)
            tt(s_(6), w1i, a_im, ALU.mult)
            tt(s_(7), w1i, a_re, ALU.mult)
            link(tt(s_(8), s_(4), a_im, ALU.mult))
            tt(s_(5), s_(5), s_(6), ALU.add)
            link(tt(s_(7), s_(7), s_(8), ALU.subtract))
            tt(s_(5), s_(5), s_(3), ALU.mult)
            link(tt(s_(7), s_(7), s_(3), ALU.mult))
            tt(s_(6), c_re, s_(5), ALU.mult)
            tt(s_(8), c_im, s_(7), ALU.mult)
            tt(s_(9), c_re, s_(7), ALU.mult)
            link(tt(s_(10), c_im, s_(5), ALU.mult))
            tt(s_(6), s_(6), s_(8), ALU.subtract)
            link(tt(s_(9), s_(9), s_(10), ALU.add))
            dve.tensor_scalar(s_(6), s_(6), 2.0, None, ALU.mult)
            link(dve.tensor_scalar(s_(9), s_(9), 2.0, None, ALU.mult))
            war, wai = w_t[:, 0, :, 16:24], w_t[:, 1, :, 16:24]
            b8 = lambda i: bc(s_(i).unsqueeze(2), (P, GR, 8))
            x8 = [pre[0][:, i * GR * 8:(i + 1) * GR * 8].rearrange("p (g a) -> p g a", g=GR) for i in range(2)]
            tt(ca[:, 0, :, :], b8(6), war, ALU.mult)
            tt(x8[0], b8(9), wai, ALU.mult)
            tt(ca[:, 1, :, :], b8(6), wai, ALU.mult)
            link(tt(x8[1], b8(9), war, ALU.mult))
            tt(ca[:, 0, :, :], ca[:, 0, :, :], x8[0], ALU.subtract)
            link(tt(ca[:, 1, :, :], ca[:, 1, :, :], x8[1], ALU.add))

            def outer_product(out, ar_, ai_, imag, negate=False):
                o4 = out.rearrange("p g (a b) -> p g a b", b=16)
                t4 = pre[0].rearrange("p (g a b) -> p g a b", g=GR, b=16)
                lo = lambda ap, k: bc(ap[:, k, :].unsqueeze(2), (P, 8, 16))
                wb = w_t[:, :, :, 0:16]
                shape = (P, GR, 8, 16)
                left = lambda ap: bc(ap.unsqueeze(3), shape)
                right = lambda c: bc(wb[:, c, :, :].unsqueeze(2), shape)
                tt(o4, left(ar_), right(1 if imag else 0), ALU.mult)
                link(tt(t4, left(ai_), right(0 if imag else 1), ALU.mult))
                of, tf = out.rearrange("p g t -> p (g t)"), pre[0]
                if negate:
                    return dve.scalar_tensor_tensor(out=of, in0=of, scalar=-1.0, in1=tf, op0=ALU.mult, op1=ALU.subtract)
                return tt(of, of, tf, ALU.add if imag else ALU.subtract)
            outer_product(g_t[:, 0, :, :], ca[:, 0, :, :], ca[:, 1, :, :], False).then_inc(s_g, 1)
            dve.wait_ge(s_g, 1)
            link(outer_product(g_t[:, 1, :, :], ca[:, 0, :, :], ca[:, 1, :, :], True, True))
            row = pre[1].rearrange("p (g t) -> p g t", g=GR)
            for c in range(2):
                if c:
                    dve.wait_ge(s_vt, GR // 4)
                outer_product(row, w_t[:, 0, :, 24:32], w_t[:, 1, :, 24:32], c == 1).then_inc(s_row, 1)
                dve.wait_ge(s_row, c + 1)
            link(dve.memset(kp, 0.0))
            dve.wait_ge(s_kk, 1)
            link(dve.tensor_copy(kp[:, :, P - 1:2 * P - 1], bank[7][:, 0:2 * P].rearrange("p (a t) -> p a t", a=2)))
            tt(kp[:, :, P - 1:P], kp[:, :, P - 1:P], chp[:, 2:4].unsqueeze(2), ALU.add).then_inc(s_kp, 1)
            norm_dve(dve, NMIX, xa, 1, None)
            dve.wait_ge(s_kd, 16)
            for n in range(2 * (GR // 4)):
                q, c = divmod(n, 2)
                dve.wait_ge(s_u, n + 1)
                if n > 1:
                    dve.wait_ge(s_ur, n - 1)
                t4 = tmp[:, n % 2, :].rearrange("p (g h t) -> p g h t", g=4, h=GC)
                tt(t4, bank[4 + n % 2][:, :].rearrange("p (g h t) -> p g h t", g=4, h=GC),
                   bc(blockd.unsqueeze(1).unsqueeze(3), (P, 4, GC, TILES)), ALU.mult).then_inc(s_um, 1)
                dve.wait_ge(s_um, n + 1)
                dve.tensor_reduce(ust[:, c, 4 * q:4 * q + 4, :], t4.rearrange("p g h t -> p g t h"), AX.X,
                                  ALU.add).then_inc(s_ur, 1)
            dve.wait_ge(s_ur, 2 * (GR // 4))
            u5 = ust.rearrange("p c g (b j) -> p c g b j", b=B)
            wr = bc(w_t[:, 0, :, NTV - 1].unsqueeze(1).unsqueeze(3), (P, 2, GR, B))
            wi = bc(w_t[:, 1, :, NTV - 1].unsqueeze(2), (P, GR, B))
            pa = tmp[:, 0, 0:2 * GR * B].rearrange("p (c g b) -> p c g b", c=2, g=GR)
            pb = tmp[:, 1, 0:2 * GR * B].rearrange("p (c g b) -> p c g b", c=2, g=GR)
            for j in range(1, SEQ_TILES):
                tt(pa, u5[:, :, :, :, j - 1], wr, ALU.mult)
                tt(pb[:, 0], u5[:, 1, :, :, j - 1], wi, ALU.mult)
                link(tt(pb[:, 1], u5[:, 0, :, :, j - 1], wi, ALU.mult))
                link(tt(u5[:, :, :, :, j], u5[:, :, :, :, j], pa, ALU.add))
                tt(u5[:, 0, :, :, j], u5[:, 0, :, :, j], pb[:, 0], ALU.subtract)
                link(tt(u5[:, 1, :, :, j], u5[:, 1, :, :, j], pb[:, 1], ALU.add))
            s6 = sh.rearrange("p c g (b j) -> p (c g) b j", b=B)
            dve.memset(s6[:, :, :, 0:1], 0.0)
            link(dve.tensor_copy(s6[:, :, :, 1:SEQ_TILES],
                                 ust.rearrange("p c g (b j) -> p (c g) b j", b=B)[:, :, :, 0:SEQ_TILES - 1]))
            for q in range(GR // 4):
                if q > 1:
                    dve.wait_ge(s_yg, 4 * (q - 1))
                for c in range(2):
                    tt(rbd[:, q % 2, c], bc(sh[:, c, 4 * q:4 * q + 4, :].unsqueeze(2), (P, 4, GC, TILES)),
                       bc(blockd.unsqueeze(1).unsqueeze(3), (P, 4, GC, TILES)), ALU.mult).then_inc(s_r, 1)

            def residual(c):
                dve.wait_ge(s_op, c + 1)
                xm = x_main[:, c * CHUNK:(c + 1) * CHUNK]
                tt(xm, xm, bank[2 + c % 2][:, :], ALU.add).then_inc(s_mix, 1)
            for n in range(2 * CHUNKS):
                c, blk = divmod(n, 2)
                dve.wait_ge(s_yt, n + 1)
                if blk == 0 and c > 1:
                    dve.wait_ge(s_op, c - 1)
                tt(yz[:, 2 * (c % 2) + blk, :], bank[n % 2][:, :], zs[blk][:, c * CHUNK:(c + 1) * CHUNK],
                   ALU.mult).then_inc(s_yz, 1)
                if blk and c:
                    residual(c - 1)
            residual(CHUNKS - 1)

        def mixer_pool(pool):
            norm_pool(pool, NMIX)

        def mixer_sync(sp):
            sp.wait_ge(s_mac, 1)
            for dst, name in ((prm, "prm"), (tv, "tv"), (blockd, "blockd"), (sel, "sel"), (ipw, "ipw"), (opw, "opw"),
                              (cw, "cw"), (chp, "chp")):
                sp.dma_start(dst, ins[name]).then_inc(s_mc, 16)
            sp.wait_ge(s_kp, 1)
            sp.dma_start(kpad.rearrange("(a p) t -> p a t", p=P), kp).then_inc(s_kd, 16)
            sp.wait_ge(s_kd, 16)
            for g in range(GR):
                if g >= TRING:
                    sp.wait_ge(s_yg, g - TRING + 1)
                src = bass.AP(tensor=kpad.tensor, offset=kpad.offset + g * GC * 2 * P, ap=[[1, P], [2 * P, GC], [1, P]])
                sp.dma_start(toep[:, g % TRING, :, :], src).then_inc(s_toep[g % TRING], 16)

        block = ctx.enter_context(nc.Block())

        @block.sync
        def _(sp):
            sp.dma_start(consts[:, :], ins["consts"]).then_inc(s_const, 16)
            sp.dma_start(x_main[:, :], ins["x"]).then_inc(s_x, 16)
            sp.dma_start(raw_m, ins["masks"]).then_inc(s_const, 16)
            def rotary_loads():
                sp.dma_start(raw_c, ins["rot_c"]).then_inc(s_raw, 16)
                sp.dma_start(raw_s, ins["rot_s"]).then_inc(s_raw, 16)
                sp.dma_start(qks, ins["qks"]).then_inc(s_raw, 16)
            rotary_loads()
            for lx in range(2 * DEPTH):
                l = lx % DEPTH
                if lx:
                    sp.wait_ge(s_wo, lx * TILES)
                sp.dma_start(wqkv[:, :], ins["wqkv"][l]).then_inc(s_wa, 16)
                sp.dma_start(wo[:, :, :], ins["wo"][l].rearrange("(j p) n -> p j n", p=P)).then_inc(s_wa, 16)
                if lx:
                    sp.wait_ge(s_xa, xa_count(lx, (lx - 1) // DEPTH))
                sp.dma_start(w1[:, :], ins["w1"][l]).then_inc(s_wf, 16)
                for f, (at, w) in enumerate(HB):
                    sp.dma_start(w2[0:w, f, :], ins["w2"][l][at:at + w, :]).then_inc(s_wf, 16)
                sp.dma_start(par[:, :], ins["par"][l]).then_inc(s_wf, 16)
                if lx == DEPTH:
                    mixer_sync(sp)
                    sp.wait_ge(s_mix, CHUNKS)
                    rotary_loads()
            sp.wait_ge(s_mac, 2)
            sp.dma_start(out, x_main[:, :]).then_inc(s_out, 16)
            sp.wait_ge(s_out, 16)

        @block.gpsimd
        def _(pool):
            pool.memset(exp_half[:, :], -0.5).then_inc(s_init, 1)
            pool.memset(xa[:, 0:1], 0.0).then_inc(s_init, 1)
            pool.memset(xb[:, 0:1], 0.0).then_inc(s_init, 1)
            pool.memset(kT[:, :, :, :], 0.0).then_inc(s_init, 1)
            for i in range(2):
                pool.memset(v[i][:, :, :], 1.0).then_inc(s_init, 1)
                pool.memset(vmix[i][:, :, :], 0.0).then_inc(s_init, 1)
            pool.wait_ge(s_init, INITS)
            pool.wait_ge(s_const, 32)
            macaron_pool(pool, 0)
            mixer_pool(pool)
            macaron_pool(pool, 1)

        @block.scalar
        def _(act):
            act.wait_ge(s_init, INITS)
            macaron_act(act, 0)
            mixer_act(act)
            macaron_act(act, 1)

        @block.vector
        def _(dve):
            dve.wait_ge(s_const, 32)
            masks_dve(dve)
            dve.wait_ge(s_init, INITS)
            macaron_dve(dve, 0)
            mixer_dve(dve)
            macaron_dve(dve, 1)

        @block.tensor
        def _(pe):
            pe.wait_ge(s_const, 32)
            pe.wait_ge(s_mask, 1)
            macaron_pe(pe, 0)
            mixer_pe(pe)
            macaron_pe(pe, 1)


def shape_constants():
    consts = np.zeros((P, C_W), np.float32)
    consts[:, C_ID:C_ID + P] = np.eye(P)
    consts[:, C_CEN:C_CEN + P] = np.eye(P) - 1.0 / P
    consts[:, C_ONE:C_ONE + P] = 1.0
    flag = np.ones(TILES)
    flag[::SEQ_TILES] = 0
    consts[:, C_FLAG:] = flag
    i = np.arange(WIN)[:, None]
    j = np.arange(WIN)[None, :]
    own, older = i >= j, j >= i
    keep = np.zeros((2, P, P), bool)
    keep[:, 0:WIN, 0:WIN], keep[:, 0:WIN, WIN:] = own, older
    keep[:, WIN:, 0:WIN], keep[:, WIN:, WIN:] = older, own
    keep[0, 0:WIN, WIN:] = False
    masks = np.where(keep, 0.0, MASKED).transpose(1, 0, 2).astype(np.float32)
    half = np.arange(0, DH, 2, dtype=np.float32)
    inv = np.float32(1.0) / np.power(np.float32(10000.0), half / np.float32(DH)).astype(np.float32)
    t = np.arange(N, dtype=np.float32)
    fr = (t[:, None] * inv[None, :]).astype(np.float32).astype(np.float64)
    base = (half.astype(np.float64) + 0.4 * DH) / (1.4 * DH)
    sc = base[None, :] ** ((t - N // 2) / float(WIN // 2))[:, None].astype(np.float64)
    cos, sin = np.cos(fr), np.sin(fr)
    qk_scale = 8.0
    c = np.stack([np.tile(cos * sc, 2) * qk_scale, np.tile(cos / sc, 2)], 1)
    s = np.stack([np.concatenate([-sin * sc, sin * sc], 1) * qk_scale, np.concatenate([-sin / sc, sin / sc], 1)], 1)
    lay = lambda a: np.ascontiguousarray(a.astype(np.float32).reshape(SEQ_TILES, P, 2, DH).transpose(1, 0, 2, 3))
    blockd = (np.arange(P)[:, None] // NS == np.arange(GC)).astype(np.float32)
    sel = np.zeros((P, SEL), np.float32)
    sel[:, P - GC:P] = blockd
    tvs = np.ascontiguousarray(np.broadcast_to(np.array(TV, np.float32), (P, NTV)))
    return dict(blockd=blockd, sel=sel, tv=tvs, consts=consts, masks=np.ascontiguousarray(masks), rot_c=lay(c), rot_s=lay(s))


def kernel(**inputs):
    import concourse.bacc as bacc
    from concourse.bass_utils import run_bass_kernel_spmd

    a = {k.replace("L0_", ""): np.asarray(v) for k, v in inputs.items()}
    f32 = np.float32
    arrays = shape_constants()
    arrays["x"] = np.ascontiguousarray(a["attn_hidden_states"].reshape(T, D).T)
    arrays["wqkv"] = a["ffn_wqkv"]
    arrays["wo"] = a["ffn_wo"]
    arrays["w1"] = a["ffn_w1"]
    arrays["w2"] = a["ffn_w2"]
    qk = np.stack([a["ffn_q_scale"], a["ffn_k_scale"]], 1)
    arrays["qks"] = np.ascontiguousarray(np.broadcast_to(qk, (P, DEPTH, 2, DH)))
    pp = np.zeros((DEPTH, P, NPAR), f32)
    for l in range(DEPTH):
        pp[l, :, 0], pp[l, :, 1], pp[l, :, 2] = a["ffn_ln_g"][l], a["ffn_ln_b"][l], a["ffn_b2"][l]
        for g in range(2):
            for f, (at, w) in enumerate(HB):
                pp[l, :w, 4 + 3 * g + f] = a["ffn_b1"][l, g * HID + at:g * HID + at + w]
    arrays["par"] = pp

    rows = lambda z: z.reshape(GR, P).T
    arrays["prm"] = np.stack([rows(np.repeat(a["attn_log_dt"][:, None], NS, 1))]
                             + [rows(a["attn_" + k]) for k in ("A_re", "A_im", "C_re", "C_im")], 1)
    arrays["ipw"] = a["attn_in_proj_w"].T
    arrays["opw"] = a["attn_out_proj_w"].T.reshape(2, P, D).transpose(1, 0, 2)
    arrays["cw"] = np.broadcast_to(a["attn_conv_w"].T, (P, 4, DIN))
    arrays["chp"] = np.concatenate([a["attn_conv_b"].reshape(2, P).T, a["attn_D_skip"].reshape(2, P).T], 1)

    nc = bacc.Bacc("TRN2", target_bir_lowering=False, num_devices=1)
    aps, feeds = {}, {}
    for name, arr in arrays.items():
        arr = np.ascontiguousarray(arr)
        feeds["in_" + name] = arr
        aps[name] = nc.dram_tensor("in_" + name, arr.shape, mybir.dt.from_np(arr.dtype), kind="ExternalInput").ap()
    out = nc.dram_tensor("out_x", (P, T), F32, kind="ExternalOutput").ap()
    kpad = nc.dram_tensor("kpad", (DIN, 2 * P), F32, kind="Internal").ap()
    build(nc, aps, kpad, out)
    got = run_bass_kernel_spmd(nc, [feeds], core_ids=[0]).results[0]["out_x"]
    return np.ascontiguousarray(got.T).reshape(B, N, D)
```

```python
from contextlib import ExitStack

import numpy as np

import concourse.bass as bass
from concourse import mybir

F32 = mybir.dt.float32
BF16 = mybir.dt.bfloat16
ALU = mybir.AluOpType
ACT = mybir.ActivationFunctionType
AX = mybir.AxisListType

P = 128
B, N = 2, 1024
T = B * N
TILES = T // P
SEQ_TILES = N // P
CHUNK = 512
CHUNKS = T // CHUNK
D = 128
H, DH = 8, 64
INNER = H * DH
WIN = 64
DEPTH = 2
HID = D * 4 * 2 // 3
HB = [(f, min(P, HID - f)) for f in range(0, HID, P)]
EPS = 1e-5
MASKED = -1e38

C_ID, C_CEN, C_ONE, C_FLAG, C_W = 0, P, 2 * P, 3 * P, 3 * P + TILES
NPAR = 10

INITS = 8
DIN, NS = 2 * D, 16
GC = P // NS
GR = DIN // GC
TV = list(range(16)) + [16 * a for a in range(8)] + [16 * a + 1 for a in range(8)] + [P]
NTV = len(TV)
SEL = 2 * P - GC
POWER_STEPS = 20
AHEAD = 3
TRING = 8
ARENA = 37920
MIX_LOADS = 8
PI_A = 6.28125
PI_B = float(np.float32(np.round((2 * np.pi - PI_A) * 2 ** 20) / 2 ** 20))
PI_C = float(np.float32(2 * np.pi - PI_A - PI_B))
PI_IN = 3.1415925
MAGIC = 1.5 * 2 ** 23
T_USES = 5
T_BANKS = 2


def bc(ap, shape):
    return ap.to_broadcast(list(shape))


def build(nc, ins, kpad, out):
    with ExitStack() as ctx:
        def sb(name, shape, dt=F32):
            return ctx.enter_context(nc.sbuf_tensor(name, shape, dt))

        def sem(name):
            return ctx.enter_context(nc.semaphore(name))

        consts = sb("consts", [P, C_W])
        ident = consts[:, C_ID:C_ID + P]
        center = consts[:, C_CEN:C_CEN + P]
        ones = consts[:, C_ONE:C_ONE + P]
        flag = consts[:, C_FLAG:C_FLAG + TILES]
        ident_bf = sb("ident_bf", [P, P], BF16)
        masks = sb("masks", [P, TILES, P], BF16)
        par = sb("par", [P, NPAR])
        x_main = sb("x_main", [P, T])
        xa = sb("xa", [P, 1 + T])
        xb = sb("xb", [P, 1 + T])
        wqkv = sb("wqkv", [P, 3 * INNER])
        wo = sb("wo", [P, INNER // P, D])
        w1 = sb("w1", [P, 2 * HID])
        w2 = sb("w2", [P, len(HB), D])
        exp_half = sb("exp_half", [P, TILES])
        kT = sb("kT", [P, 4, 4, WIN])
        v = [sb(f"v{i}", [P, H, DH]) for i in range(2)]
        vmix = [sb(f"vmix{i}", [P, H, DH]) for i in range(2)]
        ssum = sb("ssum", [P, 2 * H])
        smax = sb("smax", [P, 2 * H])
        rn = sb("rn", [P, 2 * H])
        mx = sb("mx", [P, H])
        esum = sb("esum", [P, H])
        rsum = sb("rsum", [P, H])
        vare = sb("vare", [P, TILES])
        rstd = sb("rstd", [P, TILES])
        arena = sb("arena", [P, ARENA])

        def carver(at):
            def take(*shape):
                nonlocal at
                n = int(np.prod(shape))
                ap = arena[:, at:at + n]
                at += n
                assert at <= ARENA, at
                names = "abcde"[:len(shape)]
                if len(shape) > 1:
                    ap = ap.rearrange(f"p ({' '.join(names)}) -> p {' '.join(names)}",
                                      **{k: v_ for k, v_ in zip(names, shape)})
                return ap
            return take
        common = 2 * CHUNK + 4 * P
        ln = (par[:, 0:1], par[:, 1:2])
        take = carver(0)
        sqf = take(2, CHUNK)
        diag = take(4, P)
        raw_c = take(SEQ_TILES, 2, DH)
        raw_s = take(SEQ_TILES, 2, DH)
        qks = take(DEPTH, 2, DH)
        rot_a = take(DEPTH, TILES, 2, DH)
        rot_b = take(DEPTH, TILES, 2, DH)
        raw_m = take(2, P)
        hs = [take(P) for _ in range(2)]
        sq = [take(2 * INNER) for _ in range(2)]
        t12 = take(4, 2 * INNER)
        t1 = [t12[:, i, :] for i in range(2)]
        t2 = [t12[:, 2 + i, :] for i in range(2)]
        qkn = take(2 * INNER)
        qT = take(4, P)
        prob = take(2, 4, P)
        pT = take(2, 4, P)
        oT = take(4, P)
        hsh = take(2, CHUNK)
        y = take(T)
        gel = take(2, CHUNK)
        hid = take(2, CHUNK)
        take = carver(common)
        v_t = take(2, GR, P)
        g_t = take(2, GR, P)
        xs = take(2, TILES, P)
        ysb = xs.rearrange("p a b c -> p (a b c)").rearrange("p (h t) -> p h t", t=TILES)
        x_tok = take(DIN // 2, 4, TILES)
        zs = [xb[:, 1:1 + T], xa[:, 1:1 + T]]
        toep = [v_t[:, i % 2, i // 2 * GC:(i // 2 + 1) * GC, :] for i in range(TRING)]
        w_t = take(2, GR, NTV)
        ust = take(2, GR, TILES)
        sh = take(2, GR, TILES)
        rbd = take(2, 2, 4, GC, TILES)
        tmp = sqf
        yz = rbd.rearrange("p a b c d e -> p (a b c d e)").rearrange("p (a b) -> p a b", a=4)
        ipw = take(2 * DIN)
        opw = take(2, D)
        sel = take(SEL)
        tv = take(NTV)
        blockd = take(GC)
        early = rbd.rearrange("p a b c d e -> p (a b c d e)")
        cw, ipk = (early[:, i * 4 * DIN:(i + 1) * 4 * DIN].rearrange("p (k h) -> p k h", k=4) for i in range(2))
        prm = take(5, GR)
        chp = take(4)
        early = sh.rearrange("p a b c -> p (a b c)")
        sm = early[:, 0:12 * GR].rearrange("p (i g) -> p i g", g=GR)
        ca = early[:, 16 * GR:32 * GR].rearrange("p (c g a) -> p c g a", c=2, g=GR)
        kp = ipk.rearrange("p k h -> p (k h)")[:, 0:4 * P].rearrange("p (a t) -> p a t", a=2)
        pre = g_t[:, 1].rearrange("p g t -> p (g t)")
        grow, ph, kk = (t12.rearrange("p i c -> p (i c)")[:, i * GR * NTV:(i + 1) * GR * NTV] for i in range(3))
        kscr = kT.rearrange("p a b c -> p (a b c)")
        nca = cw.rearrange("p k h -> p (k h)")[:, 0:2 * GR * 8].rearrange("p (c g a) -> p c g a", c=2, g=GR)

        bank = [ctx.enter_context(nc.psum_tensor(f"bank{i}", [P, CHUNK], F32)) for i in range(8)]
        QK = [bank[0], bank[1]]
        SC = [bank[2], bank[3]]
        TB = [bank[4], bank[5]]
        OB = bank[6]
        WO = bank[7][:, 0:P]

        s_const = sem("s_const")
        s_rawm = sem("s_rawm")
        s_mask = sem("s_mask")
        s_raw = sem("s_raw")
        s_x = [sem(f"s_x{c}") for c in range(CHUNKS)]
        s_wa = sem("s_wa")
        s_wf = sem("s_wf")
        s_rot = sem("s_rot")
        s_init = sem("s_init")
        s_hs = sem("s_hs")
        s_qk = sem("s_qk")
        s_sq = sem("s_sq")
        s_t12 = sem("s_t12")
        s_ss = sem("s_ss")
        s_ssm = sem("s_ssm")
        s_rn = sem("s_rn")
        s_add = sem("s_add")
        s_qkn = sem("s_qkn")
        s_T = sem("s_T")
        s_Tf = sem("s_Tf")
        s_sc = sem("s_sc")
        s_mx = sem("s_mx")
        s_exp = sem("s_exp")
        s_pv = sem("s_pv")
        s_vm = sem("s_vm")
        s_rs = sem("s_rs")
        s_pn = sem("s_pn")
        s_oT = sem("s_oT")
        s_wo = sem("s_wo")
        s_res = sem("s_res")
        s_hsh = sem("s_hsh")
        s_cen = sem("s_cen")
        s_csb = sem("s_csb")
        s_sqf = sem("s_sqf")
        s_var = sem("s_var")
        s_vare = sem("s_vare")
        s_rstd = sem("s_rstd")
        s_diag = sem("s_diag")
        s_rb = sem("s_rb")
        s_yn = sem("s_yn")
        s_y = sem("s_y")
        s_ag = sem("s_ag")
        s_gel = sem("s_gel")
        s_hid = sem("s_hid")
        s_down = sem("s_down")
        s_xa = sem("s_xa")
        s_mac = sem("s_mac")
        s_mc = sem("s_mc")
        s_dt = sem("s_dt")
        s_pw = sem("s_pw")
        s_mag = sem("s_mag")
        s_trig = sem("s_trig")
        s_link = sem("s_link")
        s_g = sem("s_g")
        s_g1 = sem("s_g1")
        s_row = sem("s_row")
        s_rowp = sem("s_rowp")
        s_w = sem("s_w")
        s_nca = sem("s_nca")
        s_plink = sem("s_plink")
        s_vt = sem("s_vt")
        s_ve = sem("s_ve")
        s_kk = sem("s_kk")
        s_kp = sem("s_kp")
        s_kd = sem("s_kd")
        s_toep = [sem(f"s_toep{i}") for i in range(TRING)]
        s_ipk = sem("s_ipk")
        s_in = sem("s_in")
        s_silu = sem("s_silu")
        s_xt = sem("s_xt")
        s_xe = sem("s_xe")
        s_u = sem("s_u")
        s_um = sem("s_um")
        s_ur = sem("s_ur")
        s_r = sem("s_r")
        s_tg = sem("s_tg")
        s_yg = sem("s_yg")
        s_ye = sem("s_ye")
        s_yk = sem("s_yk")
        s_yl = sem("s_yl")
        s_xz = sem("s_xz")
        s_yt = sem("s_yt")
        s_yz = sem("s_yz")
        s_op = sem("s_op")
        s_mix = sem("s_mix")
        s_out = sem("s_out")

        K_SLOT = {(0, 0): 0, (1, 0): 1, (1, 1): 2, (0, 1): 3}

        def xa_count(layers, m):
            return (layers + 2 * m + 1) * CHUNKS

        def t_before(s):
            if isinstance(s, int):
                return sum(len(t_names(r)) for r in range(s))
            return t_before(4) + T_USES * (s - 4)

        def t_base(lx):
            return lx * (T_USES * TILES)

        def steps(eng, step):
            for s in range(4):
                step(s, s % 2)
            with eng.Fori(0, (TILES - 4) // 2) as i:
                step(2 * i + 4, 0)
                step(2 * i + 5, 1)
            for s in range(TILES, TILES + 4):
                step(s, s % 2)

        def past(s, lag):
            return not isinstance(s, int) or s >= lag

        def live(s, lag):
            return not isinstance(s, int) or 0 <= s - lag < TILES

        def t_names(s):
            lags = (("qT", 2), ("kT", 2), ("pT0", 3), ("pT1", 3), ("v", 1))
            return [n for n, lag in lags if live(s, lag)]

        def t_uses(s, p):
            first = t_before(s) if isinstance(s, int) else t_before(4 + p)
            return {n: (t_before(s) + j, (first + j) % T_BANKS) for j, n in enumerate(t_names(s))}

        def norm_banks(c, ways):
            return (bank[0], bank[1], bank[1]) if ways == 1 else (bank[c % 2], bank[2 + c % 2], bank[6 + c % 2])

        def norm_shift(dve, n, n_plain, c, src, ready):
            k = (n - n_plain) * CHUNKS + c
            if c > 1:
                dve.wait_ge(s_cen, n * CHUNKS + c - 1)
            first = int(c % (N // CHUNK) == 0)
            at = c * CHUNK + 1
            dve.wait_ge(*ready)
            dve.tensor_copy(hsh[0:64, c % 2, :], src[0:64, at:at + CHUNK])
            if first:
                dve.memset(hsh[64:128, c % 2, 0:1], 0.0)
            dve.tensor_copy(hsh[64:128, c % 2, first:CHUNK],
                            src[64:128, at - 1 + first:at - 1 + CHUNK]).then_inc(s_hsh, 1)

        def norm_center(pe, n, c, ways, rhs, ready):
            pe.wait_ge(*ready)
            if c >= ways:
                pe.wait_ge(s_csb, n * CHUNKS + c + 1 - ways)
            pe.matmul(norm_banks(c, ways)[0][:, :], center, rhs, start=True, stop=True).then_inc(s_cen, 1)

        def norm_square(act, n, c, ways, dst, off):
            k = n * CHUNKS + c
            src = norm_banks(c, ways)[0]
            act.wait_ge(s_cen, k + 1)
            if c > 1:
                act.wait_ge(s_var, k - 1)
            act.activation(sqf[:, c % 2, :], src[:, :], ACT.Square).then_inc(s_sqf, 1)
            act.activation(dst[:, off + c * CHUNK:off + (c + 1) * CHUNK], src[:, :], ACT.Copy).then_inc(s_csb, 1)

        def norm_var(pe, n, c, ways):
            k = n * CHUNKS + c
            pe.wait_ge(s_sqf, k + 1)
            if c >= ways:
                pe.wait_ge(s_yn if ways == 1 else s_vare, k + 1 - ways)
            for j in range(4):
                last = pe.matmul(norm_banks(c, ways)[2][:, j:j + 1], sqf[:, c % 2, j * P:(j + 1) * P],
                                 ones[:, 0:1], start=True, stop=True, skip_group_check=True)
            last.then_inc(s_var, 1)

        def norm_vare(dve, n, c, ways):
            dve.wait_ge(s_var, n * CHUNKS + c + 1)
            dve.tensor_scalar(vare[:, 4 * c:4 * c + 4], norm_banks(c, ways)[2][:, 0:4], 1.0 / D, EPS,
                              ALU.mult, ALU.add).then_inc(s_vare, 1)

        def norm_pow(pool, n, c):
            pool.wait_ge(s_vare, n * CHUNKS + c + 1)
            pool.tensor_tensor(rstd[:, 4 * c:4 * c + 4], vare[:, 4 * c:4 * c + 4], exp_half[:, 0:4],
                               ALU.pow).then_inc(s_rstd, 1)

        def norm_diag(dve, n, c):
            k = n * CHUNKS + c
            dve.wait_ge(s_rstd, k + 1)
            if c:
                dve.wait_ge(s_rb, k)
            dve.tensor_tensor(diag[:, :, :], bc(ident.unsqueeze(1), (P, 4, P)),
                              bc(rstd[:, 4 * c:4 * c + 4].unsqueeze(2), (P, 4, P)), ALU.mult).then_inc(s_diag, 1)

        def norm_spread(pe, n, c, ways):
            pe.wait_ge(s_diag, n * CHUNKS + c + 1)
            if c >= ways > 1:
                pe.wait_ge(s_yn, n * CHUNKS + c + 1 - ways)
            pe.matmul(norm_banks(c, ways)[1][:, :], ones, diag[:, :, :].rearrange("p a b -> p (a b)"),
                      start=True, stop=True).then_inc(s_rb, 1)

        def norm_scale(dve, n, c, ways, dst, off, gb):
            k = n * CHUNKS + c
            dve.wait_ge(s_rb, k + 1)
            dve.wait_ge(s_csb, k + 1)
            d = dst[:, off + c * CHUNK:off + (c + 1) * CHUNK]
            dve.tensor_tensor(d, d, norm_banks(c, ways)[1][:, :], ALU.mult).then_inc(s_yn, 1)
            dve.wait_ge(s_yn, k + 1)
            if gb is not None:
                dve.tensor_scalar(d, d, gb[0], gb[1], ALU.mult, ALU.add).then_inc(s_y, 1)
            else:
                dve.sem_inc(s_y, 1)
                dve.sem_inc(s_xa, 1)

        def norm_pe(pe, n, src, ready):
            for k in range(CHUNKS + 2):
                if k < CHUNKS:
                    norm_center(pe, n, k, 2, src[:, k * CHUNK:(k + 1) * CHUNK], ready(k))
                if 1 <= k <= CHUNKS:
                    norm_var(pe, n, k - 1, 2)
                if k >= 2:
                    norm_spread(pe, n, k - 2, 2)

        def norm_act(act, n, dst, off):
            for c in range(CHUNKS):
                norm_square(act, n, c, 2, dst, off)

        def norm_pool(pool, n, beside=None):
            for c in range(CHUNKS):
                norm_pow(pool, n, c)
                if beside is not None:
                    beside(c)

        def norm_dve(dve, n, dst, off, gb, beside=None):
            for k in range(CHUNKS + 1):
                if k < CHUNKS:
                    norm_vare(dve, n, k, 2)
                if k:
                    norm_diag(dve, n, k - 1)
                if k < CHUNKS and beside is not None:
                    beside(k)
                if k:
                    norm_scale(dve, n, k - 1, 2, dst, off, gb)

        def tail_chunk(s, lag=0):
            return s - lag - TILES if isinstance(s, int) and 0 <= s - lag - TILES < CHUNKS - 1 else None

        def attention_pe(pe, lx, n):
            pe.wait_ge(s_wa, (lx + 1) * 32)
            base, tb = lx * TILES, t_base(lx)

            def done(s, lag):
                return base + s - lag + 1

            def take(uses, name):
                n, b = uses[name]
                if not isinstance(n, int) or n >= T_BANKS:
                    pe.wait_ge(s_Tf, tb + n - 1)
                return TB[b]

            def add_masks(s):
                if past(s, 3):
                    pe.wait_ge(s_exp, done(s, 3))
                for r in range(2):
                    pe.matmul(SC[r][:, :], ident_bf[:, :], bc(masks[:, bass.ds(s - 2, 1), :], (P, 4, P)),
                              start=True, stop=False, skip_group_check=True)

            def step(s, p):
                uses = t_uses(s, p)
                c = tail_chunk(s)
                if tail_chunk(s, 1) is not None:
                    norm_spread(pe, n, tail_chunk(s, 1), 1)
                if c is not None:
                    if c == 0:
                        pe.wait_ge(s_sq, base + TILES)
                    norm_center(pe, n, c, 1, hsh[:, c % 2, :], (s_hsh, (lx * CHUNKS) + c + 1))
                if live(s, 0):
                    pe.wait_ge(s_hs, done(s, 0))
                    if past(s, 1):
                        pe.wait_ge(s_sq, done(s, 1))
                    for j in range(2):
                        pe.matmul(QK[j][:, :], hs[p], wqkv[:, j * INNER:(j + 1) * INNER],
                                  start=True, stop=True).then_inc(s_qk, 1)
                if live(s, 2):
                    pe.wait_ge(s_qkn, done(s, 2))
                    bk = take(uses, "qT")
                    for j in range(4):
                        last = pe.transpose(bk[:, j * P:(j + 1) * P], qkn[:, j * P:(j + 1) * P], ident)
                    last.then_inc(s_T, 1)
                    if live(s, 3):
                        add_masks(s)
                    bk = take(uses, "kT")
                    for j in range(4):
                        last = pe.transpose(bk[:, j * P:(j + 1) * P], qkn[:, INNER + j * P:INNER + (j + 1) * P], ident)
                    last.then_inc(s_T, 1)

                def prob_t(r):
                    bk = take(uses, f"pT{r}")
                    for j in range(4):
                        last = pe.transpose(bk[:, j * P:(j + 1) * P], prob[:, r, j, :], ident)
                    last.then_inc(s_T, 1)
                if live(s, 4):
                    if not live(s, 2):
                        pe.wait_ge(s_res, done(s, 5))
                    pe.wait_ge(s_oT, done(s, 4))
                    for j in range(4):
                        last = pe.matmul(WO, wo[:, j, :], oT[:, j, :], start=(j == 0), stop=(j == 3),
                                         skip_group_check=True)
                    last.then_inc(s_wo, 1)
                if live(s, 3):
                    pe.wait_ge(s_pn, 2 * done(s, 3) - 1)
                    prob_t(0)
                    pe.wait_ge(s_pn, 2 * done(s, 3))
                    prob_t(1)
                if c is not None:
                    norm_var(pe, n, c, 1)
                if live(s, 2):
                    if not live(s, 3):
                        pe.wait_ge(s_Tf, tb + uses["kT"][0] + 1)
                        add_masks(s)
                    for hb in range(4):
                        for w in range(2):
                            ka = K_SLOT[(p, 0)]
                            kb = K_SLOT[(p, 1)] if w else K_SLOT[(1 - p, 1)]
                            for r in range(2):
                                last = pe.matmul(
                                    SC[r][WIN * w:WIN * (w + 1), hb * P:(hb + 1) * P],
                                    qT[DH * r:DH * (r + 1), hb, WIN * w:WIN * (w + 1)],
                                    kT[DH * r:DH * (r + 1), hb, ka:kb + 1:kb - ka, :],
                                    start=False, stop=True, skip_group_check=True)
                    last.then_inc(s_sc, 1)
                if live(s, 1):
                    bk = take(uses, "v")
                    pe.matmul(bk[:, :], hs[1 - p], wqkv[:, 2 * INNER:3 * INNER],
                              start=True, stop=True).then_inc(s_T, 1)
                if live(s, 3):
                    pe.wait_ge(s_Tf, tb + uses["pT1"][0] + 1)
                    pe.wait_ge(s_vm, done(s, 3))
                    if past(s, 4):
                        pe.wait_ge(s_oT, done(s, 4))
                    q = 1 - p
                    for j in range(4):
                        for w, vv in ((0, vmix[q]), (1, v[q])):
                            for r in range(2):
                                last = pe.matmul(OB[DH * r:DH * (r + 1), j * P + WIN * w:j * P + WIN * (w + 1)],
                                                 vv[:, 2 * j + r, :], pT[:, r, j, WIN * w:WIN * (w + 1)],
                                                 start=True, stop=True, skip_group_check=True)
                    last.then_inc(s_pv, 1)
            steps(pe, step)

        def attention_act(act, lx, n):
            base, tb = lx * TILES, t_base(lx)

            def done(s, lag):
                return base + s - lag + 1

            def empty(uses, name, dst, pattern, **sizes):
                n, b = uses[name]
                act.wait_ge(s_T, tb + n + 1)
                act.activation(dst, TB[b][:, :].rearrange(pattern, **sizes), ACT.Copy).then_inc(s_Tf, 1)

            def step(s, p):
                uses = t_uses(s, p)
                if live(s, 4):
                    act.wait_ge(s_pv, done(s, 4))
                    act.activation(oT, OB[:, :].rearrange("p (j c) -> p j c", j=4), ACT.Copy).then_inc(s_oT, 1)
                if tail_chunk(s) is not None:
                    norm_square(act, n, tail_chunk(s), 1, y, 0)
                if live(s, 2):
                    empty(uses, "qT", qT, "p (j c) -> p j c", j=4)
                    a, c = K_SLOT[(p, 0)], K_SLOT[(p, 1)]
                    empty(uses, "kT", kT[:, :, a:c + 1:c - a, :], "p (j h c) -> p j h c", j=4, h=2)
                if live(s, 3):
                    for r in range(2):
                        empty(uses, f"pT{r}", pT[:, r, :, :], "p (j c) -> p j c", j=4)
                if live(s, 0):
                    if past(s, 2):
                        act.wait_ge(s_ss, done(s, 2))
                    for j in range(2):
                        act.wait_ge(s_t12, 2 * (base + s) + j + 1)
                        last = act.activation(sq[p][:, j * INNER:(j + 1) * INNER], QK[j][:, :], ACT.Square)
                    last.then_inc(s_sq, 1)
                if live(s, 2):
                    act.wait_ge(s_mx, done(s, 2))
                    for r in range(2):
                        for j in range(4):
                            last = act.activation(prob[:, r, j, :], SC[r][:, j * P:(j + 1) * P], ACT.Exp,
                                                  bias=mx[:, 4 * r + j:4 * r + j + 1],
                                                  accum_out=esum[:, 4 * r + j:4 * r + j + 1])
                    last.then_inc(s_exp, 1)
                if live(s, 1):
                    if past(s, 3):
                        act.wait_ge(s_pv, done(s, 3))
                    if past(s, 2):
                        act.wait_ge(s_vm, done(s, 2))
                    empty(uses, "v", v[1 - p][:, :, :], "p (h c) -> p h c", h=H)
            steps(act, step)

        def attention_dve(dve, lx, l, n):
            base, tb = lx * TILES, t_base(lx)

            def done(s, lag):
                return base + s - lag + 1

            def stage(s, p):
                if past(s, 2):
                    dve.wait_ge(s_T, tb + t_before(s))
                dve.tensor_tensor(hs[p][64:128, 0:1], xa[64:128, bass.ds(s * P, 1)],
                                  flag[64:128, bass.ds(s, 1)], ALU.mult)
                dve.tensor_copy(hs[p][0:64, :], xa[0:64, bass.ds(s * P + 1, P)])
                dve.tensor_copy(hs[p][64:128, 1:P], xa[64:128, bass.ds(s * P + 1, P - 1)]).then_inc(s_hs, 1)

            def shift(c):
                norm_shift(dve, n, n - lx, c, xb, (s_res, base + (c + 1) * (CHUNK // P)))

            def step(s, p):
                c = tail_chunk(s)
                if c == 0:
                    shift(0)
                if live(s, 0):
                    stage(s, p)
                if live(s, 1):
                    dve.wait_ge(s_sq, done(s, 1))
                    dve.tensor_reduce(ssum[:, :], sq[1 - p].rearrange("p (h d) -> p h d", d=DH), AX.X,
                                      ALU.add).then_inc(s_ss, 1)
                if tail_chunk(s, 1) is not None:
                    if tail_chunk(s, 1) == 0:
                        dve.wait_ge(s_wf, (lx + 1) * (16 * (FB + 2)))
                    norm_scale(dve, n, tail_chunk(s, 1), 1, y, 0, ln)
                if live(s, 3):
                    dve.wait_ge(s_exp, done(s, 3))
                    dve.reciprocal(rsum[:, :], esum[:, :]).then_inc(s_rs, 1)
                    dve.wait_ge(s_rs, done(s, 3))
                    for r in range(2):
                        dve.tensor_tensor(prob[:, r, :, :], prob[:, r, :, :],
                                          bc(rsum[:, 4 * r:4 * r + 4].unsqueeze(2), (P, 4, P)),
                                          ALU.mult).then_inc(s_pn, 1)
                if live(s, 2):
                    dve.wait_ge(s_Tf, tb + t_before(s))
                    dve.tensor_copy(vmix[p][0:64, :, :], v[p][0:64, :, :])
                    dve.tensor_copy(vmix[p][64:128, :, :], v[1 - p][64:128, :, :]).then_inc(s_vm, 1)
                if live(s, 0):
                    if past(s, 2):
                        dve.wait_ge(s_qkn, done(s, 2))
                    row = l * TILES + s
                    ta = rot_a.rearrange("p l t a d -> p (l t) a d")[:, bass.ds(row, 1), :, :]
                    tbb = rot_b.rearrange("p l t a d -> p (l t) a d")[:, bass.ds(row, 1), :, :]
                    for j in range(2):
                        dve.wait_ge(s_qk, 2 * (base + s) + j + 1)
                        src = QK[j][:, :].rearrange("p (h d) -> p h d", h=H)
                        o1 = t1[p][:, j * INNER:(j + 1) * INNER].rearrange("p (h d) -> p h d", h=H)
                        o2 = t2[p][:, j * INNER:(j + 1) * INNER].rearrange("p (h d) -> p h d", h=H)
                        dve.tensor_tensor(o1, src, bc(ta[:, :, j, :], (P, H, DH)), ALU.mult)
                        dve.tensor_tensor(o2[:, :, 0:32], src[:, :, 32:64], bc(tbb[:, :, j, 0:32], (P, H, 32)),
                                          ALU.mult)
                        dve.tensor_tensor(o2[:, :, 32:64], src[:, :, 0:32], bc(tbb[:, :, j, 32:64], (P, H, 32)),
                                          ALU.mult).then_inc(s_t12, 1)
                        if j == 0 and live(s, 1):
                            clip(s)
                elif live(s, 1):
                    clip(s)
                if c is not None:
                    norm_vare(dve, n, c, 1)
                if live(s, 4):
                    dve.wait_ge(s_wo, done(s, 4))
                    t = s - 4
                    dve.tensor_tensor(xb[:, bass.ds(t * P + 1, P)], xa[:, bass.ds(t * P + 1, P)], WO,
                                      ALU.add).then_inc(s_res, 1)
                if live(s, 2):
                    dve.wait_ge(s_sc, done(s, 2))
                    if past(s, 3):
                        dve.wait_ge(s_exp, done(s, 3))
                    for r in range(2):
                        last = dve.tensor_reduce(mx[:, 4 * r:4 * r + 4], SC[r][:, :].rearrange("p (h d) -> p h d", d=P),
                                                 AX.X, ALU.max, negate=True)
                    last.then_inc(s_mx, 1)
                if c is not None:
                    norm_diag(dve, n, c)
                    if c < CHUNKS - 2:
                        shift(c + 1)
                if isinstance(s, int) and s == TILES + 3:
                    shift(CHUNKS - 1)

            def clip(s):
                dve.wait_ge(s_ss, done(s, 1))
                if past(s, 2):
                    dve.wait_ge(s_rn, done(s, 2))
                dve.tensor_scalar(smax[:, :], ssum[:, :], 1e-24, None, ALU.max).then_inc(s_ssm, 1)
            steps(dve, step)

        def attention_pool(pool, lx, n):
            base, tb = lx * TILES, t_base(lx)

            def done(s, lag):
                return base + s - lag + 1

            def step(s, p):
                if live(s, 1):
                    if past(s, 2):
                        pool.wait_ge(s_qkn, done(s, 2))
                    pool.wait_ge(s_ssm, done(s, 1))
                    pool.tensor_tensor(rn[:, :], smax[:, :], exp_half[:, :], ALU.pow).then_inc(s_rn, 1)
                    pool.wait_ge(s_rn, done(s, 1))
                    pool.wait_ge(s_add, done(s, 1))
                    if live(s, 2):
                        pool.wait_ge(s_T, tb + t_uses(s, p)["kT"][0] + 1)
                    pool.tensor_tensor(qkn.rearrange("p (h d) -> p h d", d=DH),
                                       t1[1 - p].rearrange("p (h d) -> p h d", d=DH),
                                       bc(rn[:, :].unsqueeze(2), (P, 2 * H, DH)), ALU.mult).then_inc(s_qkn, 1)
                if live(s, 0):
                    pool.wait_ge(s_t12, 2 * done(s, 0))
                    pool.tensor_tensor(t1[p], t1[p], t2[p], ALU.add).then_inc(s_add, 1)
                if tail_chunk(s) is not None:
                    norm_pow(pool, n, tail_chunk(s))
            steps(pool, step)

        FB = len(HB)

        LAST = CHUNKS - 1

        def up(u):
            return bank[2 + 2 * (u % 2)], bank[3 + 2 * (u % 2)]

        def ffn_pe(pe, lx, n, m):
            pe.wait_ge(s_wf, (lx + 1) * (16 * (FB + 2)))
            pe.wait_ge(s_exp, (lx + 1) * TILES)
            pe.wait_ge(s_Tf, t_base(lx + 1))
            pe.wait_ge(s_res, (lx + 1) * TILES)
            norm_center(pe, n, LAST, 1, hsh[:, LAST % 2, :], (s_hsh, (lx + 1) * CHUNKS))
            kb = lx * (CHUNKS * FB)

            def down(u):
                c, f = divmod(u, FB)
                _, w = HB[f]
                if f == 0:
                    if c > 1:
                        pe.wait_ge(s_xa, xa_count(lx, m) + c - 1)
                pe.wait_ge(s_hid, kb + u + 1)
                last = pe.matmul(bank[6 + c % 2][:, :], w2[0:w, f, :], hid[0:w, u % 2, :],
                                 start=(f == 0), stop=(f == FB - 1))
                last.then_inc(s_down, 1)
            for u in range(CHUNKS * FB):
                c, f = divmod(u, FB)
                at, w = HB[f]
                if f == 0:
                    pe.wait_ge(s_y, n * CHUNKS + c + 1)
                if u > 1:
                    pe.wait_ge(s_hid, kb + u - 1)
                for g in range(2):
                    last = pe.matmul(up(u)[g][0:w, :], w1[:, g * HID + at:g * HID + at + w],
                                     y[:, c * CHUNK:(c + 1) * CHUNK], start=True, stop=True)
                last.then_inc(s_ag, 1)
                if u == 0:
                    norm_var(pe, n, LAST, 1)
                if u:
                    down(u - 1)
                if u == 1:
                    norm_spread(pe, n, LAST, 1)
            down(CHUNKS * FB - 1)

        def ffn_act(act, lx, n):
            kb = lx * (CHUNKS * FB)
            norm_square(act, n, LAST, 1, y, 0)
            for u in range(CHUNKS * FB):
                c, f = divmod(u, FB)
                _, w = HB[f]
                act.wait_ge(s_ag, kb + u + 1)
                if u > 1:
                    act.wait_ge(s_hid, kb + u - 1)
                act.activation(gel[0:w, u % 2, :], up(u)[1][0:w, :], ACT.Gelu,
                               bias=par[0:w, 7 + f:8 + f]).then_inc(s_gel, 1)

        def ffn_dve(dve, lx, n, m):
            kb = lx * (CHUNKS * FB)
            norm_vare(dve, n, LAST, 1)

            def finish(c):
                dve.wait_ge(s_down, kb + (c + 1) * FB)
                sl = slice(1 + c * CHUNK, 1 + (c + 1) * CHUNK)
                dve.scalar_tensor_tensor(out=xa[:, sl], in0=bank[6 + c % 2][:, :], scalar=par[:, 2:3],
                                         in1=xb[:, sl], op0=ALU.add, op1=ALU.add).then_inc(s_xa, 1)
            for u in range(CHUNKS * FB):
                c, f = divmod(u, FB)
                _, w = HB[f]
                dve.wait_ge(s_gel, kb + u + 1)
                if u > 1:
                    dve.wait_ge(s_down, kb + u - 1)
                dve.scalar_tensor_tensor(out=hid[0:w, u % 2, :], in0=up(u)[0][0:w, :],
                                         scalar=par[0:w, 4 + f:5 + f], in1=gel[0:w, u % 2, :],
                                         op0=ALU.add, op1=ALU.mult).then_inc(s_hid, 1)
                if m == 0:
                    for i in range(2 * u, min(2 * u + 2, POWER_STEPS)):
                        power_step(dve, lx, i)
                if u == 0:
                    norm_diag(dve, n, LAST)
                if u == 1:
                    norm_scale(dve, n, LAST, 1, y, 0, ln)
                if f == 0 and c:
                    finish(c - 1)
            finish(CHUNKS - 1)

        def power_step(dve, lx, i):
            if i:
                dve.wait_ge(s_pw, lx * POWER_STEPS + i)
            gt = lambda ap: ap.rearrange("p (g t) -> p g t", g=GR)
            spread = lambda j: bc(sm[:, j, :].unsqueeze(2), (P, GR, NTV))
            tvb = bc(tv.unsqueeze(1), (P, GR, NTV))
            if i < 2:
                last = dve.tensor_tensor(sm[:, 1 + i, :], sm[:, 0, :], prm[:, 1 + i, :], ALU.mult)
            elif i < 4:
                if i == 2:
                    dve.wait_ge(s_qkn, (lx + 1) * TILES)
                last = dve.tensor_tensor(gt((grow, ph)[i - 2]), spread(i - 1), tvb, ALU.mult)
            else:
                turn, j = divmod(i - 4, 8)
                r = w_t[:, 1 - turn, :, :].rearrange("p g t -> p (g t)")
                quarter = 0.25 * turn
                if j == 0:
                    last = dve.tensor_scalar(kk, ph, 1 / (2 * np.pi), quarter, ALU.mult, ALU.add)
                elif j == 1:
                    last = dve.tensor_scalar(kk, kk, MAGIC, None, ALU.add)
                elif j == 2:
                    last = dve.tensor_scalar(kk, kk, -MAGIC, None, ALU.add)
                elif j < 6:
                    last = dve.scalar_tensor_tensor(out=r, in0=kk, scalar=-(PI_A, PI_B, PI_C)[j - 3],
                                                    in1=ph if j == 3 else r, op0=ALU.mult, op1=ALU.add)
                elif j == 6:
                    last = dve.tensor_scalar(r, r, 2 * np.pi * quarter, PI_IN, ALU.add, ALU.min)
                else:
                    last = dve.tensor_scalar(r, r, -PI_IN, None, ALU.max)
            last.then_inc(s_pw, 1)

        def layer_norm_index(m, l):
            return 4 * m + 1 + l

        def outer(m):
            return 4 * m

        def main_ready(m):
            return lambda c: (s_x[c], 16) if m == 0 else (s_mix, c + 1)

        def masks_dve(dve):
            dve.wait_ge(s_rawm, 16)
            dve.tensor_copy(ident_bf[:, :], ident)
            for t in range(0, TILES, SEQ_TILES):
                dve.tensor_copy(masks[:, t, :], raw_m[:, 0, :])
                last = dve.tensor_copy(masks[:, t + 1:t + SEQ_TILES, :], bc(raw_m[:, 1:2, :], (P, SEQ_TILES - 1, P)))
            last.then_inc(s_mask, 1)

        def rotary(eng, m, part):
            eng.wait_ge(s_raw, 48 * (m + 1))
            l, half = divmod(part, B)
            t = slice(half * SEQ_TILES, (half + 1) * SEQ_TILES)
            for tab, raw, to, fro in ((rot_a, raw_c, slice(0, DH), slice(0, DH)),
                                      (rot_b, raw_s, slice(0, 32), slice(32, 64)),
                                      (rot_b, raw_s, slice(32, 64), slice(0, 32))):
                last = eng.tensor_tensor(tab[:, l, t, :, to], raw[:, :, :, to],
                                          bc(qks[:, l, :, fro].unsqueeze(1), (P, SEQ_TILES, 2, to.stop - to.start)),
                                         ALU.mult)
            last.then_inc(s_rot, 1)

        def macaron_pe(pe, m):
            norm_pe(pe, outer(m), x_main, main_ready(m))
            if m == 0:
                pe.wait_ge(s_mask, 1)
            with pe.Fori(0, DEPTH) as l:
                lx = l + DEPTH * m
                attention_pe(pe, lx, layer_norm_index(m, l))
                ffn_pe(pe, lx, layer_norm_index(m, l), m)

        def macaron_act(act, m):
            norm_act(act, outer(m), xa, 1)
            if m == 0:
                act.wait_ge(s_mc, 16 * MIX_LOADS)
                act.activation(sm[:, 0, :], prm[:, 0, :], ACT.Exp).then_inc(s_dt, 1)
            with act.Fori(0, DEPTH) as l:
                lx = l + DEPTH * m
                attention_act(act, lx, layer_norm_index(m, l))
                ffn_act(act, lx, layer_norm_index(m, l))

        def macaron_dve(dve, m):
            def beside(k):
                if k > 1:
                    rotary(dve, m, k)
                elif k == 0 == m:
                    masks_dve(dve)
            norm_dve(dve, outer(m), xa, 1, None, beside)
            dve.wait_ge(s_rot, CHUNKS * (m + 1))
            if m == 0:
                dve.wait_ge(s_mc, 16 * MIX_LOADS)
                dve.wait_ge(s_dt, 1)
            with dve.Fori(0, DEPTH) as l:
                lx = l + DEPTH * m
                dve.wait_ge(s_y, layer_norm_index(m, l) * CHUNKS)
                attention_dve(dve, lx, l, layer_norm_index(m, l))
                ffn_dve(dve, lx, layer_norm_index(m, l), m)
            for c in range(CHUNKS):
                dve.wait_ge(s_xa, xa_count(DEPTH * (m + 1) - 1, m) + c + 1)
                xm = x_main[:, c * CHUNK:(c + 1) * CHUNK]
                dve.scalar_tensor_tensor(out=xm, in0=xa[:, 1 + c * CHUNK:1 + (c + 1) * CHUNK], scalar=0.5, in1=xm,
                                         op0=ALU.mult, op1=ALU.add).then_inc(s_mac, 1)

        def macaron_pool(pool, m):
            norm_pool(pool, outer(m), lambda c: rotary(pool, m, c - 1) if 0 < c < 3 else None)
            with pool.Fori(0, DEPTH) as l:
                lx = l + DEPTH * m
                pool.wait_ge(s_y, layer_norm_index(m, l) * CHUNKS)
                pool.wait_ge(s_xa, xa_count(lx, m))
                attention_pool(pool, lx, layer_norm_index(m, l))
                norm_pow(pool, layer_norm_index(m, l), LAST)

        NMIX = outer(0) + 3

        def outer_product(eng, link, out, scratch, a_, g0, groups, imag):
            shape = (P, groups, 8, 16)
            o4 = out.rearrange("p g (a b) -> p g a b", b=16)
            t4 = scratch[:, 0:groups * P].rearrange("p (g a b) -> p g a b", g=groups, b=16)
            left = lambda c: bc(a_[:, c, g0:g0 + groups, :].unsqueeze(3), shape)
            right = lambda c: bc(w_t[:, c, g0:g0 + groups, 0:16].unsqueeze(2), shape)
            eng.tensor_tensor(o4, left(0), right(1 if imag else 0), ALU.mult)
            link(eng.tensor_tensor(t4, left(1), right(0 if imag else 1), ALU.mult))
            return eng.tensor_tensor(o4, o4, t4, ALU.add if imag else ALU.subtract)

        def mixer_pe(pe):
            pe.wait_ge(s_mc, 16 * MIX_LOADS)
            norm_pe(pe, NMIX, x_main, lambda c: (s_mac, CHUNKS))
            pe.wait_ge(s_ipk, 1)
            pe.wait_ge(s_csb, (NMIX + 1) * CHUNKS)

            def x_to_tokens(n):
                blk, c = divmod(n, CHUNKS)
                pe.wait_ge(s_silu, n + 1)
                if n > 1:
                    pe.wait_ge(s_xe, n - 1)
                for j in range(4):
                    last = pe.transpose(bank[2 + n % 2][:, j * P:(j + 1) * P], xs[:, blk, 4 * c + j, :], ident)
                last.then_inc(s_xt, 1)

            def project_in(u):
                e, c = divmod(u, CHUNKS)
                if e == 0:
                    pe.wait_ge(s_y, NMIX * CHUNKS + c + 1)
                if u > 1:
                    pe.wait_ge(s_silu, u - 1)
                bk = bank[u % 2]
                at = 1 + c * CHUNK
                if e < 2:
                    for k in range(4):
                        cut = k if c % 2 == 0 else 0
                        last = pe.matmul(bk[:, cut:CHUNK], ipk[:, 3 - k, e * P:(e + 1) * P],
                                         xa[:, at + cut - k:at + CHUNK - k], start=(k == 0), stop=(k == 3),
                                         skip_group_check=True)
                else:
                    last = pe.matmul(bk[:, :], ipw[:, e * P:(e + 1) * P], xa[:, at:at + CHUNK],
                                     start=True, stop=True)
                last.then_inc(s_in, 1)
            for u in range(2 * CHUNKS):
                project_in(u)
                if u == 1:
                    pe.wait_ge(s_y, (NMIX + 1) * CHUNKS)
                    pe.wait_ge(s_xz, 1)
                if u:
                    x_to_tokens(u - 1)
            x_to_tokens(2 * CHUNKS - 1)
            pe.wait_ge(s_g, 1)
            for g in range(GR):
                half, j = divmod(g, P // GC)
                last = pe.matmul(bank[7][:, half * P:(half + 1) * P], sel[:, P - GC - GC * j:2 * P - GC - GC * j],
                                 g_t[:, 0, g, :], start=(j == 0), stop=(j == P // GC - 1), skip_group_check=True)
            last.then_inc(s_kk, 1)
            pe.wait_ge(s_xe, 2 * CHUNKS)
            for i, (c, ready) in enumerate(((1, s_rowp), (0, s_row))):
                pe.wait_ge(ready, 1)
                for k in range(GR // 4):
                    n = i * (GR // 4) + k
                    if n > 3:
                        pe.wait_ge(s_ve, n - 3)
                    for j in range(4):
                        last = pe.transpose(bank[n % 4][:, j * P:(j + 1) * P], v_t[:, c, 4 * k + j, :], ident)
                    last.then_inc(s_vt, 1)
            pe.wait_ge(s_ve, 2 * (GR // 4))
            pe.wait_ge(s_xe, 2 * CHUNKS)
            for q in range(GR // 4):
                for c in range(2):
                    n = 2 * q + c
                    if n > 1:
                        pe.wait_ge(s_um, n - 1)
                    for j in range(4):
                        g = 4 * q + j
                        last = pe.matmul(bank[4 + n % 2][:, j * P:(j + 1) * P], v_t[:, c, g, :],
                                         x_tok[:, g * GC // 2:(g + 1) * GC // 2, 0:4:3, :],
                                         start=True, stop=True, skip_group_check=True)
                    last.then_inc(s_u, 1)
                    if c:
                        project_in(2 * CHUNKS + q)
            pe.wait_ge(s_xz, 1)
            pe.wait_ge(s_g1, 1)

            def to_tokens(q):
                pe.wait_ge(s_ye, q + 1)
                if q > 1:
                    pe.wait_ge(s_yl, q - 1)
                for j in range(4):
                    last = pe.transpose(bank[2 + q % 2][:, j * P:(j + 1) * P], tmp[:, q % 2, j * P:(j + 1) * P], ident)
                last.then_inc(s_yk, 1)
            def own_tile(q):
                for j in range(4):
                    g = 4 * q + j
                    if j == 0 and q > 3:
                        pe.wait_ge(s_ye, q - 3)
                    pe.wait_ge(s_toep[g % TRING], 16 * (g // TRING + 1))
                    for a in range(2):
                        for u in range(GC // 2):
                            last = pe.matmul(bank[4 + q % 4][32 * u:32 * (u + 1), j * P:(j + 1) * P],
                                             x_tok[:, g * GC // 2 + u, 2 * a:2 * a + 2, :].rearrange("p a t -> p (a t)"),
                                             toep[g % TRING][:, 2 * u + a, :],
                                             start=(j == a == 0), stop=False, skip_group_check=True)
                    last.then_inc(s_tg, 1)
            pe.wait_ge(s_um, 2 * (GR // 4))
            pe.wait_ge(s_kp, 1)
            for q in range(AHEAD):
                own_tile(q)
            for q in range(GR // 4):
                pe.wait_ge(s_r, 2 * q + 2)
                for j in range(4):
                    for c in range(2):
                        last = pe.matmul(bank[4 + q % 4][:, j * P:(j + 1) * P],
                                         rbd[:, q % 2, c, j, :, :].rearrange("p h t -> p (h t)"),
                                         g_t[:, c, 4 * q + j, :], start=False, stop=(c == 1), skip_group_check=True)
                last.then_inc(s_yg, 1)
                if q + AHEAD < GR // 4:
                    own_tile(q + AHEAD)
                if q:
                    to_tokens(q - 1)
            to_tokens(GR // 4 - 1)
            pe.wait_ge(s_yl, GR // 4)
            pe.wait_ge(s_ye, GR // 4)

            def project(c):
                pe.wait_ge(s_yz, 2 * c + 2)
                if c > 1:
                    pe.wait_ge(s_mix, c - 1)
                for blk in range(2):
                    last = pe.matmul(bank[4 + c % 2][:, :], opw[:, blk, :], yz[:, 2 * (c % 2) + blk, :],
                                     start=(blk == 0), stop=(blk == 1))
                last.then_inc(s_op, 1)
            for c in range(CHUNKS):
                for blk in range(2):
                    n = 2 * c + blk
                    if n > 1:
                        pe.wait_ge(s_yz, n - 1)
                    for j in range(4):
                        last = pe.transpose(bank[n % 2][:, j * P:(j + 1) * P],
                                            ysb[:, blk * P:(blk + 1) * P, 4 * c + j], ident)
                    last.then_inc(s_yt, 1)
                if c:
                    project(c - 1)
            project(CHUNKS - 1)

        def mixer_act(act):
            wf = w_t.rearrange("p c g t -> p c (g t)")
            act.wait_ge(s_pw, DEPTH * POWER_STEPS)
            act.activation(grow, grow, ACT.Exp).then_inc(s_mag, 1)
            for c in range(2):
                act.activation(wf[:, c, :], wf[:, c, :], ACT.Sin).then_inc(s_trig, 1)
            norm_act(act, NMIX, xa, 1)

            def silu(u):
                e, c = divmod(u, CHUNKS)
                act.wait_ge(s_in, u + 1)
                if e < 2:
                    act.activation(xs[:, e, 4 * c:4 * c + 4, ::-1], bank[u % 2][:, :].rearrange("p (t i) -> p t i", i=P),
                                   ACT.Silu, bias=chp[:, e:e + 1]).then_inc(s_silu, 1)
                else:
                    act.activation(zs[e - 2][:, c * CHUNK:(c + 1) * CHUNK], bank[u % 2][:, :],
                                   ACT.Silu).then_inc(s_silu, 1)

            def x_to_tokens(n):
                blk, c = divmod(n, CHUNKS)
                act.wait_ge(s_xt, n + 1)
                for a in range(2):
                    last = act.activation(
                        x_tok[:, blk * P // 2:(blk + 1) * P // 2, 3 * a, 4 * c:4 * c + 4].rearrange("p u t -> p t u"),
                        bank[2 + n % 2][:, :].rearrange("p (t u a) -> p t u a", t=4, a=2)[:, :, :, a], ACT.Copy)
                last.then_inc(s_xe, 1)
            for u in range(2 * CHUNKS):
                silu(u)
                if u:
                    x_to_tokens(u - 1)
            x_to_tokens(2 * CHUNKS - 1)
            for n in range(2 * (GR // 4)):
                c, k = 1 - n // (GR // 4), n % (GR // 4)
                act.wait_ge(s_vt, n + 1)
                act.activation(v_t[:, c, 4 * k:4 * k + 4, :].rearrange("p g t -> p (g t)"), bank[n % 4][:, :],
                               ACT.Copy).then_inc(s_ve, 1)
            for u in range(2 * CHUNKS, 4 * CHUNKS):
                silu(u)

            def to_tokens(q):
                act.wait_ge(s_yk, q + 1)
                act.activation(ysb[:, 4 * q * GC:4 * (q + 1) * GC, :].rearrange("p h t -> p (h t)"),
                               bank[2 + q % 2][:, :], ACT.Copy).then_inc(s_yl, 1)
            for q in range(GR // 4):
                act.wait_ge(s_yg, q + 1)
                act.activation(tmp[:, q % 2, :], bank[4 + q % 4][:, :], ACT.Copy).then_inc(s_ye, 1)
                if q:
                    to_tokens(q - 1)
            to_tokens(GR // 4 - 1)

        def mixer_dve(dve):
            linked = [0]

            def link(ins):
                linked[0] += 1
                ins.then_inc(s_link, 1)
                dve.wait_ge(s_link, linked[0])
            dve.wait_ge(s_pw, DEPTH * POWER_STEPS)
            a_re, a_im, c_re, c_im = (prm[:, i, :] for i in range(1, 5))
            s_ = lambda i: sm[:, i, :]
            tt = dve.tensor_tensor

            def tables(part):
                if part == 0:
                    tt(ipk, cw, bc(ipw[:, 0:DIN].unsqueeze(1), (P, 4, DIN)), ALU.mult).then_inc(s_ipk, 1)
                    dve.wait_ge(s_ipk, 1)
                    dve.wait_ge(s_mag, 1)
                    dve.wait_ge(s_trig, 2)
                    wf = w_t.rearrange("p c g t -> p c (g t)")
                    link(tt(wf, wf, bc(grow.unsqueeze(1), (P, 2, GR * NTV)), ALU.mult))
                    dve.sem_inc(s_w, 1)
                elif part == 1:
                    w1r, w1i = w_t[:, 0, :, 1], w_t[:, 1, :, 1]
                    tt(s_(3), a_re, a_re, ALU.mult)
                    link(tt(s_(4), a_im, a_im, ALU.mult))
                    link(tt(s_(3), s_(3), s_(4), ALU.add))
                    link(dve.reciprocal(s_(3), s_(3)))
                    link(dve.tensor_scalar(s_(4), w1r, -1.0, None, ALU.add))
                    tt(s_(5), s_(4), a_re, ALU.mult)
                    tt(s_(6), w1i, a_im, ALU.mult)
                    tt(s_(7), w1i, a_re, ALU.mult)
                    link(tt(s_(8), s_(4), a_im, ALU.mult))
                    tt(s_(5), s_(5), s_(6), ALU.add)
                    link(tt(s_(7), s_(7), s_(8), ALU.subtract))
                    tt(s_(5), s_(5), s_(3), ALU.mult)
                    link(tt(s_(7), s_(7), s_(3), ALU.mult))
                    tt(s_(6), c_re, s_(5), ALU.mult)
                    tt(s_(8), c_im, s_(7), ALU.mult)
                    tt(s_(9), c_re, s_(7), ALU.mult)
                    link(tt(s_(10), c_im, s_(5), ALU.mult))
                    tt(s_(6), s_(6), s_(8), ALU.subtract)
                    link(tt(s_(9), s_(9), s_(10), ALU.add))
                    dve.tensor_scalar(s_(6), s_(6), 2.0, None, ALU.mult)
                    link(dve.tensor_scalar(s_(9), s_(9), 2.0, None, ALU.mult))
                elif part == 2:
                    war, wai = w_t[:, 0, :, 16:24], w_t[:, 1, :, 16:24]
                    b8 = lambda i: bc(s_(i).unsqueeze(2), (P, GR, 8))
                    x8 = [pre[:, i * GR * 8:(i + 1) * GR * 8].rearrange("p (g a) -> p g a", g=GR) for i in range(2)]
                    tt(ca[:, 0, :, :], b8(6), war, ALU.mult)
                    tt(x8[0], b8(9), wai, ALU.mult)
                    tt(ca[:, 1, :, :], b8(6), wai, ALU.mult)
                    link(tt(x8[1], b8(9), war, ALU.mult))
                    tt(ca[:, 0, :, :], ca[:, 0, :, :], x8[0], ALU.subtract)
                    link(tt(ca[:, 1, :, :], ca[:, 1, :, :], x8[1], ALU.add))
                    dve.tensor_scalar(nca.rearrange("p c g a -> p (c g a)"), ca.rearrange("p c g a -> p (c g a)"),
                                      -1.0, None, ALU.mult).then_inc(s_nca, 1)
            norm_dve(dve, NMIX, xa, 1, None, tables)
            dve.wait_ge(s_nca, 1)
            outer_product(dve, link, g_t[:, 0, :, :], pre, ca, 0, GR, False).then_inc(s_g, 1)
            dve.wait_ge(s_g, 1)
            outer_product(dve, link, v_t[:, 0, :, :], pre, w_t[:, :, :, 24:32], 0, GR, False).then_inc(s_row, 1)
            dve.wait_ge(s_kk, 1)
            link(dve.memset(kp, 0.0))
            link(dve.tensor_copy(kp[:, :, P - 1:2 * P - 1], bank[7][:, 0:2 * P].rearrange("p (a t) -> p a t", a=2)))
            tt(kp[:, :, P - 1:P], kp[:, :, P - 1:P], chp[:, 2:4].unsqueeze(2), ALU.add).then_inc(s_kp, 1)
            for n in range(2 * (GR // 4)):
                q, c = divmod(n, 2)
                dve.wait_ge(s_u, n + 1)
                if n > 1:
                    dve.wait_ge(s_ur, n - 1)
                t4 = tmp[:, n % 2, :].rearrange("p (g h t) -> p g h t", g=4, h=GC)
                tt(t4, bank[4 + n % 2][:, :].rearrange("p (g h t) -> p g h t", g=4, h=GC),
                   bc(blockd.unsqueeze(1).unsqueeze(3), (P, 4, GC, TILES)), ALU.mult).then_inc(s_um, 1)
                dve.wait_ge(s_um, n + 1)
                dve.tensor_reduce(ust[:, c, 4 * q:4 * q + 4, :], t4.rearrange("p g h t -> p g t h"), AX.X,
                                  ALU.add).then_inc(s_ur, 1)
            dve.wait_ge(s_ur, 2 * (GR // 4))
            u5 = ust.rearrange("p c g (b j) -> p c g b j", b=B)
            wr = bc(w_t[:, 0, :, NTV - 1].unsqueeze(1).unsqueeze(3), (P, 2, GR, B))
            wi = bc(w_t[:, 1, :, NTV - 1].unsqueeze(2), (P, GR, B))
            pa = tmp[:, 0, 0:2 * GR * B].rearrange("p (c g b) -> p c g b", c=2, g=GR)
            pb = tmp[:, 1, 0:2 * GR * B].rearrange("p (c g b) -> p c g b", c=2, g=GR)
            for j in range(1, SEQ_TILES):
                tt(pa, u5[:, :, :, :, j - 1], wr, ALU.mult)
                tt(pb[:, 0], u5[:, 1, :, :, j - 1], wi, ALU.mult)
                link(tt(pb[:, 1], u5[:, 0, :, :, j - 1], wi, ALU.mult))
                link(tt(u5[:, :, :, :, j], u5[:, :, :, :, j], pa, ALU.add))
                tt(u5[:, 0, :, :, j], u5[:, 0, :, :, j], pb[:, 0], ALU.subtract)
                link(tt(u5[:, 1, :, :, j], u5[:, 1, :, :, j], pb[:, 1], ALU.add))
            s6 = sh.rearrange("p c g (b j) -> p (c g) b j", b=B)
            dve.memset(s6[:, :, :, 0:1], 0.0)
            link(dve.tensor_copy(s6[:, :, :, 1:SEQ_TILES],
                                 ust.rearrange("p c g (b j) -> p (c g) b j", b=B)[:, :, :, 0:SEQ_TILES - 1]))
            dve.wait_ge(s_g1, 1)
            dve.wait_ge(s_kd, 16)
            for q in range(GR // 4):
                if q > 1:
                    dve.wait_ge(s_yg, q - 1)
                for c in range(2):
                    tt(rbd[:, q % 2, c], bc(sh[:, c, 4 * q:4 * q + 4, :].unsqueeze(2), (P, 4, GC, TILES)),
                       bc(blockd.unsqueeze(1).unsqueeze(3), (P, 4, GC, TILES)), ALU.mult).then_inc(s_r, 1)

            def residual(c):
                dve.wait_ge(s_op, c + 1)
                xm = x_main[:, c * CHUNK:(c + 1) * CHUNK]
                tt(xm, xm, bank[4 + c % 2][:, :], ALU.add).then_inc(s_mix, 1)
            for n in range(2 * CHUNKS):
                c, blk = divmod(n, 2)
                dve.wait_ge(s_yt, n + 1)
                if blk == 0 and c > 1:
                    dve.wait_ge(s_op, c - 1)
                tt(yz[:, 2 * (c % 2) + blk, :], bank[n % 2][:, :], zs[blk][:, c * CHUNK:(c + 1) * CHUNK],
                   ALU.mult).then_inc(s_yz, 1)
                if blk and c:
                    residual(c - 1)
            residual(CHUNKS - 1)

        def mixer_pool(pool):
            linked = [0]

            def link(ins):
                linked[0] += 1
                ins.then_inc(s_plink, 1)
                pool.wait_ge(s_plink, linked[0])
            pool.wait_ge(s_mac, CHUNKS)
            pool.memset(x_tok[:, :, 1:3, :], 0.0).then_inc(s_xz, 1)
            norm_pool(pool, NMIX)
            pool.wait_ge(s_w, 1)
            for g in range(0, GR, GC):
                link(outer_product(pool, link, v_t[:, 1, g:g + GC, :], kscr, w_t[:, :, :, 24:32], g, GC, True))
            pool.sem_inc(s_rowp, 1)
            pool.wait_ge(s_nca, 1)
            pool.wait_ge(s_row, 1)
            for g in range(0, GR, GC):
                link(outer_product(pool, link, g_t[:, 1, g:g + GC, :], kscr, nca, g, GC, True))
            pool.sem_inc(s_g1, 1)

        def mixer_sync(sp):
            sp.wait_ge(s_kp, 1)
            sp.dma_start(kpad.rearrange("(a p) t -> p a t", p=P), kp).then_inc(s_kd, 16)
            sp.wait_ge(s_kd, 16)
            for g in range(GR):
                if g >= TRING:
                    sp.wait_ge(s_tg, g - TRING + 1)
                elif g % 2 == 0:
                    sp.wait_ge(s_u, 2 * g + 4)
                src = bass.AP(tensor=kpad.tensor, offset=kpad.offset + g * GC * 2 * P, ap=[[1, P], [2 * P, GC], [1, P]])
                sp.dma_start(toep[g % TRING], src).then_inc(s_toep[g % TRING], 16)

        block = ctx.enter_context(nc.Block())

        @block.sync
        def _(sp):
            sp.dma_start(consts[:, :], ins["consts"]).then_inc(s_const, 16)
            for c in range(CHUNKS):
                sp.dma_start(x_main[:, c * CHUNK:(c + 1) * CHUNK],
                             ins["x"][:, c * CHUNK:(c + 1) * CHUNK]).then_inc(s_x[c], 16)
            sp.dma_start(raw_m, ins["masks"]).then_inc(s_rawm, 16)
            def rotary_loads():
                sp.dma_start(raw_c, ins["rot_c"]).then_inc(s_raw, 16)
                sp.dma_start(raw_s, ins["rot_s"]).then_inc(s_raw, 16)
                sp.dma_start(qks, ins["qks"]).then_inc(s_raw, 16)
            rotary_loads()
            for lx in range(2 * DEPTH):
                l = lx % DEPTH
                if lx:
                    sp.wait_ge(s_wo, lx * TILES)
                sp.dma_start(wqkv[:, :], ins["wqkv"][l]).then_inc(s_wa, 16)
                sp.dma_start(wo[:, :, :], ins["wo"][l].rearrange("(j p) n -> p j n", p=P)).then_inc(s_wa, 16)
                if lx:
                    sp.wait_ge(s_xa, xa_count(lx, (lx - 1) // DEPTH))
                sp.dma_start(w1[:, :], ins["w1"][l]).then_inc(s_wf, 16)
                for f, (at, w) in enumerate(HB):
                    sp.dma_start(w2[0:w, f, :], ins["w2"][l][at:at + w, :]).then_inc(s_wf, 16)
                sp.dma_start(par[:, :], ins["par"][l]).then_inc(s_wf, 16)
                if lx == 0:
                    for dst, name in ((prm, "prm"), (tv, "tv"), (blockd, "blockd"), (sel, "sel"), (ipw, "ipw"),
                                      (opw, "opw"), (cw, "cw"), (chp, "chp")):
                        sp.dma_start(dst, ins[name]).then_inc(s_mc, 16)
                if lx == DEPTH:
                    mixer_sync(sp)
                    sp.wait_ge(s_tg, GR)
                    rotary_loads()
            for c in range(CHUNKS):
                sp.wait_ge(s_mac, CHUNKS + c + 1)
                sp.dma_start(out[:, c * CHUNK:(c + 1) * CHUNK], x_main[:, c * CHUNK:(c + 1) * CHUNK]).then_inc(s_out, 16)
            sp.wait_ge(s_out, 16 * CHUNKS)

        @block.gpsimd
        def _(pool):
            pool.memset(exp_half[:, :], -0.5).then_inc(s_init, 1)
            pool.memset(xa[:, 0:1], 0.0).then_inc(s_init, 1)
            pool.memset(xb[:, 0:1], 0.0).then_inc(s_init, 1)
            pool.memset(kT[:, :, :, :], 0.0).then_inc(s_init, 1)
            for i in range(2):
                pool.memset(v[i][:, :, :], 0.0).then_inc(s_init, 1)
                pool.memset(vmix[i][:, :, :], 0.0).then_inc(s_init, 1)
            pool.wait_ge(s_init, INITS)
            macaron_pool(pool, 0)
            mixer_pool(pool)
            macaron_pool(pool, 1)

        @block.scalar
        def _(act):
            act.wait_ge(s_init, INITS)
            macaron_act(act, 0)
            mixer_act(act)
            macaron_act(act, 1)

        @block.vector
        def _(dve):
            dve.wait_ge(s_const, 16)
            dve.wait_ge(s_init, INITS)
            macaron_dve(dve, 0)
            mixer_dve(dve)
            macaron_dve(dve, 1)

        @block.tensor
        def _(pe):
            pe.wait_ge(s_const, 16)
            macaron_pe(pe, 0)
            mixer_pe(pe)
            macaron_pe(pe, 1)


def shape_constants():
    consts = np.zeros((P, C_W), np.float32)
    consts[:, C_ID:C_ID + P] = np.eye(P)
    consts[:, C_CEN:C_CEN + P] = np.eye(P) - 1.0 / P
    consts[:, C_ONE:C_ONE + P] = 1.0
    flag = np.ones(TILES)
    flag[::SEQ_TILES] = 0
    consts[:, C_FLAG:] = flag
    i = np.arange(WIN)[:, None]
    j = np.arange(WIN)[None, :]
    own, older = i >= j, j >= i
    keep = np.zeros((2, P, P), bool)
    keep[:, 0:WIN, 0:WIN], keep[:, 0:WIN, WIN:] = own, older
    keep[:, WIN:, 0:WIN], keep[:, WIN:, WIN:] = older, own
    keep[0, 0:WIN, WIN:] = False
    masks = np.where(keep, 0.0, MASKED).transpose(1, 0, 2).astype(np.float32)
    half = np.arange(0, DH, 2, dtype=np.float32)
    inv = np.float32(1.0) / np.power(np.float32(10000.0), half / np.float32(DH)).astype(np.float32)
    t = np.arange(N, dtype=np.float32)
    fr = (t[:, None] * inv[None, :]).astype(np.float32).astype(np.float64)
    base = (half.astype(np.float64) + 0.4 * DH) / (1.4 * DH)
    sc = base[None, :] ** ((t - N // 2) / float(WIN // 2))[:, None].astype(np.float64)
    cos, sin = np.cos(fr), np.sin(fr)
    qk_scale = 8.0
    c = np.stack([np.tile(cos * sc, 2) * qk_scale, np.tile(cos / sc, 2)], 1)
    s = np.stack([np.concatenate([-sin * sc, sin * sc], 1) * qk_scale, np.concatenate([-sin / sc, sin / sc], 1)], 1)
    lay = lambda a: np.ascontiguousarray(a.astype(np.float32).reshape(SEQ_TILES, P, 2, DH).transpose(1, 0, 2, 3))
    blockd = (np.arange(P)[:, None] // NS == np.arange(GC)).astype(np.float32)
    sel = np.zeros((P, SEL), np.float32)
    sel[:, P - GC:P] = blockd
    tvs = np.ascontiguousarray(np.broadcast_to(np.array(TV, np.float32), (P, NTV)))
    return dict(blockd=blockd, sel=sel, tv=tvs, consts=consts, masks=np.ascontiguousarray(masks),
                rot_c=lay(c), rot_s=lay(s))


def kernel(**inputs):
    import concourse.bacc as bacc
    from concourse.bass_utils import run_bass_kernel_spmd

    a = {k.replace("L0_", ""): np.asarray(v) for k, v in inputs.items()}
    f32 = np.float32
    arrays = shape_constants()
    arrays["x"] = np.ascontiguousarray(a["attn_hidden_states"].reshape(T, D).T)
    arrays["wqkv"] = a["ffn_wqkv"]
    arrays["wo"] = a["ffn_wo"]
    arrays["w1"] = a["ffn_w1"]
    arrays["w2"] = a["ffn_w2"]
    qk = np.stack([a["ffn_q_scale"], a["ffn_k_scale"]], 1)
    arrays["qks"] = np.ascontiguousarray(np.broadcast_to(qk, (P, DEPTH, 2, DH)))
    pp = np.zeros((DEPTH, P, NPAR), f32)
    for l in range(DEPTH):
        pp[l, :, 0], pp[l, :, 1], pp[l, :, 2] = a["ffn_ln_g"][l], a["ffn_ln_b"][l], a["ffn_b2"][l]
        for g in range(2):
            for f, (at, w) in enumerate(HB):
                pp[l, :w, 4 + 3 * g + f] = a["ffn_b1"][l, g * HID + at:g * HID + at + w]
    arrays["par"] = pp

    rows = lambda z: z.reshape(GR, P).T
    arrays["prm"] = np.stack([rows(np.repeat(a["attn_log_dt"][:, None], NS, 1))]
                             + [rows(a["attn_" + k]) for k in ("A_re", "A_im", "C_re", "C_im")], 1)
    arrays["ipw"] = a["attn_in_proj_w"].T
    arrays["opw"] = a["attn_out_proj_w"].T.reshape(2, P, D).transpose(1, 0, 2)
    arrays["cw"] = np.broadcast_to(a["attn_conv_w"].T, (P, 4, DIN))
    arrays["chp"] = np.concatenate([a["attn_conv_b"].reshape(2, P).T, a["attn_D_skip"].reshape(2, P).T], 1)

    nc = bacc.Bacc("TRN2", target_bir_lowering=False, num_devices=1)
    aps, feeds = {}, {}
    for name, arr in arrays.items():
        arr = np.ascontiguousarray(arr)
        feeds["in_" + name] = arr
        aps[name] = nc.dram_tensor("in_" + name, arr.shape, mybir.dt.from_np(arr.dtype), kind="ExternalInput").ap()
    out = nc.dram_tensor("out_x", (P, T), F32, kind="ExternalOutput").ap()
    kpad = nc.dram_tensor("kpad", (DIN, 2 * P), F32, kind="Internal").ap()
    build(nc, aps, kpad, out)
    got = run_bass_kernel_spmd(nc, [feeds], core_ids=[0]).results[0]["out_x"]
    return np.ascontiguousarray(got.T).reshape(B, N, D)
```
